# Optimizing a Trainium2 kernel written in Bass

```python
import numpy as np
import jax
import jax.numpy as jnp

def _softmax(x, axis=-1):
    return jax.nn.softmax(x, axis=axis)

def _gelu(x):
    return jax.nn.gelu(x, approximate=True)

def _silu(x):
    return jax.nn.silu(x)

def _sigmoid(x):
    return jax.nn.sigmoid(x)

def _layernorm(x, axis=-1, eps=1e-05):
    m = jnp.mean(x, axis=axis, keepdims=True)
    v = jnp.var(x, axis=axis, keepdims=True)
    return (x - m) / jnp.sqrt(v + eps)

def _scatter_add(tgt, idx, src, axis=0):
    return tgt.at[idx].add(src)

def _segment_sum(src, seg, n):
    return jax.ops.segment_sum(src, seg, n)
kernel_name = 'mk_early_fusion_d2_tok_img1024_r4_2a6641'

def setup_inputs(seed: int=0):
    np.random.seed(seed)
    _w = jnp.asarray

    def _rec_inputs():
        import jax
        import jax.numpy as jnp
        _rk = jax.random.key(seed)
        x = 7.22013e-05 + 1.00017 * jax.random.normal(jax.random.fold_in(_rk, 1), (8, 64, 256, 4), jnp.float32)
        txt = -1.32754e-10 + 0.999995 * jax.random.normal(jax.random.fold_in(_rk, 2), (8, 77, 256), jnp.float32)
        return (x, txt)
    x, txt = _rec_inputs()

    def _L0_tok_setup():
        import jax, jax.numpy as jnp
        import numpy as np
        B, F, L, H, D = (8, 64, 256, 4, 64)
        MODEL = H * F
        WIN = 128

        def _local_mask():
            m = np.ones((L, L), dtype=bool)
            m = np.tril(m, WIN - 1)
            m = np.triu(m, -(WIN - 1))
            return jnp.asarray(m)

        def _flatten(y):
            n = y.shape[0]
            return y.transpose(0, 2, 3, 1).reshape(n, L, -1)
        key = jax.random.key(seed)
        ks = jax.random.split(key, 12)
        s = lambda n: 1.0 / np.sqrt(n)
        xav = np.sqrt(6.0 / (L + L))
        return {'x': jax.random.normal(ks[0], (B, F, L, H), jnp.float32), 'Wq_w': jax.random.normal(ks[1], (D, F), jnp.float32) * s(F), 'Wq_b': jnp.zeros((D,), jnp.float32), 'Wk_w': jax.random.normal(ks[2], (D, F), jnp.float32) * s(F), 'Wk_b': jnp.zeros((D,), jnp.float32), 'Wv_w': jax.random.normal(ks[3], (D, F), jnp.float32) * s(F), 'Wv_b': jnp.zeros((D,), jnp.float32), 'w_bias': jax.random.uniform(ks[4], (L, L), jnp.float32, -xav, xav), 'out_w': jax.random.normal(ks[5], (H * D, MODEL), jnp.float32) * s(H * D), 'out_b': jnp.zeros((MODEL,), jnp.float32), 'ln_g': jnp.ones((MODEL,), jnp.float32), 'ln_b': jnp.zeros((MODEL,), jnp.float32), 'local_mask': _local_mask()}
    _L0_tok_all = _L0_tok_setup()
    _L0_tok_in = {k: v for k, v in _L0_tok_all.items() if k in ('Wq_w', 'Wq_b', 'Wk_w', 'Wk_b', 'Wv_w', 'Wv_b', 'w_bias', 'out_w', 'out_b', 'ln_g', 'ln_b', 'local_mask')}
    del _L0_tok_all

    def _L0_attn_setup():
        import jax, jax.numpy as jnp
        import numpy as np
        NUM_HEADS = 16
        DIM = 256
        HARMONICS = 32
        B, L = (2, 512)

        def holo_linear(x, basis, phase, amp):
            resonance = jnp.einsum('bli,hi->blh', x, basis)
            w = amp * jnp.cos(phase)
            return jnp.einsum('blh,oh->blo', resonance, w)
        key = jax.random.key(seed)
        ks = jax.random.split(key, 13)
        two_pi = 2.0 * np.pi

        def make_proj(k0, k1):
            basis = jax.random.normal(k0, (HARMONICS, DIM), dtype=jnp.float32)
            basis = basis / jnp.linalg.norm(basis, axis=1, keepdims=True)
            phase = jax.random.normal(k1, (DIM, HARMONICS), dtype=jnp.float32) * two_pi
            amp = jnp.ones((DIM, HARMONICS), dtype=jnp.float32) / HARMONICS
            return (basis, phase, amp)
        x = jax.random.normal(ks[0], (B, L, DIM), dtype=jnp.float32)
        bq, pq, aq = make_proj(ks[1], ks[2])
        bk, pk, ak = make_proj(ks[3], ks[4])
        bv, pv, av = make_proj(ks[5], ks[6])
        bo, po, ao = make_proj(ks[7], ks[8])
        return {'x': x, 'basis_q': bq, 'phase_q': pq, 'amp_q': aq, 'basis_k': bk, 'phase_k': pk, 'amp_k': ak, 'basis_v': bv, 'phase_v': pv, 'amp_v': av, 'basis_o': bo, 'phase_o': po, 'amp_o': ao}
    _L0_attn_all = _L0_attn_setup()
    _L0_attn_in = {k: v for k, v in _L0_attn_all.items() if k in ('basis_q', 'phase_q', 'amp_q', 'basis_k', 'phase_k', 'amp_k', 'basis_v', 'phase_v', 'amp_v', 'basis_o', 'phase_o', 'amp_o')}
    del _L0_attn_all

    def _L0_ffn_setup():
        import jax, jax.numpy as jnp
        import numpy as np
        E = 64
        K = 6
        CAP = 128
        ROUTE_SCALE = 1.0
        key = jax.random.key(seed)
        ks = jax.random.split(key, 9)
        B, S, D, I = (2, 256, 256, 176)
        SI = 2 * I
        s = 0.02
        return {'x': jax.random.normal(ks[0], (B, S, D), jnp.float32), 'gate_w': jax.random.normal(ks[1], (E, D), jnp.float32) * s, 'gate_b': jnp.zeros((E,), jnp.float32), 'w1': jax.random.normal(ks[2], (E, I, D), jnp.float32) * s, 'w2': jax.random.normal(ks[3], (E, D, I), jnp.float32) * s, 'w3': jax.random.normal(ks[4], (E, I, D), jnp.float32) * s, 'ws1': jax.random.normal(ks[5], (SI, D), jnp.float32) * s, 'ws2': jax.random.normal(ks[6], (D, SI), jnp.float32) * s, 'ws3': jax.random.normal(ks[7], (SI, D), jnp.float32) * s}
    _L0_ffn_all = _L0_ffn_setup()
    _L0_ffn_in = {k: v for k, v in _L0_ffn_all.items() if k in ('gate_w', 'gate_b', 'w1', 'w2', 'w3', 'ws1', 'ws2', 'ws3')}
    del _L0_ffn_all

    def _L1_attn_setup():
        import jax, jax.numpy as jnp
        import numpy as np
        import math
        B, S, E = (2, 512, 256)
        H, DC, DR = (16, 64, 128)
        HD = E // H

        def _linear_params(key, din, dout):
            k1, k2 = jax.random.split(key)
            bound = 1.0 / math.sqrt(din)
            w = jax.random.uniform(k1, (din, dout), minval=-bound, maxval=bound, dtype=jnp.float32)
            b = jax.random.uniform(k2, (dout,), minval=-bound, maxval=bound, dtype=jnp.float32)
            return (w, b)

        def _gelu(x):
            return jax.nn.gelu(x, approximate=False)

        def _rope_cos_sin(seq_len, d_rope):
            inv_freq = 1.0 / 10000.0 ** (jnp.arange(0, d_rope, 2, dtype=jnp.float32) / d_rope)
            t = jnp.arange(seq_len, dtype=jnp.float32)
            freqs = t[:, None] * inv_freq[None, :]
            emb = jnp.concatenate([freqs, freqs], axis=-1)
            return (jnp.cos(emb), jnp.sin(emb))

        def _apply_rope(x, cos, sin):
            d = x.shape[-1]
            x1, x2 = (x[..., :d // 2], x[..., d // 2:])
            rot = jnp.concatenate([-x2, x1], axis=-1)
            return x * cos + rot * sin
        key = jax.random.key(seed)
        ks = jax.random.split(key, 10)
        x = jax.random.normal(ks[0], (B, S, E), dtype=jnp.float32)
        wq, bq = _linear_params(ks[1], E, DC)
        wqc, bqc = _linear_params(ks[2], DC, E - DR)
        wqr, bqr = _linear_params(ks[3], E, DR)
        wkv, bkv = _linear_params(ks[4], E, DC)
        wkr, bkr = _linear_params(ks[5], E, DR)
        wkc, bkc = _linear_params(ks[6], DC, E - DR)
        wv, bv = _linear_params(ks[7], DC, E)
        wo, bo = _linear_params(ks[8], E, E)
        return dict(x=x, wq=wq, bq=bq, wqc=wqc, bqc=bqc, wqr=wqr, bqr=bqr, wkv=wkv, bkv=bkv, wkr=wkr, bkr=bkr, wkc=wkc, bkc=bkc, wv=wv, bv=bv, wo=wo, bo=bo)
    _L1_attn_all = _L1_attn_setup()
    _L1_attn_in = {k: v for k, v in _L1_attn_all.items() if k in ('wq', 'bq', 'wqc', 'bqc', 'wqr', 'bqr', 'wkv', 'bkv', 'wkr', 'bkr', 'wkc', 'bkc', 'wv', 'bv', 'wo', 'bo')}
    del _L1_attn_all

    def _L1_ffn_setup():
        import jax, jax.numpy as jnp
        import numpy as np
        D_MODEL = 256
        N_EXPERTS = 8
        TOP_K = 2
        HIDDEN = 4 * D_MODEL
        key = jax.random.key(seed)
        ks = jax.random.split(key, 6)
        B, S = (2, 512)
        x = jax.random.normal(ks[0], (B, S, D_MODEL), dtype=jnp.float32)
        shared_w1 = jax.random.normal(ks[1], (HIDDEN, D_MODEL), dtype=jnp.float32) * 0.02
        shared_w2 = jax.random.normal(ks[2], (D_MODEL, HIDDEN), dtype=jnp.float32) * 0.02
        experts_w1 = jax.random.normal(ks[3], (N_EXPERTS, HIDDEN, D_MODEL), dtype=jnp.float32) * 0.02
        experts_w2 = jax.random.normal(ks[4], (N_EXPERTS, D_MODEL, HIDDEN), dtype=jnp.float32) * 0.02
        gate_w = jax.random.normal(ks[5], (N_EXPERTS, D_MODEL), dtype=jnp.float32) * 0.02
        return {'x': x, 'shared_w1': shared_w1, 'shared_w2': shared_w2, 'experts_w1': experts_w1, 'experts_w2': experts_w2, 'gate_w': gate_w}
    _L1_ffn_all = _L1_ffn_setup()
    _L1_ffn_in = {k: v for k, v in _L1_ffn_all.items() if k in ('shared_w1', 'shared_w2', 'experts_w1', 'experts_w2', 'gate_w')}
    del _L1_ffn_all
    return {'x': x, 'txt': txt, 'L0_tok_Wq_w': _L0_tok_in['Wq_w'], 'L0_tok_Wq_b': _L0_tok_in['Wq_b'], 'L0_tok_Wk_w': _L0_tok_in['Wk_w'], 'L0_tok_Wk_b': _L0_tok_in['Wk_b'], 'L0_tok_Wv_w': _L0_tok_in['Wv_w'], 'L0_tok_Wv_b': _L0_tok_in['Wv_b'], 'L0_tok_w_bias': _L0_tok_in['w_bias'], 'L0_tok_out_w': _L0_tok_in['out_w'], 'L0_tok_out_b': _L0_tok_in['out_b'], 'L0_tok_ln_g': _L0_tok_in['ln_g'], 'L0_tok_ln_b': _L0_tok_in['ln_b'], 'L0_tok_local_mask': _L0_tok_in['local_mask'], 'L0_attn_basis_q': _L0_attn_in['basis_q'], 'L0_attn_phase_q': _L0_attn_in['phase_q'], 'L0_attn_amp_q': _L0_attn_in['amp_q'], 'L0_attn_basis_k': _L0_attn_in['basis_k'], 'L0_attn_phase_k': _L0_attn_in['phase_k'], 'L0_attn_amp_k': _L0_attn_in['amp_k'], 'L0_attn_basis_v': _L0_attn_in['basis_v'], 'L0_attn_phase_v': _L0_attn_in['phase_v'], 'L0_attn_amp_v': _L0_attn_in['amp_v'], 'L0_attn_basis_o': _L0_attn_in['basis_o'], 'L0_attn_phase_o': _L0_attn_in['phase_o'], 'L0_attn_amp_o': _L0_attn_in['amp_o'], 'L0_ffn_gate_w': _L0_ffn_in['gate_w'], 'L0_ffn_gate_b': _L0_ffn_in['gate_b'], 'L0_ffn_w1': _L0_ffn_in['w1'], 'L0_ffn_w2': _L0_ffn_in['w2'], 'L0_ffn_w3': _L0_ffn_in['w3'], 'L0_ffn_ws1': _L0_ffn_in['ws1'], 'L0_ffn_ws2': _L0_ffn_in['ws2'], 'L0_ffn_ws3': _L0_ffn_in['ws3'], 'L1_attn_wq': _L1_attn_in['wq'], 'L1_attn_bq': _L1_attn_in['bq'], 'L1_attn_wqc': _L1_attn_in['wqc'], 'L1_attn_bqc': _L1_attn_in['bqc'], 'L1_attn_wqr': _L1_attn_in['wqr'], 'L1_attn_bqr': _L1_attn_in['bqr'], 'L1_attn_wkv': _L1_attn_in['wkv'], 'L1_attn_bkv': _L1_attn_in['bkv'], 'L1_attn_wkr': _L1_attn_in['wkr'], 'L1_attn_bkr': _L1_attn_in['bkr'], 'L1_attn_wkc': _L1_attn_in['wkc'], 'L1_attn_bkc': _L1_attn_in['bkc'], 'L1_attn_wv': _L1_attn_in['wv'], 'L1_attn_bv': _L1_attn_in['bv'], 'L1_attn_wo': _L1_attn_in['wo'], 'L1_attn_bo': _L1_attn_in['bo'], 'L1_ffn_shared_w1': _L1_ffn_in['shared_w1'], 'L1_ffn_shared_w2': _L1_ffn_in['shared_w2'], 'L1_ffn_experts_w1': _L1_ffn_in['experts_w1'], 'L1_ffn_experts_w2': _L1_ffn_in['experts_w2'], 'L1_ffn_gate_w': _L1_ffn_in['gate_w']}

def reference(x, txt, L0_tok_Wq_w, L0_tok_Wq_b, L0_tok_Wk_w, L0_tok_Wk_b, L0_tok_Wv_w, L0_tok_Wv_b, L0_tok_w_bias, L0_tok_out_w, L0_tok_out_b, L0_tok_ln_g, L0_tok_ln_b, L0_tok_local_mask, L0_attn_basis_q, L0_attn_phase_q, L0_attn_amp_q, L0_attn_basis_k, L0_attn_phase_k, L0_attn_amp_k, L0_attn_basis_v, L0_attn_phase_v, L0_attn_amp_v, L0_attn_basis_o, L0_attn_phase_o, L0_attn_amp_o, L0_ffn_gate_w, L0_ffn_gate_b, L0_ffn_w1, L0_ffn_w2, L0_ffn_w3, L0_ffn_ws1, L0_ffn_ws2, L0_ffn_ws3, L1_attn_wq, L1_attn_bq, L1_attn_wqc, L1_attn_bqc, L1_attn_wqr, L1_attn_bqr, L1_attn_wkv, L1_attn_bkv, L1_attn_wkr, L1_attn_bkr, L1_attn_wkc, L1_attn_bkc, L1_attn_wv, L1_attn_bv, L1_attn_wo, L1_attn_bo, L1_ffn_shared_w1, L1_ffn_shared_w2, L1_ffn_experts_w1, L1_ffn_experts_w2, L1_ffn_gate_w):
    import jax
    import jax.numpy as jnp

    def _L0_tok_ref(x, Wq_w, Wq_b, Wk_w, Wk_b, Wv_w, Wv_b, w_bias, out_w, out_b, ln_g, ln_b, local_mask):
        import jax, jax.numpy as jnp
        import numpy as np
        B, F, L, H, D = (8, 64, 256, 4, 64)
        MODEL = H * F
        WIN = 128

        def _local_mask():
            m = np.ones((L, L), dtype=bool)
            m = np.tril(m, WIN - 1)
            m = np.triu(m, -(WIN - 1))
            return jnp.asarray(m)

        def _flatten(y):
            n = y.shape[0]
            return y.transpose(0, 2, 3, 1).reshape(n, L, -1)

        def proj(w, b):
            y = jnp.einsum('nclh,dc->ndlh', x, w) + b[None, :, None, None]
            return _flatten(y)
        q = proj(Wq_w, Wq_b)
        k = proj(Wk_w, Wk_b)
        v = proj(Wv_w, Wv_b)
        wb = w_bias * local_mask.astype(w_bias.dtype)
        ew = jnp.exp(wb)
        ek = jnp.exp(k)
        num = jnp.einsum('ts,nsd->ntd', ew, ek * v)
        den = jnp.einsum('ts,nsd->ntd', ew, ek)
        y = jax.nn.sigmoid(q) * num / den
        h = y @ out_w + out_b + _flatten(x)
        mu = jnp.mean(h, axis=-1, keepdims=True)
        var = jnp.mean(jnp.square(h - mu), axis=-1, keepdims=True)
        return (h - mu) * jax.lax.rsqrt(var + 1e-05) * ln_g + ln_b

    def _L0_attn_ref(x, basis_q, phase_q, amp_q, basis_k, phase_k, amp_k, basis_v, phase_v, amp_v, basis_o, phase_o, amp_o):
        import jax, jax.numpy as jnp
        import numpy as np
        NUM_HEADS = 16
        DIM = 256
        HARMONICS = 32
        B, L = (2, 512)

        def holo_linear(x, basis, phase, amp):
            resonance = jnp.einsum('bli,hi->blh', x, basis)
            w = amp * jnp.cos(phase)
            return jnp.einsum('blh,oh->blo', resonance, w)
        Bsz, Ls, C = x.shape
        head_dim = C // NUM_HEADS
        scale = head_dim ** (-0.5)

        def split_heads(t):
            return t.reshape(Bsz, Ls, NUM_HEADS, head_dim).transpose(0, 2, 1, 3)
        q = split_heads(holo_linear(x, basis_q, phase_q, amp_q))
        k = split_heads(holo_linear(x, basis_k, phase_k, amp_k))
        v = split_heads(holo_linear(x, basis_v, phase_v, amp_v))
        attn = jnp.einsum('bhqd,bhkd->bhqk', q, k) * scale
        attn = jax.nn.softmax(attn, axis=-1)
        out = jnp.einsum('bhqk,bhkd->bhqd', attn, v)
        out = out.transpose(0, 2, 1, 3).reshape(Bsz, Ls, C)
        return holo_linear(out, basis_o, phase_o, amp_o)

    def _L0_ffn_ref(x, gate_w, gate_b, w1, w2, w3, ws1, ws2, ws3):
        import jax, jax.numpy as jnp
        import numpy as np
        E = 64
        K = 6
        CAP = 128
        ROUTE_SCALE = 1.0
        shape = x.shape
        D = shape[-1]
        xf = x.reshape(-1, D)
        T = xf.shape[0]
        scores = jax.nn.softmax(xf @ gate_w.T, axis=-1)
        _, idx = jax.lax.top_k(scores + gate_b, K)
        weights = jnp.take_along_axis(scores, idx, axis=1) * ROUTE_SCALE
        flat_e = idx.reshape(-1)
        order = jnp.argsort(flat_e)
        se = flat_e[order]
        counts = jnp.bincount(flat_e, length=E)
        starts = jnp.cumsum(counts) - counts
        pos = jnp.arange(T * K) - starts[se]
        tok = order // K
        xb = jnp.zeros((E, CAP, D), xf.dtype).at[se, pos].set(xf[tok], mode='drop')
        h = jax.nn.silu(jnp.einsum('ecd,eid->eci', xb, w1)) * jnp.einsum('ecd,eid->eci', xb, w3)
        yb = jnp.einsum('eci,edi->ecd', h, w2)
        valid = (pos < CAP).astype(xf.dtype)
        contrib = yb[se, jnp.minimum(pos, CAP - 1)]
        wf = weights.reshape(-1)[order] * valid
        y = jnp.zeros_like(xf).at[tok].add(contrib * wf[:, None])
        z = jax.nn.silu(xf @ ws1.T) * (xf @ ws3.T) @ ws2.T
        return (y + z).reshape(shape)

    def _L1_attn_ref(x, wq, bq, wqc, bqc, wqr, bqr, wkv, bkv, wkr, bkr, wkc, bkc, wv, bv, wo, bo):
        import jax, jax.numpy as jnp
        import numpy as np
        import math
        B, S, E = (2, 512, 256)
        H, DC, DR = (16, 64, 128)
        HD = E // H

        def _linear_params(key, din, dout):
            k1, k2 = jax.random.split(key)
            bound = 1.0 / math.sqrt(din)
            w = jax.random.uniform(k1, (din, dout), minval=-bound, maxval=bound, dtype=jnp.float32)
            b = jax.random.uniform(k2, (dout,), minval=-bound, maxval=bound, dtype=jnp.float32)
            return (w, b)

        def _gelu(x):
            return jax.nn.gelu(x, approximate=False)

        def _rope_cos_sin(seq_len, d_rope):
            inv_freq = 1.0 / 10000.0 ** (jnp.arange(0, d_rope, 2, dtype=jnp.float32) / d_rope)
            t = jnp.arange(seq_len, dtype=jnp.float32)
            freqs = t[:, None] * inv_freq[None, :]
            emb = jnp.concatenate([freqs, freqs], axis=-1)
            return (jnp.cos(emb), jnp.sin(emb))

        def _apply_rope(x, cos, sin):
            d = x.shape[-1]
            x1, x2 = (x[..., :d // 2], x[..., d // 2:])
            rot = jnp.concatenate([-x2, x1], axis=-1)
            return x * cos + rot * sin
        b, s, _ = x.shape
        cq = _gelu(x @ wq + bq)
        q_c = cq @ wqc + bqc
        q_r = x @ wqr + bqr
        ckv = _gelu(x @ wkv + bkv)
        k_r = x @ wkr + bkr
        k_c = ckv @ wkc + bkc
        v = (ckv @ wv + bv).reshape(b, s, H, HD).transpose(0, 2, 1, 3)
        cos, sin = _rope_cos_sin(s, DR)
        q_r = _apply_rope(q_r, cos, sin)
        k_r = _apply_rope(k_r, cos, sin)
        q = _gelu(jnp.concatenate([q_c, q_r], axis=-1)).reshape(b, s, H, HD).transpose(0, 2, 1, 3)
        k = _gelu(jnp.concatenate([k_c, k_r], axis=-1)).reshape(b, s, H, HD).transpose(0, 2, 1, 3)
        scale = 1.0 / math.sqrt(HD)
        scores = jnp.einsum('bhqd,bhkd->bhqk', q, k) * scale
        causal = jnp.triu(jnp.ones((s, s), dtype=bool), k=1)
        scores = jnp.where(causal[None, None], -jnp.inf, scores)
        attn = jax.nn.softmax(scores, axis=-1)
        out = jnp.einsum('bhqk,bhkd->bhqd', attn, v)
        out = out.transpose(0, 2, 1, 3).reshape(b, s, E)
        return out @ wo + bo

    def _L1_ffn_ref(x, shared_w1, shared_w2, experts_w1, experts_w2, gate_w):
        import jax, jax.numpy as jnp
        import numpy as np
        D_MODEL = 256
        N_EXPERTS = 8
        TOP_K = 2
        HIDDEN = 4 * D_MODEL
        B, S, D = x.shape
        T = B * S
        x_flat = x.reshape(T, D)
        shared = jnp.einsum('td,dh->th', x_flat, shared_w1.T)
        shared = jnp.einsum('th,hd->td', jax.nn.silu(shared), shared_w2.T)
        gate_logits = x_flat @ gate_w.T
        top_k_gates, top_k_idx = jax.lax.top_k(gate_logits, TOP_K)
        top_k_gates = jax.nn.softmax(top_k_gates, axis=1)
        gates = jnp.zeros((T, N_EXPERTS), dtype=x.dtype)
        gates = gates.at[jnp.arange(T)[:, None], top_k_idx].set(top_k_gates)
        h = jnp.einsum('td,ehd->teh', x_flat, experts_w1)
        expert_out = jnp.einsum('teh,edh->ted', jax.nn.silu(h), experts_w2)
        selected = jnp.einsum('ted,te->td', expert_out, gates)
        return (shared + selected).reshape(B, S, D)
    h = _L0_tok_ref(x, L0_tok_Wq_w, L0_tok_Wq_b, L0_tok_Wk_w, L0_tok_Wk_b, L0_tok_Wv_w, L0_tok_Wv_b, L0_tok_w_bias, L0_tok_out_w, L0_tok_out_b, L0_tok_ln_g, L0_tok_ln_b, L0_tok_local_mask)
    h = jnp.concatenate([h, txt], axis=1)
    h = h + _L0_attn_ref(_layernorm(h, axis=-1), L0_attn_basis_q, L0_attn_phase_q, L0_attn_amp_q, L0_attn_basis_k, L0_attn_phase_k, L0_attn_amp_k, L0_attn_basis_v, L0_attn_phase_v, L0_attn_amp_v, L0_attn_basis_o, L0_attn_phase_o, L0_attn_amp_o)
    h = h + _L0_ffn_ref(_layernorm(h, axis=-1), L0_ffn_gate_w, L0_ffn_gate_b, L0_ffn_w1, L0_ffn_w2, L0_ffn_w3, L0_ffn_ws1, L0_ffn_ws2, L0_ffn_ws3)
    h = h + _L1_attn_ref(_layernorm(h, axis=-1), L1_attn_wq, L1_attn_bq, L1_attn_wqc, L1_attn_bqc, L1_attn_wqr, L1_attn_bqr, L1_attn_wkv, L1_attn_bkv, L1_attn_wkr, L1_attn_bkr, L1_attn_wkc, L1_attn_bkc, L1_attn_wv, L1_attn_bv, L1_attn_wo, L1_attn_bo)
    h = h + _L1_ffn_ref(_layernorm(h, axis=-1), L1_ffn_shared_w1, L1_ffn_shared_w2, L1_ffn_experts_w1, L1_ffn_experts_w2, L1_ffn_gate_w)
    return h

_drawn_inputs = setup_inputs


def setup_inputs(seed=0):
    import zlib

    import numpy as np

    out = dict(_drawn_inputs(seed))
    spreads = {'L0_tok_Wq_b': (0.0, 0.8),
     'L0_tok_Wk_b': (0.0, 2.0),
     'L0_tok_Wv_b': (0.0, 0.1),
     'L0_tok_out_b': (0.0, 0.1),
     'L0_tok_ln_g': (1.0, 0.2),
     'L0_tok_ln_b': (0.0, 0.1),
     'L0_attn_amp_q': (0.03125, 0.6),
     'L0_attn_amp_k': (0.03125, 0.6),
     'L0_attn_amp_v': (0.03125, 0.6),
     'L0_attn_amp_o': (0.03125, 0.6),
     'L0_ffn_gate_b': (0.0, 0.8)}
    factors = {'L0_tok_w_bias': 8.0,
     'L0_attn_basis_q': 8.0,
     'L0_attn_phase_q': 8.0,
     'L0_attn_basis_k': 8.0,
     'L0_attn_phase_k': 8.0,
     'L0_attn_basis_v': 8.0,
     'L0_attn_phase_v': 8.0,
     'L0_attn_basis_o': 8.0,
     'L0_attn_phase_o': 8.0,
     'L0_ffn_gate_w': 8.0,
     'L0_ffn_w1': 8.0,
     'L0_ffn_w2': 8.0,
     'L0_ffn_w3': 8.0,
     'L0_ffn_ws1': 2.699,
     'L1_attn_wq': 8.0,
     'L1_attn_bq': 200.0,
     'L1_attn_wqc': 8.0,
     'L1_attn_bqc': 200.0,
     'L1_attn_wqr': 8.0,
     'L1_attn_bqr': 187.863,
     'L1_attn_bkv': 8.0,
     'L1_attn_wkr': 8.0,
     'L1_attn_bkr': 200.0,
     'L1_attn_wkc': 8.0,
     'L1_attn_bkc': 131.703,
     'L1_attn_bv': 3.137,
     'L1_attn_bo': 3.711}
    for name, (base, spread) in spreads.items():
        noise = np.random.default_rng([zlib.crc32(name.encode()), seed]).standard_normal(out[name].shape)
        drawn = base * np.exp(spread * noise) if base else spread * noise
        out[name] = jnp.asarray(drawn.astype(out[name].dtype))
    for name, factor in factors.items():
        out[name] = (out[name] * factor).astype(out[name].dtype)
    return out
```

```python
import math
from contextlib import ExitStack

import numpy as np

import concourse.bass as bass
from concourse import mybir

F32 = mybir.dt.float32
BF16 = mybir.dt.bfloat16
U32 = mybir.dt.uint32
U8 = mybir.dt.uint8
ALU = mybir.AluOpType
ACT = mybir.ActivationFunctionType
AX_X = mybir.AxisListType.X
ds = bass.ds

B = 8
IMG = 256
TXT = 77
S = IMG + TXT
D = 256
F = 64
H = 4
TP = 111
NT = S // TP
G = B * NT
T = B * S
NH = 16
HD = D // NH
VW = HD + 1
NHALF = 8
EPS = 1e-5
IMG_TILES = [(0, TP), (TP, TP), (2 * TP, IMG - 2 * TP)]

E0, I0, K0, CAP = 64, 176, 6, 128
IC = I0 // 2
SIC = 2 * I0 // IC
IDS, WTS, TID = D, D + 8, D + 15
ROW = D + 16

DEEP = 4

E1, HID = 8, 1024
SLOT_TILES = (2 * T + E1 * (128 - 1)) // 128

Q_SLOTS = [0, 0, 1, 1, 0, 2]
K_SLOTS = [0, 1, 0, 1, 2, 0]
NSLOT = len(Q_SLOTS)
KROWS = HD * NSLOT
NPART = 3
MAXROW = KROWS


def settle(eng, t):
    eng.sem_inc(t.sem.settled, 1)


class Steps:

    def __init__(self, eng, sem):
        self.eng, self.sem, self.total, self.base, self.k = eng, sem, 0, 0, 0

    def did(self, ins):
        self.k += 1
        ins.then_inc(self.sem, 1)

    def wait(self):
        self.eng.wait_ge(self.sem, self.base + self.k)

    def enter(self, i, per):
        self.outer, self.base, self.k, self.per = self.base + self.k, self.base + self.k + i * per, 0, per

    def leave(self, times):
        assert self.k == self.per, (self.k, self.per)
        self.base, self.k = self.outer + times * self.per, 0


def load_constants(nc, io, t, sem):
    const_loads = [
        (t.tok_kv[:, :], io["tok_kv"]), (t.tok_q[:, :], io["tok_q"]), (t.tok_res[:, :, :], io["tok_res"]),
        (t.ewT[:, :, :], io["bias_t"]), (t.mask8[:, :, :], io["mask_t"]), (t.tok_out[:, :, :], io["tok_out"]),
        (t.ident[:, :], io["ident"]), (t.gb[0:TP, 0, :], io["ln_g"].partition_broadcast(TP)),
        (t.gb[0:TP, 1, :], io["ln_b"].partition_broadcast(TP)),
        (t.basis[:, :, :], io["basis"]), (t.basis_o[:, :, :], io["basis_o"]), (t.phase[:, :], io["phase"]), (t.amp[:, :], io["amp"]),
        (t.wo[:, :, :], io["wo"]), (t.bo[:, :], io["bo"].partition_broadcast(TP)), (t.above32[:, :, :], io["above"]),
        (t.iota[:, :], io["iota"].partition_broadcast(128)),
        (t.h[IMG - 2 * TP:TP, 2:G:NT, :], io["txt"].rearrange("b s d -> s b d")),
    ]
    with nc.Block() as block:
        @block.sync
        def _(sp):
            for dst, src in const_loads:
                sp.dma_start(dst, src).then_inc(sem.consts, 16)

        @block.gpsimd
        def _(pool):
            fills = [(t.xs[0][F:F + 1, :, :], 1.0), (t.xs[1][F:F + 1, :, :], 1.0), (t.half[:, :], -0.5),
                     (t.v[:, :, :, HD:VW], 1.0)]
            for n, (dst, value) in enumerate(fills):
                pool.wait_ge(sem.filled, n)
                nc.gpsimd.memset(dst, value).then_inc(sem.filled, 1)

        @block.vector
        def _(dve):
            dve.wait_ge(sem.consts, 16 * len(const_loads))
            t.dve.did(nc.vector.tensor_copy(t.maskf[:, :, :], t.mask8[:, :, :].bitcast(U8)))
            t.dve.wait()
            t.dve.did(nc.vector.tensor_tensor(t.ewT[:, :, :], t.ewT[:, :, :], t.maskf[:, :, :], ALU.mult))
            magic = 1.5 * 2.0 ** 23
            two_pi = 2.0 * math.pi
            c1 = 6.28125
            c2 = float(np.float32(np.round((two_pi - c1) * 2.0 ** 21) / 2.0 ** 21))
            c3 = float(np.float32(two_pi - c1 - c2))
            k, ph = t.trig[:, 0, :], t.trig[:, 1, :]
            t.dve.did(nc.vector.tensor_scalar(k, t.phase[:, :], 1.0 / two_pi, 0.25, ALU.mult, ALU.add))
            for op, s in ((ALU.add, magic), (ALU.subtract, magic)):
                t.dve.wait()
                t.dve.did(nc.vector.tensor_scalar(k, k, s, None, op))
            src = t.phase[:, :]
            for c in (c1, c2, c3):
                t.dve.wait()
                t.dve.did(nc.vector.scalar_tensor_tensor(out=ph, in0=k, scalar=-c, in1=src, op0=ALU.mult, op1=ALU.add))
                src = ph
            t.dve.wait()
            t.dve.did(nc.vector.tensor_scalar(ph, ph, math.pi / 2, math.pi, ALU.add, ALU.min))
            t.dve.wait()
            t.dve.did(nc.vector.tensor_scalar(ph, ph, -math.pi, None, ALU.max))
            t.dve.wait()
            t.dve.did(nc.vector.tensor_copy(t.above[:, :, :], t.above32[:, :, :]))
            nc.vector.tensor_copy(t.identb[:, :], t.ident[:, :]).then_inc(sem.prepared, 1)
            dve.wait_ge(sem.cosines, 1)
            nc.vector.tensor_tensor(t.holo[:, :], t.trig[:, 1, :], t.amp[:, :], ALU.mult).then_inc(sem.prepared, 1)

        @block.scalar
        def _(act):
            act.wait_ge(sem.prepared, 1)
            nc.scalar.activation(t.trig[:, 1, :], t.trig[:, 1, :], ACT.Sin).then_inc(sem.cosines, 1)
            nc.scalar.activation(t.ewT[:, :, :], t.ewT[:, :, :], ACT.Exp).then_inc(sem.cosines, 1)


def token_layer(nc, io, t, new_sem, ctx):
    xs_loaded, xs_free = [new_sem(f"tok_xs_loaded{u}") for u in range(2)], new_sem("tok_xs_free")
    kv_ready, ekv_act, ekv_dve = new_sem("tok_kv_ready"), new_sem("tok_ek_ready"), new_sem("tok_ekv_ready")
    q_ready, eq_ready = new_sem("tok_q_ready"), new_sem("tok_eq_ready")
    nd_ready, y_ready = new_sem("tok_nd_ready"), new_sem("tok_y_ready")
    yt_ready, yt_copied = new_sem("tok_yt_ready"), new_sem("tok_yt_copied")
    h_ready, stats_ready = new_sem("tok_h_ready"), new_sem("tok_stats_ready")
    rstd_ready, norm_ready, norm_free = new_sem("tok_rstd_ready"), new_sem("tok_norm_ready"), new_sem("tok_norm_free")

    def sb(name, shape, dt=F32):
        return ctx.enter_context(nc.sbuf_tensor(name, shape, dt))

    def ps(name, shape, dt=F32):
        return ctx.enter_context(nc.psum_tensor(name, shape, dt))

    ekv = [sb(f"tok_ekv{c}", [128, H, 2, F]) for c in range(2)]
    eq = sb("tok_eq", [TP, NT, D])
    y = [sb(f"tok_y{i}", [TP, D]) for i in range(2)]
    den = sb("tok_den", [TP, D])
    yT = [sb(f"tok_yT{i}", [128, 2, TP]) for i in range(2)]
    norm = [sb(f"tok_norm{i}", [TP, D]) for i in range(2)]
    stats = sb("tok_stats", [TP, 6])
    mv = [sb(f"tok_mv{i}", [TP, 2]) for i in range(2)]
    rstd = [sb(f"tok_rstd{i}", [TP, 1]) for i in range(2)]
    var = sb("tok_var", [TP, 1])
    p_kv = [ps(f"tok_pkv{c}", [128, H, 2, F]) for c in range(2)]
    p_q = ps("tok_pq", [TP, 2, 512])
    p_nd = [ps(f"tok_pnd{c}", [TP, H, 2, F]) for c in range(2)]
    p_yt = ps("tok_pyt", [128, 512])
    p_h = ps("tok_ph", [TP, 512])

    def q_of(j):
        n = IMG_TILES[j][1]
        return p_q[0:n, j // 2, (j % 2) * D:(j % 2) * D + D]

    with nc.Block() as block:
        @block.sync
        def _(sp):
            with sp.Fori(0, B // 2) as i:
                for u in range(2):
                    sp.wait_ge(xs_free, 2 * i + u + 1)
                    sp.dma_start(t.xs[u][0:F, :, :], io["x"][ds(2 * i + u, 1)].rearrange("a c h l -> (a c) h l")).then_inc(xs_loaded[u], 16)

        @block.tensor
        def _(pe):
            pe.sem_inc(xs_free, 2)
            pe.wait_ge(t.sem.cosines, 2)
            with pe.Fori(0, B // 2) as i:
                for u in range(2):
                    n = 2 * i + u
                    xs = t.xs[u]
                    pe.wait_ge(xs_loaded[u], 16 * i + 16)
                    for c in range(2):
                        pe.wait_ge(ekv_dve, 2 * n + c)
                        for h in range(H):
                            mm = nc.tensor.matmul(p_kv[c][:, h, :, :], xs[:, h, 128 * c:128 * c + 128], t.tok_kv[:, :],
                                                  start=True, stop=True)
                        mm.then_inc(kv_ready, 1)
                    pe.wait_ge(eq_ready, NT * n)
                    for j, (l0, rows) in enumerate(IMG_TILES):
                        for h in range(H):
                            mm = nc.tensor.matmul(q_of(j)[:, F * h:F * h + F], xs[:, h, l0:l0 + rows], t.tok_q[:, :],
                                                  start=True, stop=True)
                        if j:
                            mm.then_inc(q_ready, 1)

                    def mix(j):
                        l0, rows = IMG_TILES[j]
                        if j == 0:
                            pe.wait_ge(ekv_dve, 2 * n + 2)
                        pe.wait_ge(y_ready, NT * n + max(j - 1, 0))
                        for c in range(2):
                            mm = nc.tensor.matmul(p_nd[j % 2][0:rows, :, :, :], t.ewT[:, c, l0:l0 + rows], ekv[c][:, :, :, :],
                                                  start=(c == 0), stop=(c == 1))
                        mm.then_inc(nd_ready, 1)

                    def project(j):
                        l0, rows = IMG_TILES[j]
                        pe.wait_ge(y_ready, NT * n + j + 1)
                        pe.wait_ge(yt_copied, NT * n + j)
                        settle(pe, t)
                        for c in range(2):
                            mm = nc.tensor.transpose(p_yt[:, 128 * c:128 * c + rows], y[j % 2][0:rows, 128 * c:128 * c + 128],
                                                     t.ident[0:rows, 0:rows])
                        mm.then_inc(yt_ready, 1)
                        pe.wait_ge(norm_ready, NT * n + j)
                        for h in range(H):
                            nc.tensor.matmul(p_h[0:rows, F * h:F * h + F], xs[:, h, l0:l0 + rows], t.tok_res[:, h, :],
                                             start=(h == 0), stop=False, skip_group_check=True)
                        pe.wait_ge(yt_copied, NT * n + j + 1)
                        for c in range(2):
                            mm = nc.tensor.matmul(p_h[0:rows, 0:D], yT[j % 2][:, c, 0:rows], t.tok_out[:, c, :],
                                                  start=False, stop=(c == 1), skip_group_check=True)
                        mm.then_inc(h_ready, 1)
                        return mm

                    mix(0)
                    mix(1)
                    project(0)
                    mix(2)
                    project(1)
                    project(2)
                    pe.wait_ge(h_ready, NT * n + NT)
                    pe.sem_inc(xs_free, 1)

        @block.scalar
        def _(act):
            with act.Fori(0, B) as n:
                for c in range(2):
                    act.wait_ge(kv_ready, 2 * n + c + 1)
                    act.wait_ge(nd_ready, NT * n)
                    nc.scalar.activation(ekv[c][:, :, 0, :], p_kv[c][:, :, 0, :], ACT.Exp).then_inc(ekv_act, 1)
                for j, (l0, rows) in enumerate(IMG_TILES):
                    act.wait_ge(q_ready, 2 * n + 1 + j // 2)
                    act.wait_ge(y_ready, NT * n)
                    nc.scalar.activation(eq[0:rows, j, :], q_of(j), ACT.Exp, scale=-1.0).then_inc(eq_ready, 1)
                for j, (l0, rows) in enumerate(IMG_TILES):
                    act.wait_ge(yt_ready, NT * n + j + 1)
                    act.wait_ge(h_ready, NT * n + max(j - 1, 0))
                    nc.scalar.activation(yT[j % 2][:, :, 0:rows],
                                         p_yt[:, 0:256].rearrange("p (c r) -> p c r", c=2)[:, :, 0:rows],
                                         ACT.Copy).then_inc(yt_copied, 1)

        @block.vector
        def _(dve):
            with dve.Fori(0, B) as n:
                t.dve.enter(n, 3 * NT)
                for c in range(2):
                    dve.wait_ge(ekv_act, 2 * n + c + 1)
                    nc.vector.tensor_tensor(ekv[c][:, :, 1, :], ekv[c][:, :, 0, :], p_kv[c][:, :, 1, :],
                                            ALU.mult).then_inc(ekv_dve, 1)

                def gate(j):
                    rows = IMG_TILES[j][1]
                    split = "p (h f) -> p h f"
                    dve.wait_ge(eq_ready, NT * n + j + 1)
                    dve.wait_ge(nd_ready, NT * n + j + 1)
                    dve.wait_ge(y_ready, NT * n + j)
                    t.dve.did(nc.vector.scalar_tensor_tensor(
                        out=den[0:rows, :].rearrange(split, h=H), in0=eq[0:rows, j, :].rearrange(split, h=H), scalar=1.0,
                        in1=p_nd[j % 2][0:rows, :, 0, :], op0=ALU.add, op1=ALU.mult))
                    t.dve.wait()
                    t.dve.did(nc.vector.reciprocal(den[0:rows, :], den[0:rows, :]))
                    t.dve.wait()
                    dve.wait_ge(yt_ready, NT * n + max(j - 1, 0))
                    nc.vector.tensor_tensor(y[j % 2][0:rows, :].rearrange(split, h=H), den[0:rows, :].rearrange(split, h=H),
                                            p_nd[j % 2][0:rows, :, 1, :], ALU.mult).then_inc(y_ready, 1)

                def normalize(j):
                    rows = IMG_TILES[j][1]
                    dve.wait_ge(h_ready, NT * n + j + 1)
                    dve.wait_ge(stats_ready, NT * n + j)
                    settle(dve, t)
                    t.dve.did(nc.vector.bn_stats(stats[0:rows, :], p_h[0:rows, 0:D]))
                    t.dve.wait()
                    dve.wait_ge(norm_ready, NT * n + max(j - 1, 0))
                    dve.wait_ge(rstd_ready, NT * n + max(j - 1, 0))
                    settle(dve, t)
                    nc.vector.bn_aggr(mv[j % 2][0:rows, :], stats[0:rows, :]).then_inc(stats_ready, 1)
                    dve.wait_ge(stats_ready, NT * n + j + 1)
                    dve.wait_ge(rstd_ready, NT * n + j + 1)
                    dve.wait_ge(norm_free, NT * n + max(j - 1, 0))
                    nc.vector.tensor_scalar(norm[j % 2][0:rows, :], p_h[0:rows, 0:D], mv[j % 2][0:rows, 0:1],
                                                      rstd[j % 2][0:rows, :], ALU.subtract, ALU.mult).then_inc(norm_ready, 1)

                gate(0)
                gate(1)
                normalize(0)
                gate(2)
                normalize(1)
                normalize(2)
                t.dve.leave(B)

        @block.gpsimd
        def _(pool):
            pool.wait_ge(t.sem.filled, 4)
            with pool.Fori(0, B) as n:
                t.pool.enter(n, 2 * NT)
                for j, (l0, rows) in enumerate(IMG_TILES):
                    pool.wait_ge(stats_ready, NT * n + j + 1)
                    pool.wait_ge(rstd_ready, NT * n + j)
                    pool.wait_ge(norm_ready, NT * n + max(j - 1, 0))
                    settle(pool, t)
                    t.pool.did(nc.gpsimd.tensor_scalar(var[0:rows, :], mv[j % 2][0:rows, 1:2], EPS, None, ALU.add))
                    t.pool.wait()
                    nc.gpsimd.tensor_tensor(rstd[j % 2][0:rows, :], var[0:rows, :], t.half[0:rows, 0:1], ALU.pow).then_inc(rstd_ready, 1)
                    pool.wait_ge(norm_ready, NT * n + j + 1)
                    t.pool.did(nc.gpsimd.tensor_tensor(norm[j % 2][0:rows, :], norm[j % 2][0:rows, :], t.gb[0:rows, 0, :], ALU.mult))
                    t.pool.wait()
                    nc.gpsimd.tensor_tensor(t.h[0:rows, ds(NT * n + j, 1), :].rearrange("p a d -> p (a d)"), norm[j % 2][0:rows, :], t.gb[0:rows, 1, :],
                                            ALU.add).then_inc(norm_free, 1)
                t.pool.leave(B)


class NormalizedTransposed:

    def __init__(self, nc, t, name, new_sem, sb, ps):
        self.nc, self.t = nc, t
        self.stats_ready, self.rstd_ready = new_sem(name + "_stats_ready"), new_sem(name + "_rstd_ready")
        self.xn_ready, self.xt_turned = new_sem(name + "_xn_ready"), new_sem(name + "_xt_turned")
        self.xt_ready, self.xt_used = new_sem(name + "_xt_ready"), new_sem(name + "_xt_used")
        self.stats = sb(name + "_stats", [TP, NT, 6])
        self.mv = sb(name + "_mv", [TP, NT, 2])
        self.var = sb(name + "_var", [TP, NT])
        self.rstd = sb(name + "_rstd", [TP, NT])
        self.xn = sb(name + "_xn", [TP, NT, D])
        self.xT = sb(name + "_xT", [128, 2, S])
        self.p_xt = ps(name + "_pxt", [128, 2, 512])

    STEPS = NT

    def row_stats(self, dve, n):
        dve.wait_ge(self.xn_ready, n)
        settle(dve, self.t)
        for j in range(NT):
            self.t.dve.did(self.nc.vector.bn_stats(self.stats[:, j, :], self.t.h[:, ds(NT * n + j, 1), :].rearrange("p a d -> p (a d)")))
        self.t.dve.wait()
        settle(dve, self.t)
        for j in range(NT):
            ins = self.nc.vector.bn_aggr(self.mv[:, j, :], self.stats[:, j, :])
        ins.then_inc(self.stats_ready, 1)

    POOL_STEPS = 1

    def invert(self, pool, n):
        pool.wait_ge(self.stats_ready, n + 1)
        settle(pool, self.t)
        self.t.pool.did(self.nc.gpsimd.tensor_scalar(self.var[:, :], self.mv[:, :, 1], EPS, None, ALU.add))
        self.t.pool.wait()
        self.nc.gpsimd.tensor_tensor(self.rstd[:, :], self.var[:, :], self.t.half[0:TP, 0:NT], ALU.pow).then_inc(self.rstd_ready, 1)

    def normalize(self, dve, n):
        dve.wait_ge(self.stats_ready, n + 1)
        dve.wait_ge(self.rstd_ready, n + 1)
        dve.wait_ge(self.xt_turned, n)
        for j in range(NT):
            ins = self.nc.vector.tensor_scalar(self.xn[:, j, :], self.t.h[:, ds(NT * n + j, 1), :].rearrange("p a d -> p (a d)"),
                                               self.mv[:, j, 0:1], self.rstd[:, j:j + 1], ALU.subtract, ALU.mult)
        ins.then_inc(self.xn_ready, 1)

    def turn(self, pe, n):
        pe.wait_ge(self.xn_ready, n + 1)
        pe.wait_ge(self.xt_ready, n)
        for c in range(2):
            for j in range(NT):
                mm = self.nc.tensor.transpose(self.p_xt[:, c, TP * j:TP * j + TP], self.xn[:, j, 128 * c:128 * c + 128],
                                              self.t.ident[0:TP, 0:TP])
        mm.then_inc(self.xt_turned, 1)

    def copy(self, act, n):
        act.wait_ge(self.xt_turned, n + 1)
        act.wait_ge(self.xt_used, n)
        self.nc.scalar.activation(self.xT[:, :, :], self.p_xt[:, :, 0:S], ACT.Copy).then_inc(self.xt_ready, 1)


class Splitter:

    def __init__(self, nc, t, name, which, scale, new_sem, sb):
        self.nc, self.t, self.which, self.scale = nc, t, which, scale
        self.part0, self.rest_ready = new_sem(name + "_part0"), new_sem(name + "_rest")
        self.part1, self.part2, self.stored = new_sem(name + "_part1"), new_sem(name + "_part2"), new_sem(name + "_stored")
        self.rest = sb(name + "_rest", [128, 2, S])
        self.parts = sb(name + "_parts", [128, NPART, 2, S], BF16)

    def first(self, act, n, x):
        act.wait_ge(self.stored, 16 * n)
        self.nc.scalar.activation(self.parts[:, 0, :, :], x, ACT.Copy, scale=self.scale).then_inc(self.part0, 1)

    def residue(self, dve, n, x):
        dve.wait_ge(self.part0, n + 1)
        dve.wait_ge(self.part2, n)
        self.nc.vector.scalar_tensor_tensor(out=self.rest[:, :, :], in0=x, scalar=self.scale, in1=self.parts[:, 0, :, :],
                                            op0=ALU.mult, op1=ALU.subtract).then_inc(self.rest_ready, 1)

    def second(self, pool, n):
        pool.wait_ge(self.rest_ready, n + 1)
        pool.wait_ge(self.stored, 16 * n)
        settle(pool, self.t)
        self.nc.gpsimd.tensor_copy(self.parts[:, 1, :, :], self.rest[:, :, :]).then_inc(self.part1, 1)

    def third(self, dve, n):
        dve.wait_ge(self.rest_ready, n + 1)
        dve.wait_ge(self.part1, n + 1)
        self.nc.vector.tensor_tensor(self.parts[:, 2, :, :], self.rest[:, :, :], self.parts[:, 1, :, :],
                                     ALU.subtract).then_inc(self.part2, 1)

    def store(self, sp, n):
        sp.wait_ge(self.part2, n + 1)
        sp.dma_start(self.t.split[ds(n, 1), self.which].rearrange("b a (c p) n -> p (b a) c n", p=128),
                     self.parts[:, :, :, :]).then_inc(self.stored, 16)


def holo_qkv(nc, io, t, new_sem, ctx):
    def sb(name, shape, dt=F32):
        return ctx.enter_context(nc.sbuf_tensor(name, shape, dt))

    def ps(name, shape, dt=F32):
        return ctx.enter_context(nc.psum_tensor(name, shape, dt))

    xf = NormalizedTransposed(nc, t, "hq", new_sem, sb, ps)
    cut = [Splitter(nc, t, "hq_q", 0, float(HD) ** -0.5, new_sem, sb), Splitter(nc, t, "hq_k", 1, 1.0, new_sem, sb)]
    r_made, r_ready = new_sem("hq_r_made"), new_sem("hq_r_ready")
    q_made, k_made, v_made, v_ready = new_sem("hq_q_made"), new_sem("hq_k_made"), new_sem("hq_v_made"), new_sem("hq_v_ready")
    rT = sb("hq_rT", [96, S])
    p_r = ps("hq_pr", [96, 512])
    p_qk = [ps("hq_pq", [128, 2, 512]), ps("hq_pk", [128, 2, 512])]
    p_v = ps("hq_pv", [TP, 2, D])
    made = [q_made, k_made]

    with nc.Block() as block:
        @block.sync
        def _(sp):
            with sp.Fori(0, B) as n:
                for c in cut:
                    c.store(sp, n)
            for c in cut:
                sp.wait_ge(c.stored, 16 * B)

        @block.tensor
        def _(pe):
            with pe.Fori(0, B) as n:
                xf.turn(pe, n)
                pe.wait_ge(xf.xt_ready, n + 1)
                pe.wait_ge(r_ready, n)
                for c in range(2):
                    mm = nc.tensor.matmul(p_r[:, 0:S], t.basis[:, c, :], xf.xT[:, c, :], start=(c == 0), stop=(c == 1))
                mm.then_inc(r_made, 1)
                pe.wait_ge(r_made, n + 1)
                pe.sem_inc(xf.xt_used, 1)
                pe.wait_ge(r_ready, n + 1)
                for w in range(2):
                    pe.wait_ge(cut[w].rest_ready, n)
                    for c in range(2):
                        mm = nc.tensor.matmul(p_qk[w][:, c, 0:S], t.holo[32 * w:32 * w + 32, 128 * c:128 * c + 128],
                                              rT[32 * w:32 * w + 32, :], start=True, stop=True)
                    mm.then_inc(made[w], 1)
                for half, tiles in enumerate(([0, 1], [2])):
                    pe.wait_ge(v_ready, 2 * n + half)
                    for j in tiles:
                        mm = nc.tensor.matmul(p_v[:, j % 2, :], rT[64:96, TP * j:TP * j + TP], t.holo[64:96, :],
                                              start=True, stop=True)
                    mm.then_inc(v_made, 1)

        @block.scalar
        def _(act):
            with act.Fori(0, B) as n:
                xf.copy(act, n)
                act.wait_ge(r_made, n + 1)
                act.wait_ge(v_made, 2 * n)
                nc.scalar.activation(rT[:, :], p_r[:, 0:S], ACT.Copy).then_inc(r_ready, 1)
                for w in range(2):
                    act.wait_ge(made[w], n + 1)
                    cut[w].first(act, n, p_qk[w][:, :, 0:S])
                for half, tiles in enumerate(([0, 1], [2])):
                    act.wait_ge(v_made, 2 * n + half + 1)
                    m = len(tiles)
                    nc.scalar.activation(t.v[:, ds(NT * n + tiles[0], m), :, 0:HD],
                                         p_v[:, 0:m, :].rearrange("p j (h d) -> p j h d", h=NH), ACT.Copy).then_inc(v_ready, 1)

        @block.vector
        def _(dve):
            with dve.Fori(0, B) as n:
                t.dve.enter(n, xf.STEPS)
                xf.row_stats(dve, n)
                xf.normalize(dve, n)
                for w in range(2):
                    cut[w].residue(dve, n, p_qk[w][:, :, 0:S])
                for w in range(2):
                    cut[w].third(dve, n)
                t.dve.leave(B)

        @block.gpsimd
        def _(pool):
            with pool.Fori(0, B) as n:
                t.pool.enter(n, xf.POOL_STEPS)
                xf.invert(pool, n)
                for w in range(2):
                    cut[w].second(pool, n)
                t.pool.leave(B)


def attention(nc, t, name, causal, new_sem, ctx):
    def sb(name_, shape, dt=F32):
        return ctx.enter_context(nc.sbuf_tensor(name + name_, shape, dt))

    def ps(name_, shape, dt=F32):
        return ctx.enter_context(nc.psum_tensor(name + name_, shape, dt))

    def sm(name_):
        return new_sem(name + name_)

    stack_loaded, stack_free, ones_set = sm("_stack_loaded"), sm("_stack_free"), sm("_ones_set")
    s_made, s_max = sm("_s_made"), sm("_s_max")
    max_cut, max_stored, max_loaded = sm("_max_cut"), sm("_max_stored"), sm("_max_loaded")
    t_made, exp_made, probs_free = sm("_t_made"), sm("_exp_made"), sm("_probs_free")
    o_free = sm("_o_free")

    ring = 3
    qst = sb("_qst", [KROWS + NPART, ring, NH, S], BF16)
    kst = sb("_kst", [KROWS + NPART, ring, NH, S], BF16)
    probs = [sb(f"_probs{u}", [TP, NT, S]) for u in range(2)]
    nmax = sb("_nmax", [TP, NT, NH])
    mrest = sb("_mrest", [TP, NT, NHALF])
    mparts = sb("_mparts", [128, NT, 32], BF16)
    mturned = sb("_mturned", [128, NT, 32], BF16)
    rsum = sb("_rsum", [TP, NT, NHALF])
    p_s = ps("_ps", [TP, NT, 512])
    p_t = ps("_pt", [TP, NT, 512])
    p_o = [ps(f"_po{u}", [TP, 512]) for u in range(2)]
    n_stack = 2 * NSLOT
    halves = NH // NHALF
    chunks = [(32 * k, min(32, TP - 32 * k)) for k in range(4)]

    def o_view(half):
        return p_o[half][:, 0:NT * NHALF * VW].rearrange("p (j h d) -> p j h d", j=NT, h=NHALF)

    with nc.Block() as block:
        @block.sync
        def _(sp):
            def load_stacks(n):
                sp.wait_ge(stack_free, n + 1)
                sp.wait_ge(stack_loaded, 16 * n_stack * n)
                for slots, which, dst in ((Q_SLOTS, 0, qst), (K_SLOTS, 1, kst)):
                    for r, part in enumerate(slots):
                        sp.dma_start(dst[HD * r:HD * r + HD, ds(n % ring, 1), :, :].rearrange("d a h n -> d (a h) n"),
                                     t.split[ds(n, 1), which, part].rearrange("b (h d) n -> d (b h) n", d=HD)).then_inc(stack_loaded, 16)

            def rows_of_maxima(n, half):
                m = halves * n + half
                sp.wait_ge(max_cut, m + 1)
                settle(sp, t)
                for k, (r0, rows) in enumerate(chunks):
                    sp.dma_start(t.rowmax[ds(n, 1), half].rearrange("b a h (j p) -> (b a h) j p", p=TP)[:, :, r0:r0 + rows],
                                 mturned[32 * k:32 * k + NPART * NHALF, :, 0:rows]).then_inc(max_stored, 16)
                sp.wait_ge(max_stored, 16 * len(chunks) * (m + 1))
                settle(sp, t)
                sp.wait_ge(max_loaded, 16 * m)
                sp.dma_start(qst[MAXROW:MAXROW + NPART, ds(n % ring, 1), NHALF * half:NHALF * half + NHALF, :].rearrange("a b h n -> a (b h) n"),
                             t.rowmax[ds(n, 1), half].rearrange("b a h n -> a (b h) n")).then_inc(max_loaded, 16)

            load_stacks(0)
            with sp.Fori(0, B - 1) as n:
                load_stacks(n + 1)
                for half in range(halves):
                    rows_of_maxima(n, half)
            for half in range(halves):
                rows_of_maxima(B - 1, half)

        @block.gpsimd
        def _(pool):
            nc.gpsimd.memset(kst[MAXROW:MAXROW + NPART, :, :, :], 1.0).then_inc(ones_set, 1)
            pool.wait_ge(ones_set, 1)
            nc.gpsimd.memset(mparts[:, :, :], 0.0).then_inc(ones_set, 1)

        @block.tensor
        def _(pe):
            def scores(n, h):
                m = NH * n + h
                if h == 0:
                    pe.wait_ge(stack_loaded, 16 * n_stack * (n + 1))
                pe.wait_ge(s_max, m)
                for j in range(NT):
                    w = TP * (j + 1) if causal else S
                    mm = nc.tensor.matmul(p_s[:, j, 0:w], qst[0:KROWS, ds(n % ring, 1), h, TP * j:TP * j + TP].rearrange("p a n -> p (a n)"),
                                          kst[0:KROWS, ds(n % ring, 1), h, 0:w].rearrange("p a n -> p (a n)"),
                                          start=True, stop=not causal, skip_group_check=causal)
                    if causal:
                        mm = nc.tensor.matmul(p_s[:, j, TP * j:w], t.identb[0:TP, 0:TP], t.above[:, 0, :],
                                              start=False, stop=True, skip_group_check=True)
                mm.then_inc(s_made, 1)

            def shifted_scores(n, h):
                m = NH * n + h
                if h % NHALF == 0:
                    pe.wait_ge(max_loaded, 16 * (halves * n + h // NHALF + 1))
                pe.wait_ge(exp_made, m)
                for i in range(NT):
                    q0 = min(i, 1) * TP if causal else 0
                    mm = nc.tensor.matmul(p_t[:, i, q0:S], kst[:, ds(n % ring, 1), h, TP * i:TP * i + TP].rearrange("p a n -> p (a n)"),
                                          qst[:, ds(n % ring, 1), h, q0:S].rearrange("p a n -> p (a n)"),
                                          start=True, stop=not causal, skip_group_check=causal)
                    if causal:
                        if q0 < TP * i:
                            nc.tensor.matmul(p_t[:, i, q0:TP * i], t.identb[0:TP, 0:TP], t.above[:, 2, :],
                                             start=False, stop=False, skip_group_check=True)
                        mm = nc.tensor.matmul(p_t[:, i, TP * i:TP * i + TP], t.identb[0:TP, 0:TP], t.above[:, 1, :],
                                              start=False, stop=True, skip_group_check=True)
                mm.then_inc(t_made, 1)

            def times_values(n, h):
                m = NH * n + h
                pe.wait_ge(exp_made, m + 1)
                if h % NHALF == 0:
                    pe.wait_ge(o_free, halves * n + h // NHALF + 1)
                o = o_view(h // NHALF)
                for j in range(NT):
                    blocks = range(j + 1) if causal else range(NT)
                    for i in blocks:
                        mm = nc.tensor.matmul(o[:, j, h % NHALF, :], probs[h % 2][:, i, TP * j:TP * j + TP],
                                              t.v[:, ds(NT * n + i, 1), h, :].rearrange("p a d -> p (a d)"),
                                              start=(i == 0), stop=(i == blocks[-1]))
                mm.then_inc(probs_free, 1)

            def batch(n, first, second):
                for h in range(NH):
                    if first:
                        scores(n, h)
                    if second:
                        shifted_scores(n - 1, h)
                        if h:
                            times_values(n - 1, h - 1)
                if second:
                    times_values(n - 1, NH - 1)
                    pe.wait_ge(t_made, NH * n)
                    pe.sem_inc(stack_free, 1)

            pe.sem_inc(stack_free, ring)
            pe.sem_inc(probs_free, 2)
            pe.wait_ge(ones_set, 2)
            batch(0, True, False)
            with pe.Fori(1, B) as n:
                batch(n, True, True)
            batch(B, False, True)

        @block.scalar
        def _(act):
            with act.Fori(0, B) as n:
                for h in range(NH):
                    m = NH * n + h
                    act.wait_ge(t_made, m + 1)
                    act.wait_ge(probs_free, m + 1)
                    if causal:
                        nc.scalar.activation(probs[h % 2][:, 0, :], p_t[:, 0, 0:S], ACT.Exp)
                        ins = nc.scalar.activation(probs[h % 2][:, 1:NT, TP:S], p_t[:, 1:NT, TP:S], ACT.Exp)
                    else:
                        ins = nc.scalar.activation(probs[h % 2][:, :, :], p_t[:, :, 0:S], ACT.Exp)
                    ins.then_inc(exp_made, 1)

        @block.vector
        def _(dve):
            def maxima(n, h):
                dve.wait_ge(s_made, NH * n + h + 1)
                if h == 0:
                    dve.wait_ge(max_cut, halves * n)
                if causal:
                    for j in range(NT):
                        ins = nc.vector.tensor_reduce(nmax[:, j, h:h + 1], p_s[:, j, 0:TP * (j + 1)], AX_X, ALU.max, negate=True)
                else:
                    ins = nc.vector.tensor_reduce(nmax[:, :, h], p_s[:, :, 0:S], AX_X, ALU.max, negate=True)
                ins.then_inc(s_max, 1)

            def cut_maxima(n, half):
                m = halves * n + half
                dve.wait_ge(s_max, NH * n + NHALF * half + NHALF)
                x = nmax[:, :, NHALF * half:NHALF * half + NHALF]
                part = [mparts[0:TP, :, NHALF * a:NHALF * a + NHALF] for a in range(NPART)]
                dve.wait_ge(max_stored, 16 * len(chunks) * m)
                t.dve.did(nc.vector.tensor_copy(part[0], x))
                t.dve.wait()
                t.dve.did(nc.vector.tensor_tensor(mrest[:, :, :], x, part[0], ALU.subtract))
                t.dve.wait()
                t.dve.did(nc.vector.tensor_copy(part[1], mrest[:, :, :]))
                t.dve.wait()
                t.dve.did(nc.vector.tensor_tensor(part[2], mrest[:, :, :], part[1], ALU.subtract))
                t.dve.wait()
                nc.vector.transpose(mturned[:, :, :], mparts[:, :, :]).then_inc(max_cut, 1)
                dve.wait_ge(max_cut, m + 1)

            def normalize(n, half):
                o = o_view(half)
                dve.wait_ge(probs_free, 2 + NH * n + NHALF * half + NHALF)
                dve.wait_ge(o_free, 2 + halves * n + half)
                t.dve.did(nc.vector.reciprocal(rsum[:, :, :], o[:, :, :, HD]))
                t.dve.wait()
                nc.vector.tensor_tensor(t.att[0:TP, ds(NT * n, NT), NHALF * HD * half:NHALF * HD * (half + 1)].rearrange("p j (h d) -> p j h d", h=NHALF),
                                        o[:, :, :, 0:HD], rsum[:, :, :].unsqueeze(3).to_broadcast([TP, NT, NHALF, HD]),
                                        ALU.mult).then_inc(o_free, 1)

            def batch(n, first, second):
                for h in range(NH):
                    if first:
                        maxima(n, h)
                        if h % NHALF == NHALF - 1:
                            cut_maxima(n, h // NHALF)
                    if second and h == NHALF + 1:
                        normalize(n - 1, 0)
                if second:
                    normalize(n - 1, 1)

            dve.sem_inc(o_free, 2)
            dve.wait_ge(ones_set, 2)
            batch(0, True, False)
            with dve.Fori(0, B - 1) as i:
                t.dve.enter(i, 5 * halves)
                batch(i + 1, True, True)
                t.dve.leave(B - 1)
            batch(B, False, True)


def attention_out(nc, t, name, rank, new_sem, ctx):
    def sb(name_, shape, dt=F32):
        return ctx.enter_context(nc.sbuf_tensor(name + name_, shape, dt))

    def ps(name_, shape, dt=F32):
        return ctx.enter_context(nc.psum_tensor(name + name_, shape, dt))

    def sm(name_):
        return new_sem(name + name_)

    a_copied, a_turned, a_ready, a_used = sm("_a_copied"), sm("_a_turned"), sm("_a_ready"), sm("_a_used")
    r_made, r_ready, y_made, y_added, biased = sm("_r_made"), sm("_r_ready"), sm("_y_made"), sm("_y_added"), sm("_biased")
    a = sb("_a", [TP, NT, D])
    aT = sb("_aT", [128, 2, S])
    p_a = ps("_pa", [128, 2, 512])
    p_y = [ps(f"_py{k}", [TP, 2, D]) for k in range(2)]
    banks = ((0, 2), (2, 1))
    if rank:
        p_r = ps("_pr", [128, 512])
        rT = sb("_rT", [128, S])

    with nc.Block() as block:
        @block.gpsimd
        def _(pool):
            with pool.Fori(0, B) as n:
                pool.wait_ge(a_turned, n)
                settle(pool, t)
                nc.gpsimd.tensor_copy(a[:, :, :], t.att[0:TP, ds(NT * n, NT), :]).then_inc(a_copied, 1)

        @block.tensor
        def _(pe):
            with pe.Fori(0, B) as n:
                pe.wait_ge(a_copied, n + 1)
                pe.wait_ge(a_ready, n)
                for c in range(2):
                    for j in range(NT):
                        mm = nc.tensor.transpose(p_a[:, c, TP * j:TP * j + TP], a[:, j, 128 * c:128 * c + 128], t.ident[0:TP, 0:TP])
                mm.then_inc(a_turned, 1)
                pe.wait_ge(a_ready, n + 1)
                if rank:
                    for c in range(2):
                        mm = nc.tensor.matmul(p_r[96:128, 0:S], t.basis_o[:, c, :], aT[:, c, :], start=(c == 0), stop=(c == 1))
                    mm.then_inc(r_made, 1)
                    pe.wait_ge(r_ready, n + 1)
                for k, (j0, m) in enumerate(banks):
                    pe.wait_ge(y_added, 2 * n + k)
                    for j in range(j0, j0 + m):
                        if rank:
                            mm = nc.tensor.matmul(p_y[k][:, j - j0, :], rT[96:128, TP * j:TP * j + TP], t.holo[96:128, :],
                                                  start=True, stop=True)
                        else:
                            for c in range(2):
                                mm = nc.tensor.matmul(p_y[k][:, j - j0, :], aT[:, c, TP * j:TP * j + TP], t.wo[:, c, :],
                                                      start=(c == 0), stop=(c == 1))
                    mm.then_inc(y_made, 1)

        @block.scalar
        def _(act):
            with act.Fori(0, B) as n:
                act.wait_ge(a_turned, n + 1)
                act.wait_ge(y_made, 2 * n)
                nc.scalar.activation(aT[:, :, :], p_a[:, :, 0:S], ACT.Copy).then_inc(a_ready, 1)
                if rank:
                    act.wait_ge(r_made, n + 1)
                    nc.scalar.activation(rT[96:128, :], p_r[96:128, 0:S], ACT.Copy).then_inc(r_ready, 1)

        @block.vector
        def _(dve):
            with dve.Fori(0, B) as n:
                for k, (j0, m) in enumerate(banks):
                    h = t.h[:, ds(NT * n + j0, m), :]
                    if not rank:
                        bias = t.bo[:, :].unsqueeze(1).to_broadcast([TP, m, D])
                        nc.vector.tensor_tensor(h, h, bias, ALU.add).then_inc(biased, 1)
                    dve.wait_ge(y_made, 2 * n + k + 1)
                    if not rank:
                        dve.wait_ge(biased, 2 * n + k + 1)
                    nc.vector.tensor_tensor(h, h, p_y[k][:, 0:m, :], ALU.add).then_inc(y_added, 1)


def prefill(nc, t, new_sem):
    rows_filled, tile_ready = new_sem("rows_filled"), new_sem("row_tile_ready")
    fills = []
    for d in (t.disp0, t.disp1):
        per = d.shape[0] // 128
        for a in range(0, per, 8):
            m = min(8, per - a)
            fills.append((d[128 * a:128 * (a + m), :].rearrange("(e p) r -> p e r", p=128),
                          t.empty[:, :].unsqueeze(1).to_broadcast([128, m, ROW])))
    for d in (t.sum0, t.sum1):
        fills.append((d[0:T, :].rearrange("(g p) d -> p g d", p=TP), t.empty[0:TP, 0:D].unsqueeze(1).to_broadcast([TP, G, D])))
        fills.append((d[T:T + 128, :], t.empty[:, 0:D]))
    with nc.Block() as block:
        @block.gpsimd
        def _(pool):
            nc.gpsimd.memset(t.empty[:, :], 0.0).then_inc(tile_ready, 1)
            pool.wait_ge(tile_ready, 1)
            nc.gpsimd.iota(t.empty[:, TID:TID + 1].bitcast(U32), [[0, 1]], base=T, channel_multiplier=1).then_inc(tile_ready, 1)

        @block.sync
        def _(sp):
            sp.wait_ge(tile_ready, 2)
            for dst, src in fills:
                sp.dma_start(dst, src).then_inc(rows_filled, 16)
            sp.wait_ge(rows_filled, 16 * len(fills))


def route_and_share0(nc, io, t, new_sem, ctx):
    def sb(name, shape, dt=F32):
        return ctx.enter_context(nc.sbuf_tensor("r0_" + name, shape, dt))

    def ps(name, shape, dt=F32):
        return ctx.enter_context(nc.psum_tensor("r0_" + name, shape, dt))

    def sm(name):
        return new_sem("r0_" + name)

    xf = NormalizedTransposed(nc, t, "r0", new_sem, sb, ps)
    loaded, filled, row_filled, tid_written = sm("loaded"), sm("filled"), sm("row_filled"), sm("tid_written")
    lg_made, lg_shifted, exp_made, lg_read = sm("lg_made"), sm("lg_shifted"), sm("exp_made"), sm("lg_read")
    taken_ready, pos_made, pos_read, sent = sm("taken_ready"), sm("pos_made"), sm("pos_read"), sm("sent")
    taken_added, places_ready = sm("taken_added"), sm("places_ready")
    h1_made, h3_made, s_ready, g_ready, z_made, z_added = (sm("h1_made"), sm("h3_made"), sm("s_ready"), sm("g_ready"),
                                                           sm("z_made"), sm("z_added"))
    gate = sb("gate", [128, 2, E0])
    gate_b = sb("gate_b", [TP, E0])
    ws1, ws3 = sb("ws1", [128, 2, 2 * I0]), sb("ws3", [128, 2, 2 * I0])
    ws2 = sb("ws2", [IC, SIC, D])
    before32, before = sb("before32", [TP, TP]), sb("before", [TP, TP], BF16)
    ones = sb("ones", [TP, TP], BF16)
    rows = sb("rows", [TP, NT, ROW])
    mx, total = sb("mx", [TP, NT]), sb("total", [TP, NT])
    lg, scores, biased = sb("lg", [TP, NT, E0]), sb("scores", [TP, NT, E0]), sb("biased", [TP, NT, E0])
    top, topi = sb("top", [TP, NT, 8]), sb("topi", [TP, NT, 8], U32)
    pick, work = sb("pick", [TP, NT, K0, E0]), sb("work", [TP, NT, K0, E0])
    taken, taken_before = sb("taken", [TP, NT, E0], BF16), sb("taken_before", [TP, E0], BF16)
    place, keep = sb("place", [TP, NT, K0]), sb("keep", [TP, NT, K0])
    slots = sb("slots", [TP, NT, K0], U32)
    tidu, tid = sb("tidu", [TP, NT], U32), sb("tid", [TP, NT])
    silu = [sb(f"silu{u}", [IC, S]) for u in range(2)]
    g = sb("g", [IC, SIC, S])
    p_rt = ps("prt", [TP, 2, 256])
    p_h = [[ps(f"ph{w}{u}", [IC, 512]) for u in range(2)] for w in (1, 3)]
    p_z = ps("pz", [TP, 512])
    loads = [(gate[:, :, :], io["gate0"]), (gate_b[:, :], io["gate0_b"].partition_broadcast(TP)), (ws1[:, :, :], io["ws1"]),
             (ws3[:, :, :], io["ws3"]), (ws2[:, :, :], io["ws2"]), (before32[:, :], io["before"])]
    p_lg = p_rt[:, 0, 0:NT * E0].rearrange("p (j e) -> p j e", j=NT)
    p_pos = p_rt[:, 1, 0:NT * E0].rearrange("p (j e) -> p j e", j=NT)
    ids, wts = rows[:, :, IDS:IDS + K0], rows[:, :, WTS:WTS + K0]

    def each_choice(x):
        return x.unsqueeze(2).to_broadcast([TP, NT, K0, E0])

    with nc.Block() as block:
        @block.sync
        def _(sp):
            for dst, src in loads:
                sp.dma_start(dst, src).then_inc(loaded, 16)

        @block.gpsimd
        def _(pool):
            nc.gpsimd.iota(tidu[:, :], [[TP, NT]], base=0, channel_multiplier=1).then_inc(filled, 1)
            pool.wait_ge(filled, 1)
            nc.gpsimd.memset(ones[:, :], 1.0).then_inc(filled, 1)
            pool.wait_ge(filled, 2)
            nc.gpsimd.memset(taken_before[:, :], 0.0).then_inc(filled, 1)
            pool.wait_ge(filled, 3)
            nc.gpsimd.memset(rows[:, :, IDS:ROW], 0.0).then_inc(filled, 1)
            pool.wait_ge(filled, 4)
            with pool.Fori(0, B) as n:
                t.pool.enter(n, xf.POOL_STEPS)
                xf.invert(pool, n)
                pool.wait_ge(places_ready, n + 1)
                pool.wait_ge(row_filled, n + 1)
                settle(pool, t)
                for j in range(NT):
                    for k in range(K0):
                        nc.gpsimd.indirect_dma_start(t.disp0, bass.IndirectOffsetOnAxis(ap=slots[:, j, k:k + 1], axis=0),
                                                     rows[:, j, :], None, bounds_check=E0 * CAP - 1,
                                                     oob_is_err=False).then_inc(sent, 16)
                t.pool.leave(B)
            pool.wait_ge(sent, 16 * NT * K0 * B)

        @block.tensor
        def _(pe):
            pe.wait_ge(loaded, 16 * len(loads))
            pe.wait_ge(tid_written, 1)
            with pe.Fori(0, B) as n:
                xf.turn(pe, n)
                pe.wait_ge(xf.xt_ready, n + 1)
                pe.wait_ge(pos_read, n)
                for j in range(NT):
                    for c in range(2):
                        mm = nc.tensor.matmul(p_lg[:, j, :], xf.xT[:, c, TP * j:TP * j + TP], gate[:, c, :], start=(c == 0), stop=(c == 1))
                mm.then_inc(lg_made, 1)
                for c in range(SIC):
                    m = SIC * n + c
                    if c >= 2:
                        pe.wait_ge(g_ready, m - 1)
                    else:
                        pe.wait_ge(g_ready, SIC * n)
                    for w, (weights, made) in enumerate(((ws1, h1_made), (ws3, h3_made))):
                        for k in range(2):
                            mm = nc.tensor.matmul(p_h[w][c % 2][:, 0:S], weights[:, k, IC * c:IC * c + IC], xf.xT[:, k, :],
                                                  start=(k == 0), stop=(k == 1))
                        mm.then_inc(made, 1)
                pe.wait_ge(h3_made, SIC * (n + 1))
                pe.sem_inc(xf.xt_used, 1)
                pe.wait_ge(taken_ready, n + 1)
                for j in range(NT):
                    nc.tensor.matmul(p_pos[:, j, :], before[:, :], taken[:, j, :], start=True, stop=False)
                    for i in range(j):
                        nc.tensor.matmul(p_pos[:, j, :], ones[:, :], taken[:, i, :], start=False, stop=False)
                    mm = nc.tensor.matmul(p_pos[:, j, :], ones[:, :], taken_before[:, :], start=False, stop=True)
                mm.then_inc(pos_made, 1)
                pe.wait_ge(g_ready, SIC * (n + 1))
                for j in range(NT):
                    pe.wait_ge(z_added, NT * n + j)
                    for c in range(SIC):
                        mm = nc.tensor.matmul(p_z[:, 0:D], g[:, c, TP * j:TP * j + TP], ws2[:, c, :],
                                              start=(c == 0), stop=(c == SIC - 1))
                    mm.then_inc(z_made, 1)

        @block.scalar
        def _(act):
            with act.Fori(0, B) as n:
                xf.copy(act, n)
                act.wait_ge(xf.xn_ready, n + 1)
                act.wait_ge(sent, 16 * NT * K0 * n)
                nc.scalar.activation(rows[:, :, 0:D], xf.xn[:, :, :], ACT.Copy).then_inc(row_filled, 1)
                act.wait_ge(lg_shifted, n + 1)
                nc.scalar.activation(lg[:, :, :], lg[:, :, :], ACT.Exp).then_inc(exp_made, 1)
                for c in range(SIC):
                    m = SIC * n + c
                    act.wait_ge(h1_made, m + 1)
                    act.wait_ge(g_ready, SIC * n + max(c - 1, 0))
                    nc.scalar.activation(silu[c % 2][:, :], p_h[0][c % 2][:, 0:S], ACT.Silu).then_inc(s_ready, 1)

        @block.vector
        def _(dve):
            def step(ins):
                t.dve.did(ins)
                t.dve.wait()

            dve.wait_ge(loaded, 16 * len(loads))
            dve.wait_ge(filled, 4)
            step(nc.vector.tensor_copy(before[:, :], before32[:, :]))
            nc.vector.tensor_copy(tid[:, :], tidu[:, :]).then_inc(tid_written, 1)
            dve.wait_ge(tid_written, 1)
            with dve.Fori(0, B) as n:
                t.dve.enter(n, 30)
                xf.row_stats(dve, n)
                dve.wait_ge(row_filled, n)
                xf.normalize(dve, n)
                dve.wait_ge(lg_made, n + 1)
                step(nc.vector.tensor_reduce(mx[:, :], p_lg, AX_X, ALU.max))
                nc.vector.tensor_tensor(lg[:, :, :], p_lg, mx[:, :].unsqueeze(2).to_broadcast([TP, NT, E0]),
                                        ALU.subtract).then_inc(lg_shifted, 1)
                dve.wait_ge(exp_made, n + 1)
                step(nc.vector.tensor_reduce(total[:, :], lg[:, :, :], AX_X, ALU.add))
                step(nc.vector.reciprocal(total[:, :], total[:, :]))
                step(nc.vector.tensor_tensor(scores[:, :, :], lg[:, :, :], total[:, :].unsqueeze(2).to_broadcast([TP, NT, E0]), ALU.mult))
                step(nc.vector.tensor_tensor(biased[:, :, :], scores[:, :, :], gate_b[:, :].unsqueeze(1).to_broadcast([TP, NT, E0]), ALU.add))
                for j in range(NT):
                    settle(dve, t)
                    step(nc.vector.max(top[:, j, :], biased[:, j, :]))
                for j in range(NT):
                    settle(dve, t)
                    step(nc.vector.max_index(topi[:, j, :], top[:, j, :], biased[:, j, :]))
                dve.wait_ge(sent, 16 * NT * K0 * n)
                step(nc.vector.tensor_copy(ids, topi[:, :, 0:K0]))
                step(nc.vector.tensor_tensor(pick[:, :, :, :], t.iota[0:TP, 0:E0].unsqueeze(1).unsqueeze(1).to_broadcast([TP, NT, K0, E0]),
                                             ids.unsqueeze(3).to_broadcast([TP, NT, K0, E0]), ALU.is_equal))
                with nc.allow_low_precision(reason="zeros and ones are exact"):
                    nc.vector.tensor_reduce(taken[:, :, :], pick[:, :, :, :].rearrange("p j k e -> p j e k"), AX_X, ALU.add).then_inc(taken_ready, 1)
                step(nc.vector.tensor_tensor(work[:, :, :, :], pick[:, :, :, :], each_choice(scores[:, :, :]), ALU.mult))
                step(nc.vector.tensor_reduce(wts, work[:, :, :, :], AX_X, ALU.add))
                for c in range(SIC):
                    m = SIC * n + c
                    dve.wait_ge(s_ready, m + 1)
                    dve.wait_ge(h3_made, m + 1)
                    dve.wait_ge(z_made, NT * n)
                    nc.vector.tensor_tensor(g[:, c, :], silu[c % 2][:, :], p_h[1][c % 2][:, 0:S], ALU.mult).then_inc(g_ready, 1)
                dve.wait_ge(pos_made, n + 1)
                step(nc.vector.tensor_tensor(work[:, :, :, :], pick[:, :, :, :], each_choice(p_pos), ALU.mult))
                dve.sem_inc(pos_read, 1)
                step(nc.vector.tensor_reduce(place[:, :, :], work[:, :, :, :], AX_X, ALU.add))
                step(nc.vector.tensor_scalar(keep[:, :, :], place[:, :, :], float(CAP), None, ALU.is_lt))
                step(nc.vector.tensor_tensor(wts, wts, keep[:, :, :], ALU.mult))
                step(nc.vector.tensor_scalar(keep[:, :, :], keep[:, :, :], -float(E0 * CAP), float(E0 * CAP), ALU.mult, ALU.add))
                step(nc.vector.tensor_tensor(place[:, :, :], place[:, :, :], keep[:, :, :], ALU.add))
                step(nc.vector.scalar_tensor_tensor(out=place[:, :, :], in0=ids, scalar=float(CAP), in1=place[:, :, :], op0=ALU.mult, op1=ALU.add))
                step(nc.vector.tensor_copy(slots[:, :, :], place[:, :, :]))
                step(nc.vector.tensor_copy(rows[:, :, TID].bitcast(U32), tid[:, :]))
                nc.vector.tensor_scalar(tid[:, :], tid[:, :], float(S), None, ALU.add).then_inc(places_ready, 1)
                dve.wait_ge(places_ready, n + 1)
                for j in range(NT):
                    step(nc.vector.tensor_tensor(taken_before[:, :], taken_before[:, :], taken[:, j, :], ALU.add))
                for j in range(NT):
                    dve.wait_ge(z_made, NT * n + j + 1)
                    h = t.h[:, ds(NT * n + j, 1), :].rearrange("p a d -> p (a d)")
                    nc.vector.tensor_tensor(h, h, p_z[:, 0:D], ALU.add).then_inc(z_added, 1)
                dve.wait_ge(z_added, NT * (n + 1))
                t.dve.leave(B)


def experts0(nc, io, t, new_sem, ctx):
    def sb(name, shape, dt=F32):
        return ctx.enter_context(nc.sbuf_tensor("e0_" + name, shape, dt))

    def ps(name, shape, dt=F32):
        return ctx.enter_context(nc.psum_tensor("e0_" + name, shape, dt))

    def sm(name):
        return new_sem("e0_" + name)

    x_loaded = [sm(f"x_loaded{u}") for u in range(DEEP)]
    w_loaded = [sm(f"w_loaded{u}") for u in range(DEEP)]
    x_turned, x_ready, h1_made, h3_made, s_ready, g_ready = (sm("x_turned"), sm("x_ready"), sm("h1_made"), sm("h3_made"),
                                                             sm("s_ready"), sm("g_ready"))
    y_made, y_ready, y_added, x_free = sm("y_made"), sm("y_ready"), sm("y_added"), sm("x_free")
    x = [sb(f"x{u}", [128, ROW]) for u in range(DEEP)]
    w13 = [sb(f"w13{u}", [128, 2, 2 * I0]) for u in range(DEEP)]
    w2 = [sb(f"w2{u}", [IC, 2, D]) for u in range(DEEP)]
    xT = [sb(f"xT{u}", [128, 2, 128]) for u in range(2)]
    silu = [sb(f"silu{u}", [IC, 2, 128]) for u in range(2)]
    g = [sb(f"g{u}", [IC, 2, 128]) for u in range(2)]
    y = [sb(f"y{u}", [128, D]) for u in range(2)]
    match, weight = [sb(f"match{u}", [128, K0]) for u in range(2)], [sb(f"weight{u}", [128, 1]) for u in range(2)]
    p_x = [ps(f"px{u}", [128, 4, 128]) for u in range(2)]
    p_h = [[ps(f"ph{w}{u}", [IC, 4, 128]) for u in range(2)] for w in (1, 3)]
    p_y = [ps(f"py{u}", [128, 512]) for u in range(2)]
    rounds = E0 // DEEP

    def before(e, n):
        return max(e - n + 1, 0) if isinstance(e, int) else e - n + 1

    with nc.Block() as block:
        @block.sync
        def _(sp):
            with sp.Fori(0, rounds) as i:
                for u in range(DEEP):
                    e = DEEP * i + u
                    sp.wait_ge(x_free, e + 1)
                    sp.dma_start(w13[u][:, :, :], io["w13"][ds(e, 1)].rearrange("e p c i -> p (e c) i")).then_inc(w_loaded[u], 16)
                    sp.dma_start(w2[u][:, :, :], io["w2"][ds(e, 1)].rearrange("e p c d -> p (e c) d")).then_inc(w_loaded[u], 16)
                    sp.dma_start(x[u][:, :], t.disp0[ds(CAP * e, CAP), :]).then_inc(x_loaded[u], 16)

        @block.tensor
        def _(pe):
            def turn(i, u):
                e = DEEP * i + u
                pe.wait_ge(x_loaded[u], 16 * (i + 1))
                pe.wait_ge(x_ready, before(e, 2))
                for c in range(2):
                    mm = nc.tensor.transpose(p_x[u % 2][:, c, :], x[u][:, 128 * c:128 * c + 128], t.ident[:, :])
                mm.then_inc(x_turned, 1)

            def up(i, u):
                e = DEEP * i + u
                pe.wait_ge(x_ready, e + 1)
                pe.wait_ge(w_loaded[u], 32 * (i + 1))
                pe.wait_ge(g_ready, before(e, 2))
                for w, made in ((0, h1_made), (1, h3_made)):
                    for m in range(2):
                        for c in range(2):
                            mm = nc.tensor.matmul(p_h[w][u % 2][:, m, :], w13[u][:, c, I0 * w + IC * m:I0 * w + IC * m + IC],
                                                  xT[u % 2][:, c, :], start=(c == 0), stop=(c == 1))
                    mm.then_inc(made, 1)

            def down(i, u):
                e = DEEP * i + u
                pe.wait_ge(g_ready, e + 1)
                pe.wait_ge(y_ready, before(e, 2))
                for m in range(2):
                    mm = nc.tensor.matmul(p_y[u % 2][:, 0:D], g[u % 2][:, m, :], w2[u][:, m, :], start=(m == 0), stop=(m == 1))
                mm.then_inc(y_made, 1)

            def experts(i, first, last):
                for u in range(DEEP):
                    if u < DEEP - 1:
                        turn(i, u + 1)
                    elif not last:
                        turn(i + 1, 0)
                    up(i, u)
                    if u:
                        down(i, u - 1)
                    elif not first:
                        down(i - 1, DEEP - 1)

            turn(0, 0)
            experts(0, True, False)
            with pe.Fori(1, rounds - 1) as i:
                experts(i, False, False)
            experts(rounds - 1, False, True)
            down(rounds - 1, DEEP - 1)

        @block.scalar
        def _(act):
            def copy_x(i, u):
                e = DEEP * i + u
                act.wait_ge(x_turned, e + 1)
                act.wait_ge(h3_made, before(e, 2))
                nc.scalar.activation(xT[u % 2][:, :, :], p_x[u % 2][:, 0:2, :], ACT.Copy).then_inc(x_ready, 1)

            def gate(i, u):
                e = DEEP * i + u
                act.wait_ge(h1_made, e + 1)
                act.wait_ge(g_ready, before(e, 2))
                nc.scalar.activation(silu[u % 2][:, :, :], p_h[0][u % 2][:, 0:2, :], ACT.Silu).then_inc(s_ready, 1)

            def experts(i, last):
                for u in range(DEEP):
                    if u < DEEP - 1:
                        copy_x(i, u + 1)
                    elif not last:
                        copy_x(i + 1, 0)
                    gate(i, u)

            copy_x(0, 0)
            experts(0, False)
            with act.Fori(1, rounds - 1) as i:
                experts(i, False)
            experts(rounds - 1, True)

        @block.vector
        def _(dve):
            def gated(i, u):
                e = DEEP * i + u
                dve.wait_ge(x_loaded[u], 16 * (i + 1))
                dve.wait_ge(y_ready, before(e, 2))
                t.dve.did(nc.vector.tensor_scalar(match[u % 2][:, :], x[u][:, IDS:IDS + K0], t.iota[:, ds(e, 1)], None, ALU.is_equal))
                t.dve.wait()
                t.dve.did(nc.vector.tensor_tensor_reduce(match[u % 2][:, :], match[u % 2][:, :], x[u][:, WTS:WTS + K0], 1.0, 0.0,
                                                         ALU.mult, ALU.add, weight[u % 2][:, :]))
                dve.wait_ge(s_ready, e + 1)
                dve.wait_ge(h3_made, e + 1)
                dve.wait_ge(y_made, before(e, 2))
                nc.vector.tensor_tensor(g[u % 2][:, :, :], silu[u % 2][:, :, :], p_h[1][u % 2][:, 0:2, :], ALU.mult).then_inc(g_ready, 1)

            def weighted(i, u):
                e = DEEP * i + u
                dve.wait_ge(y_made, e + 1)
                t.dve.wait()
                dve.wait_ge(y_added, 16 * before(e, 2))
                nc.vector.tensor_scalar(y[u % 2][:, :], p_y[u % 2][:, 0:D], weight[u % 2][:, :], None, ALU.mult).then_inc(y_ready, 1)

            def experts(i, first):
                for u in range(DEEP):
                    gated(i, u)
                    if u:
                        weighted(i, u - 1)
                    elif not first:
                        weighted(i - 1, DEEP - 1)

            experts(0, True)
            with dve.Fori(0, rounds - 1) as i:
                t.dve.enter(i, 2 * DEEP)
                experts(i + 1, False)
                t.dve.leave(rounds - 1)
            weighted(rounds - 1, DEEP - 1)

        @block.gpsimd
        def _(pool):
            pool.sem_inc(x_free, DEEP)
            with pool.Fori(0, rounds) as i:
                for u in range(DEEP):
                    e = DEEP * i + u
                    pool.wait_ge(y_ready, e + 1)
                    settle(pool, t)
                    nc.gpsimd.indirect_dma_start(t.sum0, bass.IndirectOffsetOnAxis(ap=x[u][:, TID:TID + 1].bitcast(U32), axis=0),
                                                 y[u % 2][:, :], None, bounds_check=T + 127, oob_is_err=True,
                                                 compute_op=ALU.add).then_inc(y_added, 16)
                    pool.wait_ge(y_added, 16 * (e + 1))
                    pool.sem_inc(x_free, 1)


def rotary_qkv(nc, io, t, new_sem, ctx):
    def sb(name, shape, dt=F32):
        return ctx.enter_context(nc.sbuf_tensor("p1_" + name, shape, dt))

    def ps(name, shape, dt=F32):
        return ctx.enter_context(nc.psum_tensor("p1_" + name, shape, dt))

    def sm(name):
        return new_sem("p1_" + name)

    xf = NormalizedTransposed(nc, t, "p1", new_sem, sb, ps)
    cut = [Splitter(nc, t, "p1_q", 0, float(HD) ** -0.5, new_sem, sb), Splitter(nc, t, "p1_k", 1, 1.0, new_sem, sb)]
    loaded, sums_loaded, ones_set = sm("loaded"), sm("sums_loaded"), sm("ones_set")
    c_made, c_ready = sm("c_made"), sm("c_ready")
    rope_made, rope_read, low_made, low_ready = sm("rope_made"), sm("rope_read"), sm("low_made"), sm("low_ready")
    rope_ready, high_ready, v_made, v_ready = sm("rope_ready"), sm("high_ready"), sm("v_made"), sm("v_ready")
    w_c = sb("w_c", [128, 2, 128])
    w_low = sb("w_low", [128, 128])
    w_rope = [[sb(f"w_rope{w}{x}", [128, 2, 128]) for x in range(2)] for w in range(2)]
    biases = sb("biases", [128, 7])
    w_v = sb("w_v", [128, D])
    b_v = sb("b_v", [TP, D])
    trig = sb("trig", [128, 2, S])
    cT = sb("cT", [128, S])
    turned = [sb(f"turned{x}", [128, S]) for x in range(2)]
    act_in = [sb(f"qk{w}", [128, 2, S]) for w in range(2)]
    p_c = ps("pc", [128, 512])
    p_r = [ps(f"pr{x}", [128, 512]) for x in range(2)]
    p_l = ps("pl", [128, 512])
    p_v = ps("pv", [TP, 2, D])
    loads = [(w_c[:, :, :], io["w_c"]), (w_low[:, :], io["w_low"]), (biases[:, :], io["biases"]), (w_v[64:128, :], io["w_v"]),
             (b_v[:, :], io["b_v"].partition_broadcast(TP)), (trig[:, :, :], io["rope"])]
    loads += [(w_rope[w][x][:, :, :], io["w_rope"][w, x]) for w in range(2) for x in range(2)]

    with nc.Block() as block:
        @block.sync
        def _(sp):
            sp.dma_start(t.att[0:TP, :, :], t.sum0[0:T, :].rearrange("(g p) d -> p g d", p=TP)).then_inc(sums_loaded, 16)
            for dst, src in loads:
                sp.dma_start(dst, src).then_inc(loaded, 16)
            with sp.Fori(0, B) as n:
                for c in cut:
                    c.store(sp, n)
            for c in cut:
                sp.wait_ge(c.stored, 16 * B)

        @block.tensor
        def _(pe):
            pe.wait_ge(loaded, 16 * len(loads))
            with pe.Fori(0, B) as n:
                xf.turn(pe, n)
                pe.wait_ge(xf.xt_ready, n + 1)
                for c in range(2):
                    mm = nc.tensor.matmul(p_c[:, 0:S], w_c[:, c, :], xf.xT[:, c, :], start=(c == 0), stop=(c == 1))
                mm.then_inc(c_made, 1)
                for w in range(2):
                    m = 2 * n + w
                    pe.wait_ge(rope_read, m)
                    for x in range(2):
                        for c in range(2):
                            mm = nc.tensor.matmul(p_r[x][:, 0:S], w_rope[w][x][:, c, :], xf.xT[:, c, :], start=(c == 0), stop=(c == 1))
                    mm.then_inc(rope_made, 1)
                    pe.wait_ge(c_ready, n + 1)
                    pe.wait_ge(low_ready, m)
                    nc.tensor.matmul(p_l[:, 0:S], w_low[64 * w:64 * w + 64, :], cT[64 * w:64 * w + 64, :],
                                     start=True, stop=True).then_inc(low_made, 1)
                pe.wait_ge(rope_made, 2 * n + 2)
                pe.sem_inc(xf.xt_used, 1)
                for half, tiles in enumerate(([0, 1], [2])):
                    pe.wait_ge(v_ready, 2 * n + half)
                    for j in tiles:
                        mm = nc.tensor.matmul(p_v[:, j % 2, :], cT[64:128, TP * j:TP * j + TP], w_v[64:128, :], start=True, stop=True)
                    mm.then_inc(v_made, 1)

        @block.scalar
        def _(act):
            with act.Fori(0, B) as n:
                xf.copy(act, n)
                act.wait_ge(c_made, n + 1)
                act.wait_ge(v_made, 2 * n)
                nc.scalar.activation(cT[:, :], p_c[:, 0:S], ACT.Gelu, bias=biases[:, 0:1]).then_inc(c_ready, 1)
                for w in range(2):
                    m = 2 * n + w
                    act.wait_ge(low_made, m + 1)
                    act.wait_ge(cut[w].rest_ready, n)
                    nc.scalar.activation(act_in[w][:, 0, :], p_l[:, 0:S], ACT.Gelu, bias=biases[:, 1 + w:2 + w]).then_inc(low_ready, 1)
                    act.wait_ge(rope_ready, m + 1)
                    nc.scalar.activation(act_in[w][:, 1, :], turned[0][:, :], ACT.Gelu).then_inc(high_ready, 1)
                    act.wait_ge(low_ready, m + 1)
                    act.wait_ge(high_ready, m + 1)
                    cut[w].first(act, n, act_in[w][:, :, :])

        @block.vector
        def _(dve):
            dve.wait_ge(sums_loaded, 16)
            dve.wait_ge(loaded, 16 * len(loads))
            with dve.Fori(0, B) as n:
                t.dve.enter(n, 1 + xf.STEPS + 4)
                h = t.h[:, ds(NT * n, NT), :]
                t.dve.did(nc.vector.tensor_tensor(h, h, t.att[0:TP, ds(NT * n, NT), :], ALU.add))
                t.dve.wait()
                xf.row_stats(dve, n)
                xf.normalize(dve, n)
                for w in range(2):
                    m = 2 * n + w
                    dve.wait_ge(rope_made, m + 1)
                    dve.wait_ge(high_ready, m)
                    t.dve.did(nc.vector.scalar_tensor_tensor(out=turned[0][:, :], in0=p_r[0][:, 0:S], scalar=biases[:, 3 + 2 * w:4 + 2 * w],
                                                             in1=trig[:, 0, :], op0=ALU.add, op1=ALU.mult))
                    t.dve.did(nc.vector.scalar_tensor_tensor(out=turned[1][:, :], in0=p_r[1][:, 0:S], scalar=biases[:, 4 + 2 * w:5 + 2 * w],
                                                             in1=trig[:, 1, :], op0=ALU.add, op1=ALU.mult))
                    t.dve.wait()
                    dve.sem_inc(rope_read, 1)
                    nc.vector.tensor_tensor(turned[0][:, :], turned[0][:, :], turned[1][:, :], ALU.add).then_inc(rope_ready, 1)
                    dve.wait_ge(rope_ready, m + 1)
                for w in range(2):
                    cut[w].residue(dve, n, act_in[w][:, :, :])
                for half, tiles in enumerate(([0, 1], [2])):
                    dve.wait_ge(v_made, 2 * n + half + 1)
                    m = len(tiles)
                    nc.vector.tensor_tensor(t.v[:, ds(NT * n + tiles[0], m), :, 0:HD], p_v[:, 0:m, :].rearrange("p j (h d) -> p j h d", h=NH),
                                            b_v[:, :].rearrange("p (h d) -> p h d", h=NH).unsqueeze(1).to_broadcast([TP, m, NH, HD]),
                                            ALU.add).then_inc(v_ready, 1)
                for w in range(2):
                    cut[w].third(dve, n)
                t.dve.leave(B)

        @block.gpsimd
        def _(pool):
            with pool.Fori(0, B) as n:
                t.pool.enter(n, xf.POOL_STEPS)
                xf.invert(pool, n)
                for w in range(2):
                    cut[w].second(pool, n)
                t.pool.leave(B)


def route_and_share1(nc, io, t, new_sem, ctx):
    def sb(name, shape, dt=F32):
        return ctx.enter_context(nc.sbuf_tensor("r1_" + name, shape, dt))

    def ps(name, shape, dt=F32):
        return ctx.enter_context(nc.psum_tensor("r1_" + name, shape, dt))

    def sm(name):
        return new_sem("r1_" + name)

    K1 = 2
    MC = HID // 128
    xf = NormalizedTransposed(nc, t, "r1", new_sem, sb, ps)
    loaded, w_loaded, filled, row_filled, rows_ready, stored = (sm("loaded"), sm("w_loaded"), sm("filled"), sm("row_filled"),
                                                                 sm("rows_ready"), sm("stored"))
    tid_ready, xt_kept = sm("tid_ready"), sm("xt_kept")
    lg_made, lg_read, gap_ready, exp_made = sm("lg_made"), sm("lg_read"), sm("gap_ready"), sm("exp_made")
    taken_ready, pos_made, pos_read = sm("taken_ready"), sm("pos_made"), sm("pos_read")
    total_made, slots_ready = sm("total_made"), sm("slots_ready")
    back = [sm(f"back{u}") for u in range(2)]
    slot_copied, sent, = sm("slot_copied"), sm("sent")
    h_made, s_ready, z_made, z_added = sm("h_made"), sm("s_ready"), sm("z_made"), sm("z_added")
    gate = sb("gate", [128, 2, E1])
    before32, before = sb("before32", [TP, TP]), sb("before", [TP, TP], BF16)
    ones = sb("ones", [TP, 128], BF16)
    rows = sb("rows", [TP, NT, ROW])
    lg = sb("lg", [TP, NT, E1])
    top, topi = sb("top", [TP, NT, 8]), sb("topi", [TP, NT, 8], U32)
    gap = sb("gap", [TP, NT])
    pick, work = sb("pick", [TP, NT, K1, E1]), sb("work", [TP, NT, K1, E1])
    taken, taken_before = sb("taken", [TP, NT, E1], BF16), sb("taken_before", [TP, E1], BF16)
    place, expert = sb("place", [TP, G, K1]), sb("expert", [TP, G, K1])
    pick_all = sb("pick_all", [TP, G * K1, E1])
    slots = sb("slots", [TP, G, K1], U32)
    slot_now = [sb(f"slot_now{u}", [TP, NT * K1], U32) for u in range(2)]
    row_now = [sb(f"row_now{u}", [TP, NT, ROW]) for u in range(2)]
    tidu, tid = sb("tidu", [TP, NT], U32), sb("tid", [TP, NT])
    need, needu = sb("need", [128, E1]), sb("needu", [128, E1], U32)
    upto, start, plain = sb("upto", [128, E1]), sb("start", [128, E1]), sb("plain", [128, E1])
    over = sb("over", [128, SLOT_TILES, E1])
    silu = sb("silu", [128, MC, S])
    sw1, sw2 = sb("sw1", [128, 2, HID]), sb("sw2", [128, MC, D])
    kept = t.att[:, :, :].rearrange("p g d -> p (g d)")[:, 0:B * 2 * S].rearrange("p (n c s) -> p n c s", n=B, c=2)
    p_rt = ps("prt", [128, 2, 256])
    p_lg = p_rt[0:TP, 0, 0:NT * E1].rearrange("p (j e) -> p j e", j=NT)
    p_pos = p_rt[0:TP, 1, 0:NT * E1].rearrange("p (j e) -> p j e", j=NT)
    p_total = p_rt[:, 1, 0:E1]
    p_h = [ps(f"ph{u}", [128, 512]) for u in range(2)]
    p_z = [ps(f"pz{u}", [TP, 512]) for u in range(2)]
    loads = [(gate[:, :, :], io["gate1"]), (before32[:, :], io["before"]), (sw1[:, :, :], io["sw1"]), (sw2[:, :, :], io["sw2"])]
    ids, wts = rows[:, :, IDS:IDS + K1], rows[:, :, WTS:WTS + K1]

    with nc.Block() as block:
        @block.sync
        def _(sp):
            for dst, src in loads:
                sp.dma_start(dst, src).then_inc(loaded, 16)
            for e in range(E1):
                sp.dma_start(t.w1s[:, e, :, :], io["ew1"][e]).then_inc(w_loaded, 16)
            with sp.Fori(0, B) as n:
                sp.wait_ge(rows_ready, n + 1)
                sp.wait_ge(row_filled, n + 1)
                sp.dma_start(t.rows1[ds(S * n, S), :].rearrange("(j p) r -> p j r", p=TP), rows[:, :, :]).then_inc(stored, 16)
            sp.wait_ge(stored, 16 * B)
            sp.wait_ge(w_loaded, 16 * E1)
            with sp.Fori(0, B // 2) as i:
                for u in range(2):
                    n = 2 * i + u
                    sp.wait_ge(sent, 16 * NT * K1 * (2 * i))
                    sp.dma_start(row_now[u][:, :, :], t.rows1[ds(S * n, S), :].rearrange("(j p) r -> p j r", p=TP)).then_inc(back[u], 16)

        @block.gpsimd
        def _(pool):
            fills = [(ones[:, :], 1.0), (taken_before[:, :], 0.0), (rows[:, :, IDS:ROW], 0.0), (plain[:, :], 1.0)]
            for n, (dst, value) in enumerate(fills):
                nc.gpsimd.memset(dst, value).then_inc(filled, 1)
                pool.wait_ge(filled, n + 1)
            nc.gpsimd.iota(tidu[:, :], [[TP, NT]], base=0, channel_multiplier=1).then_inc(filled, 1)
            with pool.Fori(0, B) as n:
                t.pool.enter(n, xf.POOL_STEPS)
                xf.invert(pool, n)
                pool.wait_ge(xf.xt_ready, n + 1)
                settle(pool, t)
                nc.gpsimd.tensor_copy(kept[:, ds(n, 1), :, :].rearrange("p a c s -> p (a c) s"), xf.xT[:, :, :]).then_inc(xt_kept, 1)
                t.pool.leave(B)
            pool.wait_ge(slots_ready, 1)
            with pool.Fori(0, B // 2) as i:
                for u in range(2):
                    n = 2 * i + u
                    pool.wait_ge(sent, 16 * NT * K1 * n)
                    settle(pool, t)
                    nc.gpsimd.tensor_copy(slot_now[u][:, :], slots[:, ds(NT * n, NT), :].rearrange("p j k -> p (j k)")).then_inc(slot_copied, 1)
                    pool.wait_ge(slot_copied, n + 1)
                    pool.wait_ge(back[u], 16 * (i + 1))
                    settle(pool, t)
                    for j in range(NT):
                        for k in range(K1):
                            nc.gpsimd.indirect_dma_start(t.disp1, bass.IndirectOffsetOnAxis(ap=slot_now[u][:, K1 * j + k:K1 * j + k + 1], axis=0),
                                                         row_now[u][:, j, :], None, bounds_check=SLOT_TILES * 128 - 1,
                                                         oob_is_err=True).then_inc(sent, 16)
            pool.wait_ge(sent, 16 * NT * K1 * B)

        @block.tensor
        def _(pe):
            pe.wait_ge(loaded, 16 * len(loads))
            pe.wait_ge(tid_ready, 1)
            with pe.Fori(0, B) as n:
                xf.turn(pe, n)
                pe.wait_ge(xf.xt_ready, n + 1)
                pe.wait_ge(pos_read, n)
                for j in range(NT):
                    for c in range(2):
                        mm = nc.tensor.matmul(p_lg[:, j, :], xf.xT[:, c, TP * j:TP * j + TP], gate[:, c, :], start=(c == 0), stop=(c == 1))
                mm.then_inc(lg_made, 1)
                pe.wait_ge(lg_made, n + 1)
                pe.wait_ge(xt_kept, n + 1)
                pe.sem_inc(xf.xt_used, 1)
                pe.wait_ge(taken_ready, n + 1)
                for j in range(NT):
                    nc.tensor.matmul(p_pos[:, j, :], before[:, :], taken[:, j, :], start=True, stop=False)
                    for i in range(j):
                        nc.tensor.matmul(p_pos[:, j, :], ones[:, 0:TP], taken[:, i, :], start=False, stop=False)
                    mm = nc.tensor.matmul(p_pos[:, j, :], ones[:, 0:TP], taken_before[:, :], start=False, stop=True)
                mm.then_inc(pos_made, 1)
            pe.wait_ge(tid_ready, 1 + B)
            pe.wait_ge(pos_read, B)
            nc.tensor.matmul(p_total, ones[:, :], taken_before[:, :], start=True, stop=True).then_inc(total_made, 1)
            with pe.Fori(0, B) as n:
                for m in range(MC):
                    pe.wait_ge(s_ready, MC * n + max(m - 1, 0))
                    for c in range(2):
                        mm = nc.tensor.matmul(p_h[m % 2][:, 0:S], sw1[:, c, 128 * m:128 * m + 128], kept[:, ds(n, 1), c, :].rearrange("p a s -> p (a s)"),
                                              start=(c == 0), stop=(c == 1))
                    mm.then_inc(h_made, 1)
                pe.wait_ge(s_ready, MC * (n + 1))
                for j in range(NT):
                    pe.wait_ge(z_added, NT * n + max(j - 1, 0))
                    for m in range(MC):
                        mm = nc.tensor.matmul(p_z[j % 2][:, 0:D], silu[:, m, TP * j:TP * j + TP], sw2[:, m, :], start=(m == 0), stop=(m == MC - 1))
                    mm.then_inc(z_made, 1)

        @block.scalar
        def _(act):
            with act.Fori(0, B) as n:
                xf.copy(act, n)
                act.wait_ge(xf.xn_ready, n + 1)
                act.wait_ge(stored, 16 * n)
                nc.scalar.activation(rows[:, :, 0:D], xf.xn[:, :, :], ACT.Copy).then_inc(row_filled, 1)
                act.wait_ge(gap_ready, n + 1)
                nc.scalar.activation(gap[:, :], gap[:, :], ACT.Exp).then_inc(exp_made, 1)
            with act.Fori(0, B) as n:
                act.wait_ge(z_made, NT * n)
                for m in range(MC):
                    act.wait_ge(h_made, MC * n + m + 1)
                    nc.scalar.activation(silu[:, m, :], p_h[m % 2][:, 0:S], ACT.Silu).then_inc(s_ready, 1)

        @block.vector
        def _(dve):
            def step(ins):
                t.dve.did(ins)
                t.dve.wait()

            dve.wait_ge(loaded, 16 * len(loads))
            dve.wait_ge(filled, 5)
            step(nc.vector.tensor_copy(before[:, :], before32[:, :]))
            nc.vector.tensor_copy(tid[:, :], tidu[:, :]).then_inc(tid_ready, 1)
            dve.wait_ge(tid_ready, 1)
            with dve.Fori(0, B) as n:
                t.dve.enter(n, 20 + xf.STEPS)
                xf.row_stats(dve, n)
                dve.wait_ge(row_filled, n)
                xf.normalize(dve, n)
                dve.wait_ge(lg_made, n + 1)
                step(nc.vector.tensor_copy(lg[:, :, :], p_lg))
                for j in range(NT):
                    settle(dve, t)
                    step(nc.vector.max(top[:, j, :], lg[:, j, :]))
                for j in range(NT):
                    settle(dve, t)
                    step(nc.vector.max_index(topi[:, j, :], top[:, j, :], lg[:, j, :]))
                nc.vector.tensor_tensor(gap[:, :], top[:, :, 1], top[:, :, 0], ALU.subtract).then_inc(gap_ready, 1)
                dve.wait_ge(stored, 16 * n)
                step(nc.vector.tensor_copy(ids, topi[:, :, 0:K1]))
                step(nc.vector.tensor_copy(expert[:, ds(NT * n, NT), :], topi[:, :, 0:K1]))
                step(nc.vector.tensor_tensor(pick[:, :, :, :], t.iota[0:TP, 0:E1].unsqueeze(1).unsqueeze(1).to_broadcast([TP, NT, K1, E1]),
                                             ids.unsqueeze(3).to_broadcast([TP, NT, K1, E1]), ALU.is_equal))
                with nc.allow_low_precision(reason="zeros and ones are exact"):
                    nc.vector.tensor_reduce(taken[:, :, :], pick[:, :, :, :].rearrange("p j k e -> p j e k"), AX_X, ALU.add).then_inc(taken_ready, 1)
                dve.wait_ge(exp_made, n + 1)
                step(nc.vector.tensor_scalar(wts[:, :, 0], gap[:, :], 1.0, None, ALU.add))
                step(nc.vector.reciprocal(wts[:, :, 0], wts[:, :, 0]))
                step(nc.vector.tensor_tensor(wts[:, :, 1], wts[:, :, 0], gap[:, :], ALU.mult))
                step(nc.vector.tensor_copy(rows[:, :, TID].bitcast(U32), tid[:, :]))
                step(nc.vector.tensor_scalar(tid[:, :], tid[:, :], float(S), None, ALU.add))
                dve.sem_inc(rows_ready, 1)
                dve.wait_ge(pos_made, n + 1)
                step(nc.vector.tensor_tensor(work[:, :, :, :], pick[:, :, :, :], p_pos.unsqueeze(2).to_broadcast([TP, NT, K1, E1]), ALU.mult))
                dve.sem_inc(pos_read, 1)
                step(nc.vector.tensor_reduce(place[:, ds(NT * n, NT), :], work[:, :, :, :], AX_X, ALU.add))
                for j in range(NT):
                    step(nc.vector.tensor_tensor(taken_before[:, :], taken_before[:, :], taken[:, j, :], ALU.add))
                dve.sem_inc(tid_ready, 1)
                t.dve.leave(B)
            dve.wait_ge(total_made, 1)
            step(nc.vector.tensor_scalar(needu[:, :], p_total, 127.0, None, ALU.add))
            step(nc.vector.tensor_scalar(needu[:, :], needu[:, :], 7, None, ALU.logical_shift_right))
            step(nc.vector.tensor_copy(need[:, :], needu[:, :]))
            step(nc.vector.tensor_tensor_scan(upto[:, :], plain[:, :], need[:, :], 0.0, ALU.mult, ALU.add))
            step(nc.vector.tensor_tensor(start[:, :], upto[:, :], need[:, :], ALU.subtract))
            step(nc.vector.tensor_scalar(start[:, :], start[:, :], 128.0, None, ALU.mult))
            choice = [TP, G * K1, E1]
            experts_of = expert[:, :, :].rearrange("p g k -> p (g k)")
            places = place[:, :, :].rearrange("p g k -> p (g k)")
            step(nc.vector.tensor_tensor(pick_all[:, :, :], t.iota[0:TP, 0:E1].unsqueeze(1).to_broadcast(choice),
                                         experts_of.unsqueeze(2).to_broadcast(choice), ALU.is_equal))
            step(nc.vector.tensor_tensor(pick_all[:, :, :], pick_all[:, :, :], start[0:TP, :].unsqueeze(1).to_broadcast(choice), ALU.mult))
            step(nc.vector.tensor_reduce(experts_of, pick_all[:, :, :], AX_X, ALU.add))
            step(nc.vector.tensor_tensor(places, places, experts_of, ALU.add))
            nc.vector.tensor_copy(slots[:, :, :], place[:, :, :]).then_inc(slots_ready, 1)
            cells = [128, SLOT_TILES, E1]
            step(nc.vector.tensor_tensor(over[:, :, :], upto[:, :].unsqueeze(1).to_broadcast(cells),
                                         t.iota[:, 0:SLOT_TILES].unsqueeze(2).to_broadcast(cells), ALU.is_le))
            step(nc.vector.tensor_reduce(t.tile_expert[:, :], over[:, :, :], AX_X, ALU.add))
            step(nc.vector.tensor_scalar(t.tile_expert[:, :], t.tile_expert[:, :], float(E1 - 1), None, ALU.min))
            step(nc.vector.tensor_copy(t.tile_expert_u[:, :], t.tile_expert[:, :]))
            with dve.Fori(0, B) as n:
                for j in range(NT):
                    dve.wait_ge(z_made, NT * n + j + 1)
                    h = t.h[:, ds(NT * n + j, 1), :].rearrange("p a d -> p (a d)")
                    nc.vector.tensor_tensor(h, h, p_z[j % 2][:, 0:D], ALU.add).then_inc(z_added, 1)


def experts1(nc, io, t, new_sem, ctx):
    def sb(name, shape, dt=F32):
        return ctx.enter_context(nc.sbuf_tensor("e1_" + name, shape, dt))

    def ps(name, shape, dt=F32):
        return ctx.enter_context(nc.psum_tensor("e1_" + name, shape, dt))

    def sm(name):
        return new_sem("e1_" + name)

    K1, MC, HALF = 2, HID // 128, HID // 2
    w_loaded, x_loaded = sm("w_loaded"), [sm(f"x_loaded{u}") for u in range(2)]
    x_free, x_turned, x_ready = sm("x_free"), sm("x_turned"), sm("x_ready")
    h_made, s_ready, s_turned, g_ready = sm("h_made"), sm("s_ready"), sm("s_turned"), sm("g_ready")
    y_made, y_ready, y_added = sm("y_made"), sm("y_ready"), sm("y_added")
    w2s = sb("w2s", [128, E1, MC, D])
    x = [sb(f"x{u}", [128, ROW]) for u in range(2)]
    who = [sb(f"who{u}", [128, 2 * K1 + 1]) for u in range(2)]
    xT = [sb(f"xT{u}", [128, 2, 128]) for u in range(2)]
    silu = sb("silu", [128, HID])
    g = sb("g", [128, MC, 128])
    y = [sb(f"y{u}", [128, D]) for u in range(2)]
    match, weight = [sb(f"match{u}", [128, K1]) for u in range(2)], [sb(f"weight{u}", [128, 1]) for u in range(2)]
    p_x = ps("px", [128, 4, 128])
    p_h = [ps(f"ph{u}", [128, 512]) for u in range(2)]
    p_s = [ps(f"ps{u}", [128, 4, 128]) for u in range(2)]
    p_y = [ps(f"py{u}", [128, 512]) for u in range(2)]
    assert SLOT_TILES % 2 == 1

    with nc.Block() as block:
        @block.sync
        def _(sp):
            def load(i, r, u):
                sp.wait_ge(x_free, i + 1)
                sp.dma_start(x[u][:, :], t.disp1[ds(128 * i, 128), :]).then_inc(x_loaded[u], 16)

            load(0, 0, 0)
            for e in range(E1):
                sp.dma_start(w2s[:, e, :, :], io["ew2"][e]).then_inc(w_loaded, 16)
            with sp.Fori(0, (SLOT_TILES - 1) // 2) as r:
                load(2 * r + 1, r, 1)
                load(2 * r + 2, r, 0)

        @block.tensor
        def _(pe):
            def turn(i, r, u):
                pe.wait_ge(x_loaded[u], 16 * (r + 1))
                pe.wait_ge(x_ready, i)
                for c in range(2):
                    mm = nc.tensor.transpose(p_x[:, c, :], x[u][:, 128 * c:128 * c + 128], t.ident[:, :])
                mm.then_inc(x_turned, 1)

            def up(i, u):
                e = nc.tensor.value_load(t.tile_expert_u[0:1, ds(i, 1)], min_val=0, max_val=E1 - 1)
                pe.wait_ge(x_ready, i + 1)
                for m in range(2):
                    pe.wait_ge(s_ready, 2 * i - 1 + m if not isinstance(i, int) or i else 0)
                    for c in range(2):
                        mm = nc.tensor.matmul(p_h[m][:, :], xT[u][:, c, :], t.w1s[:, ds(e, 1), c, HALF * m:HALF * m + HALF].rearrange("p a n -> p (a n)"),
                                              start=(c == 0), stop=(c == 1))
                    mm.then_inc(h_made, 1)
                return e

            def turn_hidden(i):
                for m in range(2):
                    pe.wait_ge(s_ready, 2 * i + m + 1)
                    pe.wait_ge(g_ready, 2 * i - 1 + m if not isinstance(i, int) or i else 0)
                    for k in range(4):
                        mm = nc.tensor.transpose(p_s[m][:, k, :], silu[:, HALF * m + 128 * k:HALF * m + 128 * k + 128], t.ident[:, :])
                    mm.then_inc(s_turned, 1)

            def down(i, u):
                e = nc.tensor.value_load(t.tile_expert_u[0:1, ds(i, 1)], min_val=0, max_val=E1 - 1)
                pe.wait_ge(g_ready, 2 * i + 2)
                pe.wait_ge(y_ready, i)
                for m in range(MC):
                    mm = nc.tensor.matmul(p_y[u][:, 0:D], g[:, m, :], w2s[:, ds(e, 1), m, :].rearrange("p a n -> p (a n)"),
                                          start=(m == 0), stop=(m == MC - 1))
                mm.then_inc(y_made, 1)

            turn(0, 0, 0)
            up(0, 0)
            pe.wait_ge(w_loaded, 16 * E1)
            turn_hidden(0)
            turn(1, 0, 1)
            with pe.Fori(0, (SLOT_TILES - 3) // 2) as r:
                up(2 * r + 1, 1)
                down(2 * r, 0)
                turn_hidden(2 * r + 1)
                turn(2 * r + 2, r + 1, 0)
                up(2 * r + 2, 0)
                down(2 * r + 1, 1)
                turn_hidden(2 * r + 2)
                turn(2 * r + 3, r + 1, 1)
            last = SLOT_TILES - 1
            up(last - 1, 1)
            down(last - 2, 0)
            turn_hidden(last - 1)
            turn(last, last // 2, 0)
            up(last, 0)
            down(last - 1, 1)
            turn_hidden(last)
            down(last, 0)

        @block.scalar
        def _(act):
            def copy_x(i, u):
                act.wait_ge(x_turned, i + 1)
                act.wait_ge(h_made, 2 * i - 2 if not isinstance(i, int) or i > 1 else 0)
                nc.scalar.activation(xT[u][:, :, :], p_x[:, 0:2, :], ACT.Copy).then_inc(x_ready, 1)

            def hidden(i):
                for m in range(2):
                    act.wait_ge(h_made, 2 * i + m + 1)
                    act.wait_ge(s_turned, 2 * i - 1 + m if not isinstance(i, int) or i else 0)
                    nc.scalar.activation(silu[:, HALF * m:HALF * m + HALF], p_h[m][:, :], ACT.Silu).then_inc(s_ready, 1)

            copy_x(0, 0)
            hidden(0)
            with act.Fori(0, (SLOT_TILES - 1) // 2) as r:
                copy_x(2 * r + 1, 1)
                hidden(2 * r + 1)
                copy_x(2 * r + 2, 0)
                hidden(2 * r + 2)

        @block.vector
        def _(dve):
            def who_of(i, r, u):
                dve.wait_ge(x_loaded[u], 16 * (r + 1))
                dve.wait_ge(y_added, 16 * (max(i - 1, 0) if isinstance(i, int) else i - 1))
                t.dve.did(nc.vector.tensor_copy(who[u][:, 0:1], x[u][:, TID:TID + 1]))
                t.dve.did(nc.vector.tensor_scalar(match[u][:, :], x[u][:, IDS:IDS + K1], t.tile_expert[:, ds(i, 1)], None, ALU.is_equal))
                t.dve.wait()
                t.dve.did(nc.vector.tensor_tensor_reduce(match[u][:, :], match[u][:, :], x[u][:, WTS:WTS + K1], 1.0, 0.0,
                                                         ALU.mult, ALU.add, weight[u][:, :]))
                t.dve.wait()
                dve.wait_ge(x_turned, i + 1)
                dve.sem_inc(x_free, 1)

            def copy_hidden(i):
                for m in range(2):
                    dve.wait_ge(s_turned, 2 * i + m + 1)
                    dve.wait_ge(y_made, i)
                    nc.vector.tensor_copy(g[:, 4 * m:4 * m + 4, :], p_s[m][:, :, :]).then_inc(g_ready, 1)

            def weighted(i, u):
                dve.wait_ge(y_made, i + 1)
                dve.wait_ge(y_added, 16 * (max(i - 1, 0) if isinstance(i, int) else i - 1))
                nc.vector.tensor_scalar(y[u][:, :], p_y[u][:, 0:D], weight[u][:, :], None, ALU.mult).then_inc(y_ready, 1)

            dve.sem_inc(x_free, 2)
            dve.sem_inc(y_ready, 1)
            who_of(0, 0, 0)
            copy_hidden(0)
            who_of(1, 0, 1)
            weighted(0, 0)
            copy_hidden(1)
            with dve.Fori(0, (SLOT_TILES - 3) // 2) as r:
                t.dve.enter(r, 6)
                who_of(2 * r + 2, r + 1, 0)
                weighted(2 * r + 1, 1)
                copy_hidden(2 * r + 2)
                who_of(2 * r + 3, r + 1, 1)
                weighted(2 * r + 2, 0)
                copy_hidden(2 * r + 3)
                t.dve.leave((SLOT_TILES - 3) // 2)
            who_of(SLOT_TILES - 1, (SLOT_TILES - 1) // 2, 0)
            weighted(SLOT_TILES - 2, 1)
            copy_hidden(SLOT_TILES - 1)
            weighted(SLOT_TILES - 1, 0)

        @block.gpsimd
        def _(pool):
            def add(i, u):
                pool.wait_ge(y_ready, i + 2)
                settle(pool, t)
                nc.gpsimd.indirect_dma_start(t.sum1, bass.IndirectOffsetOnAxis(ap=who[u][:, 0:1].bitcast(U32), axis=0),
                                             y[u][:, :], None, bounds_check=T + 127, oob_is_err=True,
                                             compute_op=ALU.add).then_inc(y_added, 16)
                pool.wait_ge(y_added, 16 * (i + 1))

            with pool.Fori(0, (SLOT_TILES - 1) // 2) as r:
                add(2 * r, 0)
                add(2 * r + 1, 1)
            add(SLOT_TILES - 1, 0)


def finish(nc, io, t, new_sem, ctx):
    loaded, added, stored = new_sem("f_loaded"), new_sem("f_added"), new_sem("f_stored")
    with nc.Block() as block:
        @block.sync
        def _(sp):
            sp.dma_start(t.att[0:TP, :, :], t.sum1[0:T, :].rearrange("(g p) d -> p g d", p=TP)).then_inc(loaded, 16)
            for n in range(4):
                sp.wait_ge(added, n + 1)
                g0 = G // 4 * n
                sp.dma_start(io["out"][TP * g0:TP * (g0 + G // 4), :].rearrange("(g p) d -> p g d", p=TP), t.h[:, g0:g0 + G // 4, :]).then_inc(stored, 16)
            sp.wait_ge(stored, 64)

        @block.vector
        def _(dve):
            dve.wait_ge(loaded, 16)
            for n in range(4):
                h = t.h[:, G // 4 * n:G // 4 * (n + 1), :]
                nc.vector.tensor_tensor(h, h, t.att[0:TP, G // 4 * n:G // 4 * (n + 1), :], ALU.add).then_inc(added, 1)


class Names:
    pass


def build_program(nc, io, dumps=None, stop=99):
    with ExitStack() as ctx:
        def sb(name, shape, dt=F32, where=ctx):
            return where.enter_context(nc.sbuf_tensor(name, shape, dt))

        def new_sem(name):
            return ctx.enter_context(nc.semaphore(name))

        t, sem = Names(), Names()
        sem.consts, sem.filled, sem.prepared = new_sem("consts"), new_sem("filled"), new_sem("prepared")
        sem.cosines, sem.settled = new_sem("cosines"), new_sem("settled")
        t.sem = sem
        t.dve = Steps(nc.vector, new_sem("dve_steps"))
        t.pool = Steps(nc.gpsimd, new_sem("pool_steps"))

        t.h = sb("h", [TP, G, D])
        t.att = sb("att", [128, G, D])
        t.ident = sb("ident", [128, 128])
        t.identb = sb("identb", [128, 128], BF16)
        t.half = sb("half", [128, 4])
        t.iota = sb("iota", [128, E0])
        t.tile_expert = sb("tile_expert", [128, SLOT_TILES])
        t.tile_expert_u = sb("tile_expert_u", [128, SLOT_TILES], U32)
        t.empty = sb("empty", [128, ROW])
        t.disp0 = nc.dram_tensor("disp0", [E0 * CAP, ROW], F32).ap()
        t.disp1 = nc.dram_tensor("disp1", [SLOT_TILES * 128, ROW], F32).ap()
        t.rows1 = nc.dram_tensor("rows1", [T, ROW], F32).ap()
        t.sum0 = nc.dram_tensor("sum0", [T + 128, D], F32).ap()
        t.sum1 = nc.dram_tensor("sum1", [T + 128, D], F32).ap()
        t.split = nc.dram_tensor("split", [B, 2, NPART, D, S], BF16).ap()
        t.rowmax = nc.dram_tensor("rowmax", [B, 2, NPART, NHALF, S], BF16).ap()

        def phase(number, body):
            if stop < number:
                return
            with ExitStack() as inner:
                used = []

                def phase_sem(name):
                    used.append(inner.enter_context(nc.semaphore(name)))
                    return used[-1]

                body(phase_sem, inner)
                with nc.Block() as block:
                    @block.gpsimd
                    def _(pool):
                        for one in used:
                            pool.sem_clear(one)

        with ExitStack() as early:
            t.v = sb("v", [TP, G, NH, VW], F32, early)
            t.basis = sb("basis", [128, 2, 96], F32, early)
            t.basis_o = sb("basis_o", [128, 2, 32], F32, early)
            t.holo = sb("holo", [128, D], F32, early)
            t.wo = sb("wo", [128, 2, D], F32, early)
            t.bo = sb("bo", [TP, D], F32, early)
            t.above = sb("above", [TP, 3, TP], BF16, early)
            with ExitStack() as tok:
                t.xs = [sb(f"xs{u}", [F + 1, H, IMG], F32, tok) for u in range(2)]
                t.tok_kv = sb("tok_kv", [F + 1, 2 * F], F32, tok)
                t.tok_q = sb("tok_q", [F + 1, F], F32, tok)
                t.tok_res = sb("tok_res", [F + 1, H, F], F32, tok)
                t.ewT = sb("ewT", [128, 2, IMG], F32, tok)
                t.mask8 = sb("mask8", [128, 2, IMG // 4], U32, tok)
                t.maskf = sb("maskf", [128, 2, IMG], F32, tok)
                t.tok_out = sb("tok_out_w", [128, 2, D], F32, tok)
                t.gb = sb("gb", [TP, 2, D], F32, tok)
                t.phase = sb("phase", [128, D], F32, tok)
                t.amp = sb("amp", [128, D], F32, tok)
                t.trig = sb("trig", [128, 2, D], F32, tok)
                t.above32 = sb("above32", [TP, 3, TP], F32, tok)
                load_constants(nc, io, t, sem)
                phase(1, lambda ns, c: token_layer(nc, io, t, ns, tok))
            phase(2, lambda ns, c: holo_qkv(nc, io, t, ns, c))
            phase(3, lambda ns, c: attention(nc, t, "a0", False, ns, c))
            phase(4, lambda ns, c: attention_out(nc, t, "o0", 32, ns, c))
            phase(5, lambda ns, c: prefill(nc, t, ns))
            phase(6, lambda ns, c: route_and_share0(nc, io, t, ns, c))
            phase(7, lambda ns, c: experts0(nc, io, t, ns, c))
            phase(8, lambda ns, c: rotary_qkv(nc, io, t, ns, c))
            phase(9, lambda ns, c: attention(nc, t, "a1", True, ns, c))
            phase(10, lambda ns, c: attention_out(nc, t, "o1", 0, ns, c))
        with ExitStack() as late:
            t.w1s = sb("w1s", [128, E1, 2, HID], F32, late)
            phase(11, lambda ns, c: route_and_share1(nc, io, t, ns, c))
            phase(12, lambda ns, c: experts1(nc, io, t, ns, c))
            phase(13, lambda ns, c: finish(nc, io, t, ns, c))
        if dumps is not None:
            dumps(nc, t, new_sem)


def layouts(a):
    f = {}

    def T_(w):
        return w.T

    def chunked(w, p=128):
        return w.reshape(w.shape[0] // p, p, w.shape[1]).transpose(1, 0, 2)

    f["x"] = a["x"].transpose(0, 1, 3, 2)
    f["txt"] = a["txt"]
    f["tok_kv"] = np.concatenate([np.concatenate([a["L0_tok_Wk_w"].T, a["L0_tok_Wv_w"].T], 1),
                                  np.concatenate([a["L0_tok_Wk_b"], a["L0_tok_Wv_b"]])[None]], 0)
    f["tok_kv"] = f["tok_kv"][:, :]
    f["tok_q"] = np.concatenate([a["L0_tok_Wq_w"].T, a["L0_tok_Wq_b"][None]], 0)
    eye = np.eye(F, dtype=np.float32)
    f["tok_res"] = np.concatenate([np.broadcast_to(eye[:, None, :], (F, H, F)), a["L0_tok_out_b"].reshape(1, H, F)], 0)
    f["bias_t"] = chunked(a["L0_tok_w_bias"].T)
    f["mask_t"] = chunked(np.ascontiguousarray(a["L0_tok_local_mask"].T).view(np.uint32))
    f["tok_out"] = chunked(a["L0_tok_out_w"])
    f["ln_g"], f["ln_b"] = a["L0_tok_ln_g"], a["L0_tok_ln_b"]
    f["ident"] = np.eye(128, dtype=np.float32)
    f["basis"] = chunked(np.concatenate([a[f"L0_attn_basis_{c}"].T for c in "qkv"], 1))
    f["basis_o"] = chunked(a["L0_attn_basis_o"].T)
    f["phase"] = np.concatenate([a[f"L0_attn_phase_{c}"].T for c in "qkvo"], 0)
    f["amp"] = np.concatenate([a[f"L0_attn_amp_{c}"].T for c in "qkvo"], 0)
    f["iota"] = np.arange(E0, dtype=np.float32)
    f["before"] = np.triu(np.ones((TP, TP), np.float32), 1)
    f["gate0"], f["gate0_b"] = chunked(a["L0_ffn_gate_w"].T), a["L0_ffn_gate_b"]
    f["ws1"], f["ws3"], f["ws2"] = (chunked(a["L0_ffn_ws1"].T), chunked(a["L0_ffn_ws3"].T), chunked(a["L0_ffn_ws2"].T, IC))
    w13 = np.concatenate([a["L0_ffn_w1"].transpose(0, 2, 1), a["L0_ffn_w3"].transpose(0, 2, 1)], 2)
    f["w13"] = w13.reshape(E0, 2, 128, 2 * I0).transpose(0, 2, 1, 3)
    f["w2"] = a["L0_ffn_w2"].transpose(0, 2, 1).reshape(E0, 2, IC, D).transpose(0, 2, 1, 3)
    f["wo"], f["bo"] = chunked(a["L1_attn_wo"]), a["L1_attn_bo"]
    after = np.triu(np.full((TP, TP), -1e30, np.float32), 1)
    f["above"] = np.stack([after, after.T, np.full_like(after, -1e30)], 1)
    f["w_c"] = chunked(np.concatenate([a["L1_attn_wq"], a["L1_attn_wkv"]], 1))
    f["w_low"] = np.concatenate([a["L1_attn_wqc"], a["L1_attn_wkc"]], 0)
    swap = np.r_[64:128, 0:64]
    f["w_rope"] = np.stack([np.stack([chunked(w), chunked(w[:, swap])]) for w in (a["L1_attn_wqr"], a["L1_attn_wkr"])])
    bq, bk = a["L1_attn_bqr"], a["L1_attn_bkr"]
    f["biases"] = np.stack([np.concatenate([a["L1_attn_bq"], a["L1_attn_bkv"]]), a["L1_attn_bqc"], a["L1_attn_bkc"],
                            bq, bq[swap], bk, bk[swap]], 1)
    f["w_v"], f["b_v"] = a["L1_attn_wv"], a["L1_attn_bv"]
    inv = (1.0 / np.float32(10000.0) ** (np.arange(0, 128, 2, dtype=np.float32) / np.float32(128))).astype(np.float32)
    angle = np.arange(S, dtype=np.float32)[None] * np.concatenate([inv, inv])[:, None]
    sign = np.where(np.arange(128) < 64, -1.0, 1.0).astype(np.float32)[:, None]
    f["rope"] = np.stack([np.cos(angle), np.sin(angle) * sign], 1).astype(np.float32)
    f["gate1"] = chunked(a["L1_ffn_gate_w"].T)
    f["sw1"], f["sw2"] = chunked(a["L1_ffn_shared_w1"].T), chunked(a["L1_ffn_shared_w2"].T)
    f["ew1"] = a["L1_ffn_experts_w1"].transpose(0, 2, 1).reshape(E1, 2, 128, HID).transpose(0, 2, 1, 3)
    f["ew2"] = a["L1_ffn_experts_w2"].transpose(0, 2, 1).reshape(E1, HID // 128, 128, D).transpose(0, 2, 1, 3)
    return {k: np.ascontiguousarray(v) for k, v in f.items()}


def kernel(**inputs):
    import concourse.bacc as bacc
    from concourse.bass_utils import run_bass_kernel_spmd

    laid = layouts({name: np.asarray(value) for name, value in inputs.items()})
    nc = bacc.Bacc("TRN2", target_bir_lowering=False, num_devices=1)
    io, arrays = {}, {}
    for name, value in laid.items():
        arrays["in_" + name] = value
        io[name] = nc.dram_tensor("in_" + name, value.shape, mybir.dt.from_np(value.dtype), kind="ExternalInput").ap()
    io["out"] = nc.dram_tensor("out", (T, D), F32, kind="ExternalOutput").ap()
    build_program(nc, io)
    results = run_bass_kernel_spmd(nc, [arrays], core_ids=[0])
    return results.results[0]["out"].reshape(B, S, D)
```

```python
import math
from contextlib import ExitStack

import numpy as np

import concourse.bass as bass
from concourse import mybir

F32 = mybir.dt.float32
BF16 = mybir.dt.bfloat16
U32 = mybir.dt.uint32
U8 = mybir.dt.uint8
ALU = mybir.AluOpType
ACT = mybir.ActivationFunctionType
AX_X = mybir.AxisListType.X
ds = bass.ds

B = 8
IMG = 256
TXT = 77
S = IMG + TXT
D = 256
F = 64
H = 4
TP = 111
NT = S // TP
G = B * NT
T = B * S
NH = 16
HD = D // NH
VW = 2 * HD
NGROUP = 4
NHALF = 8
EPS = 1e-5
IMG_TILES = [(0, TP), (TP, TP), (2 * TP, IMG - 2 * TP)]

E0, I0, K0, CAP = 64, 176, 6, 128
IC = I0 // 2
SIC = 2 * I0 // IC
IDS, WTS, TID = D, D + 8, D + 15
ROW = D + 16

DEEP = 4

E1, HID = 8, 1024
SLOT_TILES = (2 * T + E1 * (128 - 1)) // 128

Q_SLOTS = [0, 0, 1, 1, 0, 2]
K_SLOTS = [0, 1, 0, 1, 2, 0]
NSLOT = len(Q_SLOTS)
KROWS = HD * NSLOT
NPART = 3
MAXROW = KROWS


def settle(eng, t):
    eng.sem_inc(t.sem.settled, 1)


class Steps:

    def __init__(self, eng, sem):
        self.eng, self.sem, self.total, self.base, self.k = eng, sem, 0, 0, 0

    def did(self, ins):
        self.k += 1
        ins.then_inc(self.sem, 1)

    def wait(self):
        self.eng.wait_ge(self.sem, self.base + self.k)

    def enter(self, i, per):
        self.outer, self.base, self.k, self.per = self.base + self.k, self.base + self.k + i * per, 0, per

    def leave(self, times):
        assert self.k == self.per, (self.k, self.per)
        self.base, self.k = self.outer + times * self.per, 0


def prefills(t):
    fills = []
    for d in (t.disp0, t.disp1):
        per = d.shape[0] // 128
        for a in range(0, per, 8):
            m = min(8, per - a)
            fills.append((d[128 * a:128 * (a + m), :].rearrange("(e p) r -> p e r", p=128),
                          t.empty[:, :].unsqueeze(1).to_broadcast([128, m, ROW])))
    for d in (*t.sum0, t.sum1):
        fills.append((d[0:T, :].rearrange("(g p) d -> p g d", p=TP), t.empty[0:TP, 0:D].unsqueeze(1).to_broadcast([TP, G, D])))
        fills.append((d[T:T + 128, :], t.empty[:, 0:D]))
    return fills


def load_constants(nc, io, t, sem):
    const_loads = [
        (t.tok_kv[:, :], io["tok_kv"]), (t.tok_q[:, :], io["tok_q"]), (t.tok_res[:, :, :], io["tok_res"]),
        (t.ewT[:, :, :], io["bias_t"]), (t.mask8[:, :, :], io["mask_t"]), (t.tok_out[:, :, :], io["tok_out"]),
        (t.ident[:, :], io["ident"]), (t.gb[0:TP, 0, :], io["ln_g"].partition_broadcast(TP)),
        (t.gb[0:TP, 1, :], io["ln_b"].partition_broadcast(TP)),
        (t.basis[:, :, :], io["basis"]), (t.basis_o[:, :, :], io["basis_o"]), (t.phase[:, :], io["phase"]), (t.amp[:, :], io["amp"]),
        (t.wo[:, :, :], io["wo"]), (t.bo[:, :], io["bo"].partition_broadcast(TP)), (t.above32[:, :, :], io["above"]),
        (t.iota[:, :], io["iota"].partition_broadcast(128)),
        (t.h[IMG - 2 * TP:TP, 2:G:NT, :], io["txt"].rearrange("b s d -> s b d")),
    ]
    with nc.Block() as block:
        @block.sync
        def _(sp):
            for dst, src in const_loads:
                sp.dma_start(dst, src).then_inc(sem.consts, 16)

        @block.gpsimd
        def _(pool):
            fills = [(t.empty[:, :], 0.0), (t.xs[0][F:F + 1, :, :], 1.0), (t.xs[1][F:F + 1, :, :], 1.0), (t.half[:, :], -0.5)]
            for n, (dst, value) in enumerate(fills):
                pool.wait_ge(sem.filled, n)
                nc.gpsimd.memset(dst, value).then_inc(sem.filled, 1)
            pool.wait_ge(sem.filled, len(fills))
            nc.gpsimd.iota(t.empty[:, TID:TID + 1].bitcast(U32), [[0, 1]], base=T, channel_multiplier=1).then_inc(sem.filled, 1)

        @block.vector
        def _(dve):
            dve.wait_ge(sem.consts, 16 * len(const_loads))
            t.dve.did(nc.vector.tensor_copy(t.maskf[:, :, :], t.mask8[:, :, :].bitcast(U8)))
            t.dve.wait()
            t.dve.did(nc.vector.tensor_tensor(t.ewT[:, :, :], t.ewT[:, :, :], t.maskf[:, :, :], ALU.mult))
            magic = 1.5 * 2.0 ** 23
            two_pi = 2.0 * math.pi
            c1 = 6.28125
            c2 = float(np.float32(np.round((two_pi - c1) * 2.0 ** 21) / 2.0 ** 21))
            c3 = float(np.float32(two_pi - c1 - c2))
            k, ph = t.trig[:, 0, :], t.trig[:, 1, :]
            t.dve.did(nc.vector.tensor_scalar(k, t.phase[:, :], 1.0 / two_pi, 0.25, ALU.mult, ALU.add))
            for op, s in ((ALU.add, magic), (ALU.subtract, magic)):
                t.dve.wait()
                t.dve.did(nc.vector.tensor_scalar(k, k, s, None, op))
            src = t.phase[:, :]
            for c in (c1, c2, c3):
                t.dve.wait()
                t.dve.did(nc.vector.scalar_tensor_tensor(out=ph, in0=k, scalar=-c, in1=src, op0=ALU.mult, op1=ALU.add))
                src = ph
            t.dve.wait()
            t.dve.did(nc.vector.tensor_scalar(ph, ph, math.pi / 2, math.pi, ALU.add, ALU.min))
            t.dve.wait()
            t.dve.did(nc.vector.tensor_scalar(ph, ph, -math.pi, None, ALU.max))
            t.dve.wait()
            t.dve.did(nc.vector.tensor_copy(t.above[:, :, :], t.above32[:, :, :]))
            nc.vector.tensor_copy(t.identb[:, :], t.ident[:, :]).then_inc(sem.prepared, 1)
            dve.wait_ge(sem.cosines, 1)
            nc.vector.tensor_tensor(t.holo[:, :], t.trig[:, 1, :], t.amp[:, :], ALU.mult).then_inc(sem.prepared, 1)

        @block.scalar
        def _(act):
            act.wait_ge(sem.prepared, 1)
            nc.scalar.activation(t.trig[:, 1, :], t.trig[:, 1, :], ACT.Sin).then_inc(sem.cosines, 1)
            nc.scalar.activation(t.ewT[:, :, :], t.ewT[:, :, :], ACT.Exp).then_inc(sem.cosines, 1)


def token_layer(nc, io, t, new_sem, ctx):
    xs_loaded, xs_free = [new_sem(f"tok_xs_loaded{u}") for u in range(2)], new_sem("tok_xs_free")
    kv_ready, ekv_act, ekv_dve = new_sem("tok_kv_ready"), new_sem("tok_ek_ready"), new_sem("tok_ekv_ready")
    q_ready, eq_ready = new_sem("tok_q_ready"), new_sem("tok_eq_ready")
    nd_ready, y_ready = new_sem("tok_nd_ready"), new_sem("tok_y_ready")
    yt_ready, yt_copied = new_sem("tok_yt_ready"), new_sem("tok_yt_copied")
    h_ready, stats_ready = new_sem("tok_h_ready"), new_sem("tok_stats_ready")
    rstd_ready, norm_ready, norm_free = new_sem("tok_rstd_ready"), new_sem("tok_norm_ready"), new_sem("tok_norm_free")

    def sb(name, shape, dt=F32):
        return ctx.enter_context(nc.sbuf_tensor(name, shape, dt))

    def ps(name, shape, dt=F32):
        return ctx.enter_context(nc.psum_tensor(name, shape, dt))

    ekv = [sb(f"tok_ekv{c}", [128, H, 2, F]) for c in range(2)]
    eq = sb("tok_eq", [TP, NT, D])
    y = [sb(f"tok_y{i}", [TP, D]) for i in range(2)]
    den = sb("tok_den", [TP, D])
    yT = [sb(f"tok_yT{i}", [128, 2, TP]) for i in range(2)]
    norm = [sb(f"tok_norm{i}", [TP, D]) for i in range(2)]
    stats = sb("tok_stats", [TP, 6])
    mv = [sb(f"tok_mv{i}", [TP, 2]) for i in range(2)]
    rstd = [sb(f"tok_rstd{i}", [TP, 1]) for i in range(2)]
    var = sb("tok_var", [TP, 1])
    p_kv = [ps(f"tok_pkv{c}", [128, H, 2, F]) for c in range(2)]
    p_q = ps("tok_pq", [TP, 2, 512])
    p_nd = [ps(f"tok_pnd{c}", [TP, H, 2, F]) for c in range(2)]
    p_yt = ps("tok_pyt", [128, 512])
    p_h = ps("tok_ph", [TP, 512])

    def q_of(j):
        n = IMG_TILES[j][1]
        return p_q[0:n, j // 2, (j % 2) * D:(j % 2) * D + D]

    with nc.Block() as block:
        @block.sync
        def _(sp):
            def load(i):
                for u in range(2):
                    sp.wait_ge(xs_free, 2 * i + u + 1)
                    sp.dma_start(t.xs[u][0:F, :, :], io["x"][ds(2 * i + u, 1)].rearrange("a c h l -> (a c) h l")).then_inc(xs_loaded[u], 16)

            fills = prefills(t)
            per = -(-len(fills) // (B // 2 - 1))
            sp.wait_ge(t.sem.filled, 5)
            for i in range(B // 2):
                load(i)
                for dst, src in fills[per * i:per * (i + 1)]:
                    sp.dma_start(dst, src).then_inc(t.sem.prefilled, 16)

        @block.tensor
        def _(pe):
            pe.sem_inc(xs_free, 2)
            pe.wait_ge(t.sem.cosines, 2)
            def project_inputs(i, u):
                n = 2 * i + u
                xs = t.xs[u]
                pe.wait_ge(xs_loaded[u], 16 * i + 16)
                for c in range(2):
                    pe.wait_ge(ekv_dve, 2 * n)
                    for h in range(H):
                        mm = nc.tensor.matmul(p_kv[c][:, h, :, :], xs[:, h, 128 * c:128 * c + 128], t.tok_kv[:, :],
                                              start=True, stop=True)
                    mm.then_inc(kv_ready, 1)
                pe.wait_ge(eq_ready, NT * n)
                for j, (l0, rows) in enumerate(IMG_TILES):
                    for h in range(H):
                        mm = nc.tensor.matmul(q_of(j)[:, F * h:F * h + F], xs[:, h, l0:l0 + rows], t.tok_q[:, :],
                                              start=True, stop=True)
                    if j:
                        mm.then_inc(q_ready, 1)

            def body(i, u, more):
                n = 2 * i + u
                xs = t.xs[u]

                def mix(j):
                    l0, rows = IMG_TILES[j]
                    if j == 0:
                        pe.wait_ge(ekv_dve, 2 * n + 2)
                    pe.wait_ge(y_ready, NT * n + max(j - 1, 0))
                    for c in range(2):
                        mm = nc.tensor.matmul(p_nd[j % 2][0:rows, :, :, :], t.ewT[:, c, l0:l0 + rows], ekv[c][:, :, :, :],
                                              start=(c == 0), stop=(c == 1))
                    mm.then_inc(nd_ready, 1)

                def project(j):
                    l0, rows = IMG_TILES[j]
                    pe.wait_ge(y_ready, NT * n + j + 1)
                    pe.wait_ge(yt_copied, NT * n + j)
                    settle(pe, t)
                    for c in range(2):
                        mm = nc.tensor.transpose(p_yt[:, 128 * c:128 * c + rows], y[j % 2][0:rows, 128 * c:128 * c + 128],
                                                 t.ident[0:rows, 0:rows])
                    mm.then_inc(yt_ready, 1)
                    pe.wait_ge(norm_ready, NT * n + j)
                    for h in range(H):
                        nc.tensor.matmul(p_h[0:rows, F * h:F * h + F], xs[:, h, l0:l0 + rows], t.tok_res[:, h, :],
                                         start=(h == 0), stop=False, skip_group_check=True)
                    pe.wait_ge(yt_copied, NT * n + j + 1)
                    for c in range(2):
                        mm = nc.tensor.matmul(p_h[0:rows, 0:D], yT[j % 2][:, c, 0:rows], t.tok_out[:, c, :],
                                              start=False, stop=(c == 1), skip_group_check=True)
                    mm.then_inc(h_ready, 1)
                    return mm

                mix(0)
                mix(1)
                project(0)
                mix(2)
                if more:
                    project_inputs(i + u, 1 - u)
                project(1)
                project(2)
                pe.wait_ge(h_ready, NT * n + NT)
                pe.sem_inc(xs_free, 1)

            project_inputs(0, 0)
            with pe.Fori(0, B // 2 - 1) as i:
                for u in range(2):
                    body(i, u, True)
            body(B // 2 - 1, 0, True)
            body(B // 2 - 1, 1, False)

        @block.scalar
        def _(act):
            def exps_of_keys(n):
                for c in range(2):
                    act.wait_ge(kv_ready, 2 * n + c + 1)
                    act.wait_ge(nd_ready, NT * n)
                    nc.scalar.activation(ekv[c][:, :, 0, :], p_kv[c][:, :, 0, :], ACT.Exp).then_inc(ekv_act, 1)

            def exps_of_queries(n):
                for j, (l0, rows) in enumerate(IMG_TILES):
                    act.wait_ge(q_ready, 2 * n + 1 + j // 2)
                    act.wait_ge(y_ready, NT * n)
                    nc.scalar.activation(eq[0:rows, j, :], q_of(j), ACT.Exp, scale=-1.0).then_inc(eq_ready, 1)

            def body(n, more):
                for j, (l0, rows) in enumerate(IMG_TILES):
                    act.wait_ge(yt_ready, NT * n + j + 1)
                    act.wait_ge(h_ready, NT * n + max(j - 1, 0))
                    nc.scalar.activation(yT[j % 2][:, :, 0:rows],
                                         p_yt[:, 0:256].rearrange("p (c r) -> p c r", c=2)[:, :, 0:rows],
                                         ACT.Copy).then_inc(yt_copied, 1)
                    if j == 0 and more:
                        exps_of_keys(n + 1)
                    if j == 1 and more:
                        exps_of_queries(n + 1)

            exps_of_keys(0)
            exps_of_queries(0)
            with act.Fori(0, B - 1) as n:
                body(n, True)
            body(B - 1, False)

        @block.vector
        def _(dve):
            def times_v(n):
                for c in range(2):
                    dve.wait_ge(ekv_act, 2 * n + c + 1)
                    nc.vector.tensor_tensor(ekv[c][:, :, 1, :], ekv[c][:, :, 0, :], p_kv[c][:, :, 1, :],
                                            ALU.mult).then_inc(ekv_dve, 1)

            def body(n, more):
                def gate(j):
                    rows = IMG_TILES[j][1]
                    split = "p (h f) -> p h f"
                    dve.wait_ge(eq_ready, NT * n + j + 1)
                    dve.wait_ge(nd_ready, NT * n + j + 1)
                    dve.wait_ge(y_ready, NT * n + j)
                    t.dve.did(nc.vector.scalar_tensor_tensor(
                        out=den[0:rows, :].rearrange(split, h=H), in0=eq[0:rows, j, :].rearrange(split, h=H), scalar=1.0,
                        in1=p_nd[j % 2][0:rows, :, 0, :], op0=ALU.add, op1=ALU.mult))
                    t.dve.wait()
                    t.dve.did(nc.vector.reciprocal(den[0:rows, :], den[0:rows, :]))
                    t.dve.wait()
                    dve.wait_ge(yt_ready, NT * n + max(j - 1, 0))
                    nc.vector.tensor_tensor(y[j % 2][0:rows, :].rearrange(split, h=H), den[0:rows, :].rearrange(split, h=H),
                                            p_nd[j % 2][0:rows, :, 1, :], ALU.mult).then_inc(y_ready, 1)

                def normalize(j):
                    rows = IMG_TILES[j][1]
                    dve.wait_ge(h_ready, NT * n + j + 1)
                    dve.wait_ge(stats_ready, NT * n + j)
                    settle(dve, t)
                    t.dve.did(nc.vector.bn_stats(stats[0:rows, :], p_h[0:rows, 0:D]))
                    t.dve.wait()
                    dve.wait_ge(norm_ready, NT * n + max(j - 1, 0))
                    dve.wait_ge(rstd_ready, NT * n + max(j - 1, 0))
                    settle(dve, t)
                    nc.vector.bn_aggr(mv[j % 2][0:rows, :], stats[0:rows, :]).then_inc(stats_ready, 1)
                    dve.wait_ge(stats_ready, NT * n + j + 1)
                    dve.wait_ge(rstd_ready, NT * n + j + 1)
                    dve.wait_ge(norm_free, NT * n + max(j - 1, 0))
                    nc.vector.tensor_scalar(norm[j % 2][0:rows, :], p_h[0:rows, 0:D], mv[j % 2][0:rows, 0:1],
                                                      rstd[j % 2][0:rows, :], ALU.subtract, ALU.mult).then_inc(norm_ready, 1)

                gate(0)
                gate(1)
                normalize(0)
                gate(2)
                normalize(1)
                if more:
                    times_v(n + 1)
                normalize(2)

            times_v(0)
            with dve.Fori(0, B - 1) as n:
                t.dve.enter(n, 3 * NT)
                body(n, True)
                t.dve.leave(B - 1)
            body(B - 1, False)

        @block.gpsimd
        def _(pool):
            pool.wait_ge(t.sem.filled, 5)
            with pool.Fori(0, B) as n:
                t.pool.enter(n, 2 * NT)
                for j, (l0, rows) in enumerate(IMG_TILES):
                    pool.wait_ge(stats_ready, NT * n + j + 1)
                    pool.wait_ge(rstd_ready, NT * n + j)
                    pool.wait_ge(norm_ready, NT * n + max(j - 1, 0))
                    settle(pool, t)
                    t.pool.did(nc.gpsimd.tensor_scalar(var[0:rows, :], mv[j % 2][0:rows, 1:2], EPS, None, ALU.add))
                    t.pool.wait()
                    nc.gpsimd.tensor_tensor(rstd[j % 2][0:rows, :], var[0:rows, :], t.half[0:rows, 0:1], ALU.pow).then_inc(rstd_ready, 1)
                    pool.wait_ge(norm_ready, NT * n + j + 1)
                    t.pool.did(nc.gpsimd.tensor_tensor(norm[j % 2][0:rows, :], norm[j % 2][0:rows, :], t.gb[0:rows, 0, :], ALU.mult))
                    t.pool.wait()
                    nc.gpsimd.tensor_tensor(t.h[0:rows, ds(NT * n + j, 1), :].rearrange("p a d -> p (a d)"), norm[j % 2][0:rows, :], t.gb[0:rows, 1, :],
                                            ALU.add).then_inc(norm_free, 1)
                t.pool.leave(B)


class NormalizedTransposed:

    def __init__(self, nc, t, name, new_sem, sb, ps):
        self.nc, self.t = nc, t
        self.stats_ready, self.rstd_ready = new_sem(name + "_stats_ready"), new_sem(name + "_rstd_ready")
        self.xn_ready, self.xt_turned = new_sem(name + "_xn_ready"), new_sem(name + "_xt_turned")
        self.xt_ready, self.xt_used = new_sem(name + "_xt_ready"), new_sem(name + "_xt_used")
        self.stats = sb(name + "_stats", [TP, NT, 6])
        self.mv = sb(name + "_mv", [TP, NT, 2])
        self.var = sb(name + "_var", [TP, NT])
        self.rstd = sb(name + "_rstd", [TP, NT])
        self.xn = sb(name + "_xn", [TP, NT, D])
        self.xT = sb(name + "_xT", [128, 2, S])
        self.p_xt = ps(name + "_pxt", [128, 2, 512])

    STEPS = NT

    def row_stats(self, dve, n):
        dve.wait_ge(self.xn_ready, n)
        settle(dve, self.t)
        for j in range(NT):
            self.t.dve.did(self.nc.vector.bn_stats(self.stats[:, j, :], self.t.h[:, ds(NT * n + j, 1), :].rearrange("p a d -> p (a d)")))
        self.t.dve.wait()
        settle(dve, self.t)
        for j in range(NT):
            ins = self.nc.vector.bn_aggr(self.mv[:, j, :], self.stats[:, j, :])
        ins.then_inc(self.stats_ready, 1)

    POOL_STEPS = 1

    def invert(self, pool, n):
        pool.wait_ge(self.stats_ready, n + 1)
        settle(pool, self.t)
        self.t.pool.did(self.nc.gpsimd.tensor_scalar(self.var[:, :], self.mv[:, :, 1], EPS, None, ALU.add))
        self.t.pool.wait()
        self.nc.gpsimd.tensor_tensor(self.rstd[:, :], self.var[:, :], self.t.half[0:TP, 0:NT], ALU.pow).then_inc(self.rstd_ready, 1)

    def normalize(self, dve, n):
        dve.wait_ge(self.stats_ready, n + 1)
        dve.wait_ge(self.rstd_ready, n + 1)
        dve.wait_ge(self.xt_turned, n)
        for j in range(NT):
            ins = self.nc.vector.tensor_scalar(self.xn[:, j, :], self.t.h[:, ds(NT * n + j, 1), :].rearrange("p a d -> p (a d)"),
                                               self.mv[:, j, 0:1], self.rstd[:, j:j + 1], ALU.subtract, ALU.mult)
        ins.then_inc(self.xn_ready, 1)

    def turn(self, pe, n):
        pe.wait_ge(self.xn_ready, n + 1)
        pe.wait_ge(self.xt_ready, n)
        for c in range(2):
            for j in range(NT):
                mm = self.nc.tensor.transpose(self.p_xt[:, c, TP * j:TP * j + TP], self.xn[:, j, 128 * c:128 * c + 128],
                                              self.t.ident[0:TP, 0:TP])
        mm.then_inc(self.xt_turned, 1)

    def copy(self, act, n):
        act.wait_ge(self.xt_turned, n + 1)
        act.wait_ge(self.xt_used, n)
        self.nc.scalar.activation(self.xT[:, :, :], self.p_xt[:, :, 0:S], ACT.Copy).then_inc(self.xt_ready, 1)


class Splitter:

    def __init__(self, nc, t, name, which, scale, new_sem, sb):
        self.nc, self.t, self.which, self.scale = nc, t, which, scale
        self.part0, self.rest_ready = new_sem(name + "_part0"), new_sem(name + "_rest")
        self.part1, self.part2, self.stored = new_sem(name + "_part1"), new_sem(name + "_part2"), new_sem(name + "_stored")
        self.rest = sb(name + "_rest", [128, 2, S])
        self.parts = sb(name + "_parts", [128, NPART, 2, S], BF16)

    def first(self, act, n, x):
        act.wait_ge(self.stored, 16 * n)
        self.nc.scalar.activation(self.parts[:, 0, :, :], x, ACT.Copy, scale=self.scale).then_inc(self.part0, 1)

    def residue(self, dve, n, x):
        dve.wait_ge(self.part0, n + 1)
        dve.wait_ge(self.part2, n)
        self.nc.vector.scalar_tensor_tensor(out=self.rest[:, :, :], in0=x, scalar=self.scale, in1=self.parts[:, 0, :, :],
                                            op0=ALU.mult, op1=ALU.subtract).then_inc(self.rest_ready, 1)

    def second(self, pool, n):
        pool.wait_ge(self.rest_ready, n + 1)
        pool.wait_ge(self.stored, 16 * n)
        settle(pool, self.t)
        self.nc.gpsimd.tensor_copy(self.parts[:, 1, :, :], self.rest[:, :, :]).then_inc(self.part1, 1)

    def third(self, dve, n):
        dve.wait_ge(self.rest_ready, n + 1)
        dve.wait_ge(self.part1, n + 1)
        self.nc.vector.tensor_tensor(self.parts[:, 2, :, :], self.rest[:, :, :], self.parts[:, 1, :, :],
                                     ALU.subtract).then_inc(self.part2, 1)

    def store(self, sp, n):
        sp.wait_ge(self.part2, n + 1)
        sp.dma_start(self.t.split[ds(n, 1), self.which].rearrange("b a (c p) n -> p (b a) c n", p=128),
                     self.parts[:, :, :, :]).then_inc(self.stored, 16)


def holo_qkv(nc, io, t, new_sem, ctx):
    def sb(name, shape, dt=F32):
        return ctx.enter_context(nc.sbuf_tensor(name, shape, dt))

    def ps(name, shape, dt=F32):
        return ctx.enter_context(nc.psum_tensor(name, shape, dt))

    xf = NormalizedTransposed(nc, t, "hq", new_sem, sb, ps)
    cut = [Splitter(nc, t, "hq_q", 0, float(HD) ** -0.5, new_sem, sb), Splitter(nc, t, "hq_k", 1, 1.0, new_sem, sb)]
    r_made, r_ready = new_sem("hq_r_made"), new_sem("hq_r_ready")
    q_made, k_made, v_made, v_ready = new_sem("hq_q_made"), new_sem("hq_k_made"), new_sem("hq_v_made"), new_sem("hq_v_ready")
    rT = sb("hq_rT", [96, S])
    p_r = ps("hq_pr", [96, 512])
    p_qk = [ps("hq_pq", [128, 2, 512]), ps("hq_pk", [128, 2, 512])]
    p_v = ps("hq_pv", [TP, 2, D])
    made = [q_made, k_made]

    with nc.Block() as block:
        @block.sync
        def _(sp):
            with sp.Fori(0, B) as n:
                for c in cut:
                    c.store(sp, n)
            for c in cut:
                sp.wait_ge(c.stored, 16 * B)

        @block.tensor
        def _(pe):
            def body(n, more):
                pe.wait_ge(xf.xt_ready, n + 1)
                pe.wait_ge(r_ready, n)
                for c in range(2):
                    mm = nc.tensor.matmul(p_r[:, 0:S], t.basis[:, c, :], xf.xT[:, c, :], start=(c == 0), stop=(c == 1))
                mm.then_inc(r_made, 1)
                pe.wait_ge(r_made, n + 1)
                pe.sem_inc(xf.xt_used, 1)
                pe.wait_ge(r_ready, n + 1)
                for w in range(2):
                    pe.wait_ge(cut[w].rest_ready, n)
                    for c in range(2):
                        mm = nc.tensor.matmul(p_qk[w][:, c, 0:S], t.holo[32 * w:32 * w + 32, 128 * c:128 * c + 128],
                                              rT[32 * w:32 * w + 32, :], start=True, stop=True)
                    mm.then_inc(made[w], 1)
                if more:
                    xf.turn(pe, n + 1)
                for half, tiles in enumerate(([0, 1], [2])):
                    pe.wait_ge(v_ready, 2 * n + half)
                    for j in tiles:
                        mm = nc.tensor.matmul(p_v[:, j % 2, :], rT[64:96, TP * j:TP * j + TP], t.holo[64:96, :],
                                              start=True, stop=True)
                    mm.then_inc(v_made, 1)

            xf.turn(pe, 0)
            with pe.Fori(0, B - 1) as n:
                body(n, True)
            body(B - 1, False)

        @block.scalar
        def _(act):
            def body(n, more):
                act.wait_ge(r_made, n + 1)
                act.wait_ge(v_made, 2 * n)
                nc.scalar.activation(rT[:, :], p_r[:, 0:S], ACT.Copy).then_inc(r_ready, 1)
                for w in range(2):
                    act.wait_ge(made[w], n + 1)
                    cut[w].first(act, n, p_qk[w][:, :, 0:S])
                if more:
                    xf.copy(act, n + 1)
                for half, tiles in enumerate(([0, 1], [2])):
                    act.wait_ge(v_made, 2 * n + half + 1)
                    m = len(tiles)
                    nc.scalar.activation(t.v[:, ds(NT * n + tiles[0], m), :, 0:HD],
                                         p_v[:, 0:m, :].rearrange("p j (h d) -> p j h d", h=NH), ACT.Copy).then_inc(v_ready, 1)

            xf.copy(act, 0)
            with act.Fori(0, B - 1) as n:
                body(n, True)
            body(B - 1, False)

        @block.vector
        def _(dve):
            def body(n, more):
                if more:
                    xf.row_stats(dve, n + 1)
                    xf.normalize(dve, n + 1)
                for w in range(2):
                    cut[w].residue(dve, n, p_qk[w][:, :, 0:S])
                for w in range(2):
                    cut[w].third(dve, n)

            xf.row_stats(dve, 0)
            xf.normalize(dve, 0)
            with dve.Fori(0, B - 1) as n:
                t.dve.enter(n, xf.STEPS)
                body(n, True)
                t.dve.leave(B - 1)
            body(B - 1, False)

        @block.gpsimd
        def _(pool):
            def body(n, more):
                if more:
                    xf.invert(pool, n + 1)
                for w in range(2):
                    cut[w].second(pool, n)

            xf.invert(pool, 0)
            with pool.Fori(0, B - 1) as n:
                t.pool.enter(n, xf.POOL_STEPS)
                body(n, True)
                t.pool.leave(B - 1)
            body(B - 1, False)


def attention(nc, t, name, causal, new_sem, ctx):
    def sb(name_, shape, dt=F32):
        return ctx.enter_context(nc.sbuf_tensor(name + name_, shape, dt))

    def ps(name_, shape, dt=F32):
        return ctx.enter_context(nc.psum_tensor(name + name_, shape, dt))

    def sm(name_):
        return new_sem(name + name_)

    stack_loaded, stack_free, ones_set = sm("_stack_loaded"), sm("_stack_free"), sm("_ones_set")
    s_made, s_max = sm("_s_made"), sm("_s_max")
    max_cut, max_stored, max_loaded = sm("_max_cut"), sm("_max_stored"), sm("_max_loaded")
    t_made, exp_made, probs_free = sm("_t_made"), sm("_exp_made"), sm("_probs_free")
    v_copied, o_copied, o_turned, o_free = sm("_v_copied"), sm("_o_copied"), sm("_o_turned"), sm("_o_free")

    ring = 3
    qst = sb("_qst", [KROWS + NPART, ring, NH, S], BF16)
    kst = sb("_kst", [KROWS + NPART, ring, NH, S], BF16)
    probs = [sb(f"_probs{u}", [TP, NT, S]) for u in range(2)]
    nmax = sb("_nmax", [TP, NT, NH])
    mrest = sb("_mrest", [TP, NT, NHALF])
    mparts = sb("_mparts", [128, NT, 32], BF16)
    mturned = sb("_mturned", [128, NT, 32], BF16)
    rsum = sb("_rsum", [TP, NT, NGROUP])
    values = [sb(f"_values{u}", [TP, NT, NHALF, VW]) for u in range(2)]
    oT = sb("_oT", [128, S])
    p_s = ps("_ps", [TP, NT, 512])
    p_t = ps("_pt", [TP, NT, 512])
    p_o = ps("_po", [128, 512])
    p_r = ps("_pr", [TP, NT, NGROUP, VW])
    n_stack = 2 * NSLOT
    halves, groups = NH // NHALF, NH // NGROUP
    chunks = [(32 * k, min(32, TP - 32 * k)) for k in range(4)]

    with nc.Block() as block:
        @block.sync
        def _(sp):
            def load_stacks(n):
                sp.wait_ge(stack_free, n + 1)
                sp.wait_ge(stack_loaded, 16 * n_stack * n)
                for slots, which, dst in ((Q_SLOTS, 0, qst), (K_SLOTS, 1, kst)):
                    for r, part in enumerate(slots):
                        sp.dma_start(dst[HD * r:HD * r + HD, ds(n % ring, 1), :, :].rearrange("d a h n -> d (a h) n"),
                                     t.split[ds(n, 1), which, part].rearrange("b (h d) n -> d (b h) n", d=HD)).then_inc(stack_loaded, 16)

            def rows_of_maxima(n, half):
                m = halves * n + half
                sp.wait_ge(max_cut, m + 1)
                settle(sp, t)
                for k, (r0, rows) in enumerate(chunks):
                    sp.dma_start(t.rowmax[ds(n, 1), half].rearrange("b a h (j p) -> (b a h) j p", p=TP)[:, :, r0:r0 + rows],
                                 mturned[32 * k:32 * k + NPART * NHALF, :, 0:rows]).then_inc(max_stored, 16)
                sp.wait_ge(max_stored, 16 * len(chunks) * (m + 1))
                settle(sp, t)
                sp.wait_ge(max_loaded, 16 * m)
                sp.dma_start(qst[MAXROW:MAXROW + NPART, ds(n % ring, 1), NHALF * half:NHALF * half + NHALF, :].rearrange("a b h n -> a (b h) n"),
                             t.rowmax[ds(n, 1), half].rearrange("b a h n -> a (b h) n")).then_inc(max_loaded, 16)

            load_stacks(0)
            with sp.Fori(0, B - 1) as n:
                load_stacks(n + 1)
                for half in range(halves):
                    rows_of_maxima(n, half)
            for half in range(halves):
                rows_of_maxima(B - 1, half)

        @block.gpsimd
        def _(pool):
            nc.gpsimd.memset(kst[MAXROW:MAXROW + NPART, :, :, :], 1.0).then_inc(ones_set, 1)
            pool.wait_ge(ones_set, 1)
            nc.gpsimd.memset(mparts[:, :, :], 0.0).then_inc(ones_set, 1)
            for half in range(halves):
                pool.wait_ge(ones_set, 2 + half)
                nc.gpsimd.memset(values[half][:, :, :, HD:VW], 1.0).then_inc(ones_set, 1)

            def copy_values(n, half):
                settle(pool, t)
                nc.gpsimd.tensor_copy(values[half][:, :, :, 0:HD],
                                      t.v[:, ds(NT * n, NT), NHALF * half:NHALF * half + NHALF, :]).then_inc(v_copied, 1)

            for half in range(halves):
                copy_values(0, half)
            with pool.Fori(1, B) as n:
                for half in range(halves):
                    pool.wait_ge(probs_free, 2 + NH * n - NH + NHALF * (half + 1))
                    copy_values(n, half)

        @block.tensor
        def _(pe):
            def scores(n, h):
                m = NH * n + h
                if h == 0:
                    pe.wait_ge(stack_loaded, 16 * n_stack * (n + 1))
                for j in range(NT):
                    pe.wait_ge(s_max, NT * m + j + 1)
                    w = TP * (j + 1) if causal else S
                    mm = nc.tensor.matmul(p_s[:, j, 0:w], qst[0:KROWS, ds(n % ring, 1), h, TP * j:TP * j + TP].rearrange("p a n -> p (a n)"),
                                          kst[0:KROWS, ds(n % ring, 1), h, 0:w].rearrange("p a n -> p (a n)"),
                                          start=True, stop=not causal, skip_group_check=causal)
                    if causal:
                        mm = nc.tensor.matmul(p_s[:, j, TP * j:w], t.identb[0:TP, 0:TP], t.above[:, 0, :],
                                              start=False, stop=True, skip_group_check=True)
                    mm.then_inc(s_made, 1)

            def shifted_scores(n, h):
                m = NH * n + h
                if h % NHALF == 0:
                    pe.wait_ge(max_loaded, 16 * (halves * n + h // NHALF + 1))
                for i in range(NT):
                    pe.wait_ge(exp_made, NT * m + i + 1)
                    q0 = min(i, 1) * TP if causal else 0
                    mm = nc.tensor.matmul(p_t[:, i, q0:S], kst[:, ds(n % ring, 1), h, TP * i:TP * i + TP].rearrange("p a n -> p (a n)"),
                                          qst[:, ds(n % ring, 1), h, q0:S].rearrange("p a n -> p (a n)"),
                                          start=True, stop=not causal, skip_group_check=causal)
                    if causal:
                        if q0 < TP * i:
                            nc.tensor.matmul(p_t[:, i, q0:TP * i], t.identb[0:TP, 0:TP], t.above[:, 2, :],
                                             start=False, stop=False, skip_group_check=True)
                        mm = nc.tensor.matmul(p_t[:, i, TP * i:TP * i + TP], t.identb[0:TP, 0:TP], t.above[:, 1, :],
                                              start=False, stop=True, skip_group_check=True)
                    mm.then_inc(t_made, 1)

            def times_values(n, h):
                m = NH * n + h
                if h % NHALF == 0:
                    pe.wait_ge(v_copied, halves * n + h // NHALF + 1)
                if h % NGROUP == 0:
                    pe.wait_ge(o_copied, groups * n + h // NGROUP + 1)
                r0 = VW * (h % NGROUP)
                for i in range(NT):
                    pe.wait_ge(exp_made, NT * (m + 1) + i + 1)
                    q0 = TP * i if causal else 0
                    mm = nc.tensor.matmul(p_o[r0:r0 + VW, q0:S], values[h // NHALF][:, i, h % NHALF, :], probs[h % 2][:, i, q0:S],
                                          start=(i == 0), stop=(i == NT - 1), skip_group_check=True)
                mm.then_inc(probs_free, 1)

            def turn_outputs(n, group):
                m = groups * n + group
                pe.wait_ge(o_copied, m + 2)
                pe.wait_ge(o_free, m + 1)
                settle(pe, t)
                for j in range(NT):
                    mm = nc.tensor.transpose(p_r[:, j, :, :], oT[:, TP * j:TP * j + TP], t.ident[:, :])
                mm.then_inc(o_turned, 1)

            def batch(n, first, second):
                for h in range(NH):
                    if first:
                        scores(n, h)
                    if second:
                        shifted_scores(n - 1, h)
                        if h:
                            times_values(n - 1, h - 1)
                        if h > NGROUP and h % NGROUP == 1:
                            turn_outputs(n - 1, h // NGROUP - 1)
                if second:
                    times_values(n - 1, NH - 1)
                    turn_outputs(n - 1, groups - 1)
                    pe.wait_ge(t_made, NT * NH * n)
                    pe.sem_inc(stack_free, 1)

            pe.sem_inc(stack_free, ring)
            pe.sem_inc(probs_free, 2)
            pe.sem_inc(o_turned, 1)
            pe.wait_ge(ones_set, 4)
            batch(0, True, False)
            with pe.Fori(1, B) as n:
                batch(n, True, True)
            batch(B, False, True)

        @block.scalar
        def _(act):
            def copy_outputs(n, group):
                act.wait_ge(probs_free, 2 + NH * n + NGROUP * (group + 1))
                act.wait_ge(o_turned, groups * n + group + 1)
                nc.scalar.activation(oT[:, :], p_o[:, 0:S], ACT.Copy).then_inc(o_copied, 1)

            act.sem_inc(o_copied, 1)
            act.sem_inc(exp_made, NT)
            with act.Fori(0, B) as n:
                for h in range(NH):
                    m = NH * n + h
                    act.wait_ge(probs_free, m + 1)
                    for i in range(NT):
                        q0 = min(i, 1) * TP if causal else 0
                        act.wait_ge(t_made, NT * m + i + 1)
                        nc.scalar.activation(probs[h % 2][:, i, q0:S], p_t[:, i, q0:S], ACT.Exp).then_inc(exp_made, 1)
                    if h and h % NGROUP == 0:
                        copy_outputs(n, h // NGROUP - 1)
                copy_outputs(n, groups - 1)

        @block.vector
        def _(dve):
            def maxima(n, h):
                if h == 0:
                    dve.wait_ge(max_cut, halves * n)
                for j in range(NT):
                    w = TP * (j + 1) if causal else S
                    dve.wait_ge(s_made, NT * (NH * n + h) + j + 1)
                    nc.vector.tensor_reduce(nmax[:, j, h:h + 1], p_s[:, j, 0:w], AX_X, ALU.max, negate=True).then_inc(s_max, 1)

            def cut_maxima(n, half):
                m = halves * n + half
                dve.wait_ge(s_max, NT * (1 + NH * n + NHALF * half + NHALF))
                x = nmax[:, :, NHALF * half:NHALF * half + NHALF]
                part = [mparts[0:TP, :, NHALF * a:NHALF * a + NHALF] for a in range(NPART)]
                dve.wait_ge(max_stored, 16 * len(chunks) * m)
                t.dve.did(nc.vector.tensor_copy(part[0], x))
                t.dve.wait()
                t.dve.did(nc.vector.tensor_tensor(mrest[:, :, :], x, part[0], ALU.subtract))
                t.dve.wait()
                t.dve.did(nc.vector.tensor_copy(part[1], mrest[:, :, :]))
                t.dve.wait()
                t.dve.did(nc.vector.tensor_tensor(part[2], mrest[:, :, :], part[1], ALU.subtract))
                t.dve.wait()
                nc.vector.transpose(mturned[:, :, :], mparts[:, :, :]).then_inc(max_cut, 1)
                dve.wait_ge(max_cut, m + 1)

            def normalize(n, group):
                dve.wait_ge(o_turned, groups * n + group + 2)
                dve.wait_ge(o_free, groups * n + group + 1)
                t.dve.did(nc.vector.reciprocal(rsum[:, :, :], p_r[:, :, :, HD]))
                t.dve.wait()
                nc.vector.tensor_tensor(t.att[0:TP, ds(NT * n, NT), NGROUP * HD * group:NGROUP * HD * (group + 1)].rearrange("p j (h d) -> p j h d", h=NGROUP),
                                        p_r[:, :, :, 0:HD], rsum[:, :, :].unsqueeze(3).to_broadcast([TP, NT, NGROUP, HD]),
                                        ALU.mult).then_inc(o_free, 1)

            def batch(n, first, second):
                for h in range(NH):
                    if first:
                        maxima(n, h)
                        if h % NHALF == NHALF - 1:
                            cut_maxima(n, h // NHALF)
                    if second and h > NGROUP and h % NGROUP == 2:
                        normalize(n - 1, h // NGROUP - 1)
                if second:
                    normalize(n - 1, groups - 1)

            dve.sem_inc(o_free, 1)
            dve.sem_inc(s_max, NT)
            dve.wait_ge(ones_set, 4)
            batch(0, True, False)
            with dve.Fori(0, B - 1) as i:
                t.dve.enter(i, 4 * halves + groups)
                batch(i + 1, True, True)
                t.dve.leave(B - 1)
            batch(B, False, True)


def attention_out(nc, t, name, rank, new_sem, ctx):
    def sb(name_, shape, dt=F32):
        return ctx.enter_context(nc.sbuf_tensor(name + name_, shape, dt))

    def ps(name_, shape, dt=F32):
        return ctx.enter_context(nc.psum_tensor(name + name_, shape, dt))

    def sm(name_):
        return new_sem(name + name_)

    a_copied, a_turned, a_ready, a_used = sm("_a_copied"), sm("_a_turned"), sm("_a_ready"), sm("_a_used")
    r_made, r_ready, y_made, y_added, biased = sm("_r_made"), sm("_r_ready"), sm("_y_made"), sm("_y_added"), sm("_biased")
    a = sb("_a", [TP, NT, D])
    aT = sb("_aT", [128, 2, S])
    p_a = ps("_pa", [128, 2, 512])
    p_y = [ps(f"_py{k}", [TP, 2, D]) for k in range(2)]
    banks = ((0, 2), (2, 1))
    if rank:
        p_r = ps("_pr", [128, 512])
        rT = sb("_rT", [128, S])

    with nc.Block() as block:
        @block.gpsimd
        def _(pool):
            with pool.Fori(0, B) as n:
                pool.wait_ge(a_turned, n)
                settle(pool, t)
                nc.gpsimd.tensor_copy(a[:, :, :], t.att[0:TP, ds(NT * n, NT), :]).then_inc(a_copied, 1)

        @block.tensor
        def _(pe):
            def turn(n):
                pe.wait_ge(a_copied, n + 1)
                pe.wait_ge(a_ready, n)
                for c in range(2):
                    for j in range(NT):
                        mm = nc.tensor.transpose(p_a[:, c, TP * j:TP * j + TP], a[:, j, 128 * c:128 * c + 128], t.ident[0:TP, 0:TP])
                mm.then_inc(a_turned, 1)

            def body(n, more):
                pe.wait_ge(a_ready, n + 1)
                if rank:
                    for c in range(2):
                        mm = nc.tensor.matmul(p_r[96:128, 0:S], t.basis_o[:, c, :], aT[:, c, :], start=(c == 0), stop=(c == 1))
                    mm.then_inc(r_made, 1)
                if more:
                    turn(n + 1)
                if rank:
                    pe.wait_ge(r_ready, n + 1)
                for k, (j0, m) in enumerate(banks):
                    pe.wait_ge(y_added, 2 * n + k)
                    for j in range(j0, j0 + m):
                        if rank:
                            mm = nc.tensor.matmul(p_y[k][:, j - j0, :], rT[96:128, TP * j:TP * j + TP], t.holo[96:128, :],
                                                  start=True, stop=True)
                        else:
                            for c in range(2):
                                mm = nc.tensor.matmul(p_y[k][:, j - j0, :], aT[:, c, TP * j:TP * j + TP], t.wo[:, c, :],
                                                      start=(c == 0), stop=(c == 1))
                    mm.then_inc(y_made, 1)

            turn(0)
            with pe.Fori(0, B - 1) as n:
                body(n, True)
            body(B - 1, False)

        @block.scalar
        def _(act):
            def copy(n):
                act.wait_ge(a_turned, n + 1)
                act.wait_ge(r_made if rank else y_made, n if rank else 2 * n)
                nc.scalar.activation(aT[:, :, :], p_a[:, :, 0:S], ACT.Copy).then_inc(a_ready, 1)

            def body(n, more):
                if rank:
                    act.wait_ge(r_made, n + 1)
                    act.wait_ge(y_made, 2 * n)
                    nc.scalar.activation(rT[96:128, :], p_r[96:128, 0:S], ACT.Copy).then_inc(r_ready, 1)
                if more:
                    copy(n + 1)

            copy(0)
            with act.Fori(0, B - 1) as n:
                body(n, True)
            body(B - 1, False)

        @block.vector
        def _(dve):
            with dve.Fori(0, B) as n:
                for k, (j0, m) in enumerate(banks):
                    h = t.h[:, ds(NT * n + j0, m), :]
                    if not rank:
                        bias = t.bo[:, :].unsqueeze(1).to_broadcast([TP, m, D])
                        nc.vector.tensor_tensor(h, h, bias, ALU.add).then_inc(biased, 1)
                    dve.wait_ge(y_made, 2 * n + k + 1)
                    if not rank:
                        dve.wait_ge(biased, 2 * n + k + 1)
                    nc.vector.tensor_tensor(h, h, p_y[k][:, 0:m, :], ALU.add).then_inc(y_added, 1)


def route_and_share0(nc, io, t, new_sem, ctx):
    def sb(name, shape, dt=F32):
        return ctx.enter_context(nc.sbuf_tensor("r0_" + name, shape, dt))

    def ps(name, shape, dt=F32):
        return ctx.enter_context(nc.psum_tensor("r0_" + name, shape, dt))

    def sm(name):
        return new_sem("r0_" + name)

    xf = NormalizedTransposed(nc, t, "r0", new_sem, sb, ps)
    all_stats, all_rstd = sm("all_stats"), sm("all_rstd")
    loaded, filled, row_filled, tid_written = sm("loaded"), sm("filled"), sm("row_filled"), sm("tid_written")
    lg_made, lg_shifted, exp_made, lg_read = sm("lg_made"), sm("lg_shifted"), sm("exp_made"), sm("lg_read")
    taken_ready, pos_made, pos_read, sent = sm("taken_ready"), sm("pos_made"), sm("pos_read"), sm("sent")
    rows_copied, slots_copied, places_ready = sm("rows_copied"), sm("slots_copied"), sm("places_ready")
    h1_made, h3_made, s_ready, g_ready, z_made, z_added = (sm("h1_made"), sm("h3_made"), sm("s_ready"), sm("g_ready"),
                                                           sm("z_made"), sm("z_added"))
    stats, mv = sb("stats", [TP, G, 6]), sb("mv", [TP, G, 2])
    var, rstd = sb("var", [TP, G]), sb("rstd", [TP, G])
    gate = sb("gate", [128, 2, E0])
    gate_b = sb("gate_b", [TP, E0])
    ws1, ws3 = sb("ws1", [128, 2, 2 * I0]), sb("ws3", [128, 2, 2 * I0])
    ws2 = sb("ws2", [IC, SIC, D])
    before32, before = sb("before32", [TP, TP]), sb("before", [TP, TP], BF16)
    ones = sb("ones", [TP, TP], BF16)
    rows = sb("rows", [TP, NT, ROW])
    mx, total = sb("mx", [TP, NT]), sb("total", [TP, NT])
    lg, scores, biased = sb("lg", [TP, NT, E0]), sb("scores", [TP, NT, E0]), sb("biased", [TP, NT, E0])
    top, topi = sb("top", [TP, NT, 8]), sb("topi", [TP, NT, 8], U32)
    pick, work = sb("pick", [TP, NT, K0, E0]), sb("work", [TP, NT, K0, E0])
    taken, taken_before = sb("taken", [TP, NT, E0], BF16), sb("taken_before", [TP, E0], BF16)
    place, keep = sb("place", [TP, NT, K0]), sb("keep", [TP, NT, K0])
    slots = sb("slots", [TP, NT, K0], U32)
    tidu, tid = sb("tidu", [TP, NT], U32), sb("tid", [TP, NT])
    row_now, slot_now = sb("row_now", [TP, NT, ROW]), sb("slot_now", [TP, NT, K0], U32)
    silu = [sb(f"silu{u}", [IC, S]) for u in range(2)]
    g = sb("g", [IC, SIC, S])
    p_rt = ps("prt", [TP, 2, 256])
    p_h = [[ps(f"ph{w}{u}", [IC, 512]) for u in range(2)] for w in (1, 3)]
    p_z = ps("pz", [TP, 2, D])
    loads = [(gate[:, :, :], io["gate0"]), (gate_b[:, :], io["gate0_b"].partition_broadcast(TP)), (ws1[:, :, :], io["ws1"]),
             (ws3[:, :, :], io["ws3"]), (ws2[:, :, :], io["ws2"]), (before32[:, :], io["before"])]
    p_lg = p_rt[:, 0, 0:NT * E0].rearrange("p (j e) -> p j e", j=NT)
    p_pos = p_rt[:, 1, 0:NT * E0].rearrange("p (j e) -> p j e", j=NT)
    ids, wts = rows[:, :, IDS:IDS + K0], rows[:, :, WTS:WTS + K0]

    def each_choice(x):
        return x.unsqueeze(2).to_broadcast([TP, NT, K0, E0])

    with nc.Block() as block:
        @block.sync
        def _(sp):
            for dst, src in loads:
                sp.dma_start(dst, src).then_inc(loaded, 16)

        @block.gpsimd
        def _(pool):
            nc.gpsimd.iota(tidu[:, :], [[TP, NT]], base=0, channel_multiplier=1).then_inc(filled, 1)
            pool.wait_ge(filled, 1)
            nc.gpsimd.memset(ones[:, :], 1.0).then_inc(filled, 1)
            pool.wait_ge(filled, 2)
            nc.gpsimd.memset(taken_before[:, :], 0.0).then_inc(filled, 1)
            pool.wait_ge(filled, 3)
            nc.gpsimd.memset(rows[:, :, IDS:ROW], 0.0).then_inc(filled, 1)
            pool.wait_ge(filled, 4)
            pool.wait_ge(t.sem.prefilled, 16 * len(prefills(t)))
            def body(n, more):
                pool.wait_ge(places_ready, n + 1)
                pool.wait_ge(sent, 16 * NT * K0 * n)
                settle(pool, t)
                nc.gpsimd.tensor_copy(row_now[:, :, TID].bitcast(U32), rows[:, :, TID].bitcast(U32))
                nc.gpsimd.tensor_copy(slot_now[:, :, :], slots[:, :, :]).then_inc(slots_copied, 1)
                pool.wait_ge(slots_copied, n + 1)
                pool.wait_ge(rows_copied, n + 1)
                settle(pool, t)
                for j in range(NT):
                    for k in range(K0):
                        nc.gpsimd.indirect_dma_start(t.disp0, bass.IndirectOffsetOnAxis(ap=slot_now[:, j, k:k + 1], axis=0),
                                                     row_now[:, j, :], None, bounds_check=E0 * CAP - 1,
                                                     oob_is_err=False).then_inc(sent, 16)

            pool.wait_ge(all_stats, 1)
            t.pool.did(nc.gpsimd.tensor_scalar(var[:, :], mv[:, :, 1], EPS, None, ALU.add))
            t.pool.wait()
            nc.gpsimd.tensor_tensor(rstd[:, :], var[:, :], t.half[0:TP, 0:1].to_broadcast([TP, G]), ALU.pow).then_inc(all_rstd, 1)
            with pool.Fori(0, B - 1) as n:
                body(n, True)
            body(B - 1, False)
            pool.wait_ge(sent, 16 * NT * K0 * B)

        @block.tensor
        def _(pe):
            pe.wait_ge(loaded, 16 * len(loads))
            pe.wait_ge(tid_written, 1)
            def body(n, more):
                pe.wait_ge(xf.xt_ready, n + 1)
                pe.wait_ge(pos_read, n)
                for j in range(NT):
                    for c in range(2):
                        mm = nc.tensor.matmul(p_lg[:, j, :], xf.xT[:, c, TP * j:TP * j + TP], gate[:, c, :], start=(c == 0), stop=(c == 1))
                mm.then_inc(lg_made, 1)
                for c in range(SIC):
                    m = SIC * n + c
                    if c >= 2:
                        pe.wait_ge(g_ready, m - 1)
                    else:
                        pe.wait_ge(g_ready, SIC * n)
                    for w, (weights, made) in enumerate(((ws1, h1_made), (ws3, h3_made))):
                        for k in range(2):
                            mm = nc.tensor.matmul(p_h[w][c % 2][:, 0:S], weights[:, k, IC * c:IC * c + IC], xf.xT[:, k, :],
                                                  start=(k == 0), stop=(k == 1))
                        mm.then_inc(made, 1)
                pe.wait_ge(h3_made, SIC * (n + 1))
                pe.sem_inc(xf.xt_used, 1)
                pe.wait_ge(taken_ready, n + 1)
                for j in range(NT):
                    nc.tensor.matmul(p_pos[:, j, :], before[:, :], taken[:, j, :], start=True, stop=False)
                    for i in range(j):
                        nc.tensor.matmul(p_pos[:, j, :], ones[:, :], taken[:, i, :], start=False, stop=False)
                    mm = nc.tensor.matmul(p_pos[:, j, :], ones[:, :], taken_before[:, :], start=False, stop=True)
                mm.then_inc(pos_made, 1)
                pe.wait_ge(g_ready, SIC * (n + 1))
                for half, tiles in enumerate(([0, 1], [2])):
                    pe.wait_ge(z_added, 2 * n + half)
                    for j in tiles:
                        for c in range(SIC):
                            mm = nc.tensor.matmul(p_z[:, j % 2, :], g[:, c, TP * j:TP * j + TP], ws2[:, c, :],
                                                  start=(c == 0), stop=(c == SIC - 1))
                    mm.then_inc(z_made, 1)
                    if half == 0 and more:
                        xf.turn(pe, n + 1)

            xf.turn(pe, 0)
            with pe.Fori(0, B - 1) as n:
                body(n, True)
            body(B - 1, False)

        @block.scalar
        def _(act):
            def body(n, more):
                act.wait_ge(xf.xn_ready, n + 1)
                act.wait_ge(rows_copied, n)
                nc.scalar.activation(rows[:, :, 0:D], xf.xn[:, :, :], ACT.Copy).then_inc(row_filled, 1)
                act.wait_ge(lg_shifted, n + 1)
                nc.scalar.activation(lg[:, :, :], lg[:, :, :], ACT.Exp).then_inc(exp_made, 1)
                for c in range(SIC):
                    m = SIC * n + c
                    act.wait_ge(h1_made, m + 1)
                    act.wait_ge(g_ready, SIC * n + max(c - 1, 0))
                    nc.scalar.activation(silu[c % 2][:, :], p_h[0][c % 2][:, 0:S], ACT.Silu).then_inc(s_ready, 1)
                if more:
                    xf.copy(act, n + 1)
                act.wait_ge(places_ready, n + 1)
                act.wait_ge(sent, 16 * NT * K0 * n)
                nc.scalar.activation(row_now[:, :, 0:TID], rows[:, :, 0:TID], ACT.Copy).then_inc(rows_copied, 1)

            xf.copy(act, 0)
            with act.Fori(0, B - 1) as n:
                body(n, True)
            body(B - 1, False)

        @block.vector
        def _(dve):
            def step(ins):
                t.dve.did(ins)
                t.dve.wait()

            for g0 in range(G):
                t.dve.did(nc.vector.bn_stats(stats[:, g0, :], t.h[:, g0, :]))
            t.dve.wait()
            for g0 in range(G):
                ins = nc.vector.bn_aggr(mv[:, g0, :], stats[:, g0, :])
            ins.then_inc(all_stats, 1)
            dve.wait_ge(loaded, 16 * len(loads))
            dve.wait_ge(filled, 4)
            step(nc.vector.tensor_copy(before[:, :], before32[:, :]))
            nc.vector.tensor_copy(tid[:, :], tidu[:, :]).then_inc(tid_written, 1)
            dve.wait_ge(tid_written, 1)
            def normalize(n):
                dve.wait_ge(xf.xt_turned, n)
                dve.wait_ge(row_filled, n)
                for j in range(NT):
                    ins = nc.vector.tensor_scalar(xf.xn[:, j, :], t.h[:, ds(NT * n + j, 1), :].rearrange("p a d -> p (a d)"),
                                                  mv[:, ds(NT * n + j, 1), 0:1].rearrange("p a o -> p (a o)"), rstd[:, ds(NT * n + j, 1)],
                                                  ALU.subtract, ALU.mult)
                ins.then_inc(xf.xn_ready, 1)

            def body(n, more):
                def gated(chunks):
                    for c in chunks:
                        m = SIC * n + c
                        dve.wait_ge(s_ready, m + 1)
                        dve.wait_ge(h3_made, m + 1)
                        dve.wait_ge(z_made, 2 * n)
                        nc.vector.tensor_tensor(g[:, c, :], silu[c % 2][:, :], p_h[1][c % 2][:, 0:S], ALU.mult).then_inc(g_ready, 1)

                dve.wait_ge(lg_made, n + 1)
                step(nc.vector.tensor_reduce(mx[:, :], p_lg, AX_X, ALU.max))
                nc.vector.tensor_tensor(lg[:, :, :], p_lg, mx[:, :].unsqueeze(2).to_broadcast([TP, NT, E0]),
                                        ALU.subtract).then_inc(lg_shifted, 1)
                dve.wait_ge(exp_made, n + 1)
                step(nc.vector.tensor_reduce(total[:, :], lg[:, :, :], AX_X, ALU.add))
                step(nc.vector.reciprocal(total[:, :], total[:, :]))
                step(nc.vector.tensor_tensor(scores[:, :, :], lg[:, :, :], total[:, :].unsqueeze(2).to_broadcast([TP, NT, E0]), ALU.mult))
                step(nc.vector.tensor_tensor(biased[:, :, :], scores[:, :, :], gate_b[:, :].unsqueeze(1).to_broadcast([TP, NT, E0]), ALU.add))
                for j in range(NT):
                    settle(dve, t)
                    step(nc.vector.max(top[:, j, :], biased[:, j, :]))
                for j in range(NT):
                    settle(dve, t)
                    step(nc.vector.max_index(topi[:, j, :], top[:, j, :], biased[:, j, :]))
                gated([0, 1])
                dve.wait_ge(rows_copied, n)
                dve.wait_ge(slots_copied, n)
                step(nc.vector.tensor_copy(ids, topi[:, :, 0:K0]))
                step(nc.vector.tensor_tensor(pick[:, :, :, :], t.iota[0:TP, 0:E0].unsqueeze(1).unsqueeze(1).to_broadcast([TP, NT, K0, E0]),
                                             ids.unsqueeze(3).to_broadcast([TP, NT, K0, E0]), ALU.is_equal))
                with nc.allow_low_precision(reason="zeros and ones are exact"):
                    nc.vector.tensor_reduce(taken[:, :, :], pick[:, :, :, :].rearrange("p j k e -> p j e k"), AX_X, ALU.add).then_inc(taken_ready, 1)
                step(nc.vector.tensor_tensor(work[:, :, :, :], pick[:, :, :, :], each_choice(scores[:, :, :]), ALU.mult))
                step(nc.vector.tensor_reduce(wts, work[:, :, :, :], AX_X, ALU.add))
                if more:
                    normalize(n + 1)
                gated([2, 3])
                dve.wait_ge(pos_made, n + 1)
                step(nc.vector.tensor_tensor(work[:, :, :, :], pick[:, :, :, :], each_choice(p_pos), ALU.mult))
                dve.sem_inc(pos_read, 1)
                step(nc.vector.tensor_reduce(place[:, :, :], work[:, :, :, :], AX_X, ALU.add))
                step(nc.vector.tensor_scalar(keep[:, :, :], place[:, :, :], float(CAP), None, ALU.is_lt))
                step(nc.vector.tensor_tensor(wts, wts, keep[:, :, :], ALU.mult))
                step(nc.vector.tensor_scalar(keep[:, :, :], keep[:, :, :], -float(E0 * CAP), float(E0 * CAP), ALU.mult, ALU.add))
                step(nc.vector.tensor_tensor(place[:, :, :], place[:, :, :], keep[:, :, :], ALU.add))
                step(nc.vector.scalar_tensor_tensor(out=place[:, :, :], in0=ids, scalar=float(CAP), in1=place[:, :, :], op0=ALU.mult, op1=ALU.add))
                step(nc.vector.tensor_copy(slots[:, :, :], place[:, :, :]))
                step(nc.vector.tensor_copy(rows[:, :, TID].bitcast(U32), tid[:, :]))
                nc.vector.tensor_scalar(tid[:, :], tid[:, :], float(S), None, ALU.add).then_inc(places_ready, 1)
                dve.wait_ge(places_ready, n + 1)
                def add_shared(half, tiles):
                    dve.wait_ge(z_made, 2 * n + half + 1)
                    m = len(tiles)
                    h = t.h[:, ds(NT * n + tiles[0], m), :]
                    nc.vector.tensor_tensor(h, h, p_z[:, 0:m, :], ALU.add).then_inc(z_added, 1)

                add_shared(0, [0, 1])
                for j in range(NT):
                    step(nc.vector.tensor_tensor(taken_before[:, :], taken_before[:, :], taken[:, j, :], ALU.add))
                add_shared(1, [2])
                dve.wait_ge(z_added, 2 * (n + 1))

            dve.wait_ge(all_rstd, 1)
            normalize(0)
            with dve.Fori(0, B - 1) as n:
                t.dve.enter(n, 27)
                body(n, True)
                t.dve.leave(B - 1)
            body(B - 1, False)


def experts0(nc, io, t, new_sem, ctx):
    def sb(name, shape, dt=F32):
        return ctx.enter_context(nc.sbuf_tensor("e0_" + name, shape, dt))

    def ps(name, shape, dt=F32):
        return ctx.enter_context(nc.psum_tensor("e0_" + name, shape, dt))

    def sm(name):
        return new_sem("e0_" + name)

    x_loaded = [sm(f"x_loaded{u}") for u in range(DEEP)]
    w_loaded = [sm(f"w_loaded{u}") for u in range(DEEP)]
    x_turned, x_ready, h1_made, h3_made, s_ready, g_ready = (sm("x_turned"), sm("x_ready"), sm("h1_made"), sm("h3_made"),
                                                             sm("s_ready"), sm("g_ready"))
    y_made, y_ready, x_free = sm("y_made"), sm("y_ready"), sm("x_free")
    y_added = [sm(f"y_added{u}") for u in range(2)]
    x = [sb(f"x{u}", [128, ROW]) for u in range(DEEP)]
    w13 = [sb(f"w13{u}", [128, 2, 2 * I0]) for u in range(DEEP)]
    w2 = [sb(f"w2{u}", [IC, 2, D]) for u in range(DEEP)]
    xT = [sb(f"xT{u}", [128, 2, 128]) for u in range(2)]
    silu = [sb(f"silu{u}", [IC, 2, 128]) for u in range(2)]
    g = [sb(f"g{u}", [IC, 2, 128]) for u in range(2)]
    y = [sb(f"y{u}", [128, D]) for u in range(DEEP)]
    who = [sb(f"who{u}", [128, 1], U32) for u in range(DEEP)]
    match, weight = [sb(f"match{u}", [128, K0]) for u in range(2)], [sb(f"weight{u}", [128, 1]) for u in range(2)]
    p_x = [ps(f"px{u}", [128, 4, 128]) for u in range(2)]
    p_h = [[ps(f"ph{w}{u}", [IC, 4, 128]) for u in range(2)] for w in (1, 3)]
    p_y = [ps(f"py{u}", [128, 512]) for u in range(2)]
    rounds = E0 // DEEP

    def before(e, n):
        return max(e - n + 1, 0) if isinstance(e, int) else e - n + 1

    with nc.Block() as block:
        @block.sync
        def _(sp):
            def load(i, first):
                for u in range(DEEP):
                    e = DEEP * i + u
                    sp.wait_ge(x_free, e + 1)
                    sp.dma_start(x[u][:, :], t.disp0[ds(CAP * e, CAP), :]).then_inc(x_loaded[u], 16)
                    if not first:
                        sp.wait_ge(y_made, e - DEEP + 1)
                    sp.dma_start(w13[u][:, :, :], io["w13"][ds(e, 1)].rearrange("e p c i -> p (e c) i")).then_inc(w_loaded[u], 16)
                    sp.dma_start(w2[u][:, :, :], io["w2"][ds(e, 1)].rearrange("e p c d -> p (e c) d")).then_inc(w_loaded[u], 16)

            load(0, True)
            with sp.Fori(1, rounds) as i:
                load(i, False)

        @block.tensor
        def _(pe):
            def turn(i, u):
                e = DEEP * i + u
                pe.wait_ge(x_loaded[u], 16 * (i + 1))
                pe.wait_ge(x_ready, before(e, 2))
                for c in range(2):
                    mm = nc.tensor.transpose(p_x[u % 2][:, c, :], x[u][:, 128 * c:128 * c + 128], t.ident[:, :])
                mm.then_inc(x_turned, 1)

            def up(i, u):
                e = DEEP * i + u
                pe.wait_ge(x_ready, e + 1)
                pe.wait_ge(w_loaded[u], 32 * (i + 1))
                pe.wait_ge(g_ready, before(e, 2))
                for w, made in ((0, h1_made), (1, h3_made)):
                    for m in range(2):
                        for c in range(2):
                            mm = nc.tensor.matmul(p_h[w][u % 2][:, m, :], w13[u][:, c, I0 * w + IC * m:I0 * w + IC * m + IC],
                                                  xT[u % 2][:, c, :], start=(c == 0), stop=(c == 1))
                    mm.then_inc(made, 1)

            def down(i, u):
                e = DEEP * i + u
                pe.wait_ge(g_ready, e + 1)
                pe.wait_ge(y_ready, before(e, 2))
                for m in range(2):
                    mm = nc.tensor.matmul(p_y[u % 2][:, 0:D], g[u % 2][:, m, :], w2[u][:, m, :], start=(m == 0), stop=(m == 1))
                mm.then_inc(y_made, 1)

            def experts(i, first, last):
                for u in range(DEEP):
                    if u < DEEP - 1:
                        turn(i, u + 1)
                    elif not last:
                        turn(i + 1, 0)
                    up(i, u)
                    if u:
                        down(i, u - 1)
                    elif not first:
                        down(i - 1, DEEP - 1)

            turn(0, 0)
            experts(0, True, False)
            with pe.Fori(1, rounds - 1) as i:
                experts(i, False, False)
            experts(rounds - 1, False, True)
            down(rounds - 1, DEEP - 1)

        @block.scalar
        def _(act):
            def copy_x(i, u):
                e = DEEP * i + u
                act.wait_ge(x_turned, e + 1)
                act.wait_ge(h3_made, before(e, 2))
                nc.scalar.activation(xT[u % 2][:, :, :], p_x[u % 2][:, 0:2, :], ACT.Copy).then_inc(x_ready, 1)

            def gate(i, u):
                e = DEEP * i + u
                act.wait_ge(h1_made, e + 1)
                act.wait_ge(g_ready, before(e, 2))
                nc.scalar.activation(silu[u % 2][:, :, :], p_h[0][u % 2][:, 0:2, :], ACT.Silu).then_inc(s_ready, 1)

            def experts(i, last):
                for u in range(DEEP):
                    if u < DEEP - 1:
                        copy_x(i, u + 1)
                    elif not last:
                        copy_x(i + 1, 0)
                    gate(i, u)

            copy_x(0, 0)
            experts(0, False)
            with act.Fori(1, rounds - 1) as i:
                experts(i, False)
            experts(rounds - 1, True)

        @block.vector
        def _(dve):
            def gated(i, u):
                e = DEEP * i + u
                dve.wait_ge(x_loaded[u], 16 * (i + 1))
                dve.wait_ge(y_ready, before(e, 2))
                if not isinstance(i, int) or i:
                    dve.wait_ge(y_added[u % 2], 16 * (DEEP // 2 * (i - 1) + u // 2 + 1))
                t.dve.did(nc.vector.tensor_copy(who[u][:, :], x[u][:, TID:TID + 1].bitcast(U32)))
                t.dve.did(nc.vector.tensor_scalar(match[u % 2][:, :], x[u][:, IDS:IDS + K0], t.iota[:, ds(e, 1)], None, ALU.is_equal))
                t.dve.wait()
                t.dve.did(nc.vector.tensor_tensor_reduce(match[u % 2][:, :], match[u % 2][:, :], x[u][:, WTS:WTS + K0], 1.0, 0.0,
                                                         ALU.mult, ALU.add, weight[u % 2][:, :]))
                t.dve.wait()
                dve.wait_ge(x_turned, e + 1)
                dve.sem_inc(x_free, 1)
                dve.wait_ge(s_ready, e + 1)
                dve.wait_ge(h3_made, e + 1)
                dve.wait_ge(y_made, before(e, 2))
                nc.vector.tensor_tensor(g[u % 2][:, :, :], silu[u % 2][:, :, :], p_h[1][u % 2][:, 0:2, :], ALU.mult).then_inc(g_ready, 1)

            def weighted(i, u):
                e = DEEP * i + u
                dve.wait_ge(y_made, e + 1)
                nc.vector.tensor_scalar(y[u][:, :], p_y[u % 2][:, 0:D], weight[u % 2][:, :], None, ALU.mult).then_inc(y_ready, 1)

            def experts(i, first):
                for u in range(DEEP):
                    gated(i, u)
                    if u:
                        weighted(i, u - 1)
                    elif not first:
                        weighted(i - 1, DEEP - 1)

            dve.sem_inc(x_free, DEEP)
            experts(0, True)
            with dve.Fori(0, rounds - 1) as i:
                t.dve.enter(i, 3 * DEEP)
                experts(i + 1, False)
                t.dve.leave(rounds - 1)
            weighted(rounds - 1, DEEP - 1)

        @block.gpsimd
        def _(pool):
            with pool.Fori(0, rounds) as i:
                for u in range(DEEP):
                    e = DEEP * i + u
                    pool.wait_ge(y_ready, e + 1)
                    pool.wait_ge(y_added[u % 2], 16 * (DEEP // 2 * i + u // 2))
                    settle(pool, t)
                    nc.gpsimd.indirect_dma_start(t.sum0[u % 2], bass.IndirectOffsetOnAxis(ap=who[u][:, 0:1], axis=0),
                                                 y[u][:, :], None, bounds_check=T + 127, oob_is_err=True,
                                                 compute_op=ALU.add).then_inc(y_added[u % 2], 16)
            for u in range(2):
                pool.wait_ge(y_added[u], 16 * (E0 // 2))


def rotary_qkv(nc, io, t, new_sem, ctx):
    def sb(name, shape, dt=F32):
        return ctx.enter_context(nc.sbuf_tensor("p1_" + name, shape, dt))

    def ps(name, shape, dt=F32):
        return ctx.enter_context(nc.psum_tensor("p1_" + name, shape, dt))

    def sm(name):
        return new_sem("p1_" + name)

    xf = NormalizedTransposed(nc, t, "p1", new_sem, sb, ps)
    cut = [Splitter(nc, t, "p1_q", 0, float(HD) ** -0.5, new_sem, sb), Splitter(nc, t, "p1_k", 1, 1.0, new_sem, sb)]
    loaded, sums_loaded, ones_set = sm("loaded"), sm("sums_loaded"), sm("ones_set")
    c_made, c_ready = sm("c_made"), sm("c_ready")
    rope_made, rope_read, low_made, low_ready = sm("rope_made"), sm("rope_read"), sm("low_made"), sm("low_ready")
    rope_ready, high_ready, v_made, v_ready = sm("rope_ready"), sm("high_ready"), sm("v_made"), sm("v_ready")
    w_c = sb("w_c", [128, 2, 128])
    w_low = sb("w_low", [128, 128])
    w_rope = [[sb(f"w_rope{w}{x}", [128, 2, 128]) for x in range(2)] for w in range(2)]
    biases = sb("biases", [128, 7])
    w_v = sb("w_v", [128, D])
    b_v = sb("b_v", [TP, D])
    trig = sb("trig", [128, 2, S])
    cT = sb("cT", [128, S])
    joined = [t.att, sb("more_sums", [TP, G, D])]
    turned = [sb(f"turned{x}", [128, S]) for x in range(2)]
    act_in = [sb(f"qk{w}", [128, 2, S]) for w in range(2)]
    p_c = ps("pc", [128, 512])
    p_r = [ps(f"pr{x}", [128, 512]) for x in range(2)]
    p_l = ps("pl", [128, 512])
    p_v = ps("pv", [TP, 2, D])
    loads = [(w_c[:, :, :], io["w_c"]), (w_low[:, :], io["w_low"]), (biases[:, :], io["biases"]), (w_v[64:128, :], io["w_v"]),
             (b_v[:, :], io["b_v"].partition_broadcast(TP)), (trig[:, :, :], io["rope"])]
    loads += [(w_rope[w][x][:, :, :], io["w_rope"][w, x]) for w in range(2) for x in range(2)]

    with nc.Block() as block:
        @block.sync
        def _(sp):
            def load_sums(n):
                for u, sums in enumerate(joined):
                    sp.dma_start(sums[0:TP, ds(NT * n, NT), :],
                                 t.sum0[u][ds(S * n, S), :].rearrange("(g p) d -> p g d", p=TP)).then_inc(sums_loaded, 16)

            load_sums(0)
            for dst, src in loads:
                sp.dma_start(dst, src).then_inc(loaded, 16)
            def body(n, more):
                if more:
                    sp.wait_ge(sums_loaded, 16 * len(joined) * (n + 2))
                    load_sums(n + 2)
                for c in cut:
                    c.store(sp, n)

            sp.wait_ge(sums_loaded, 16 * len(joined))
            load_sums(1)
            with sp.Fori(0, B - 2) as n:
                body(n, True)
            body(B - 2, False)
            body(B - 1, False)
            for c in cut:
                sp.wait_ge(c.stored, 16 * B)

        @block.tensor
        def _(pe):
            pe.wait_ge(loaded, 16 * len(loads))
            def body(n, more):
                pe.wait_ge(xf.xt_ready, n + 1)
                for c in range(2):
                    mm = nc.tensor.matmul(p_c[:, 0:S], w_c[:, c, :], xf.xT[:, c, :], start=(c == 0), stop=(c == 1))
                mm.then_inc(c_made, 1)
                for w in range(2):
                    m = 2 * n + w
                    pe.wait_ge(rope_read, m)
                    for x in range(2):
                        for c in range(2):
                            mm = nc.tensor.matmul(p_r[x][:, 0:S], w_rope[w][x][:, c, :], xf.xT[:, c, :], start=(c == 0), stop=(c == 1))
                    mm.then_inc(rope_made, 1)
                    pe.wait_ge(c_ready, n + 1)
                    pe.wait_ge(low_ready, m)
                    nc.tensor.matmul(p_l[:, 0:S], w_low[64 * w:64 * w + 64, :], cT[64 * w:64 * w + 64, :],
                                     start=True, stop=True).then_inc(low_made, 1)
                pe.wait_ge(rope_made, 2 * n + 2)
                pe.sem_inc(xf.xt_used, 1)
                if more:
                    xf.turn(pe, n + 1)
                for half, tiles in enumerate(([0, 1], [2])):
                    pe.wait_ge(v_ready, 2 * n + half)
                    for j in tiles:
                        mm = nc.tensor.matmul(p_v[:, j % 2, :], cT[64:128, TP * j:TP * j + TP], w_v[64:128, :], start=True, stop=True)
                    mm.then_inc(v_made, 1)

            xf.turn(pe, 0)
            with pe.Fori(0, B - 1) as n:
                body(n, True)
            body(B - 1, False)

        @block.scalar
        def _(act):
            def body(n, more):
                act.wait_ge(c_made, n + 1)
                act.wait_ge(v_made, 2 * n)
                nc.scalar.activation(cT[:, :], p_c[:, 0:S], ACT.Gelu, bias=biases[:, 0:1]).then_inc(c_ready, 1)
                for w in range(2):
                    m = 2 * n + w
                    act.wait_ge(low_made, m + 1)
                    act.wait_ge(cut[w].rest_ready, n)
                    nc.scalar.activation(act_in[w][:, 0, :], p_l[:, 0:S], ACT.Gelu, bias=biases[:, 1 + w:2 + w]).then_inc(low_ready, 1)
                    if w and more:
                        xf.copy(act, n + 1)
                    act.wait_ge(rope_ready, m + 1)
                    nc.scalar.activation(act_in[w][:, 1, :], turned[0][:, :], ACT.Gelu).then_inc(high_ready, 1)
                    act.wait_ge(low_ready, m + 1)
                    act.wait_ge(high_ready, m + 1)
                    cut[w].first(act, n, act_in[w][:, :, :])

            xf.copy(act, 0)
            with act.Fori(0, B - 1) as n:
                body(n, True)
            body(B - 1, False)

        @block.vector
        def _(dve):
            dve.wait_ge(loaded, 16 * len(loads))
            def add_sums(n):
                dve.wait_ge(sums_loaded, 16 * len(joined) * (n + 1))
                h = t.h[:, ds(NT * n, NT), :]
                for sums in joined:
                    t.dve.did(nc.vector.tensor_tensor(h, h, sums[0:TP, ds(NT * n, NT), :], ALU.add))
                    t.dve.wait()
                xf.row_stats(dve, n)

            def body(n, more):
                if more:
                    add_sums(n + 1)
                for w in range(2):
                    if w and more:
                        xf.normalize(dve, n + 1)
                    m = 2 * n + w
                    dve.wait_ge(rope_made, m + 1)
                    dve.wait_ge(high_ready, m)
                    t.dve.did(nc.vector.scalar_tensor_tensor(out=turned[0][:, :], in0=p_r[0][:, 0:S], scalar=biases[:, 3 + 2 * w:4 + 2 * w],
                                                             in1=trig[:, 0, :], op0=ALU.add, op1=ALU.mult))
                    t.dve.did(nc.vector.scalar_tensor_tensor(out=turned[1][:, :], in0=p_r[1][:, 0:S], scalar=biases[:, 4 + 2 * w:5 + 2 * w],
                                                             in1=trig[:, 1, :], op0=ALU.add, op1=ALU.mult))
                    t.dve.wait()
                    dve.sem_inc(rope_read, 1)
                    nc.vector.tensor_tensor(turned[0][:, :], turned[0][:, :], turned[1][:, :], ALU.add).then_inc(rope_ready, 1)
                    dve.wait_ge(rope_ready, m + 1)
                for w in range(2):
                    cut[w].residue(dve, n, act_in[w][:, :, :])
                for half, tiles in enumerate(([0, 1], [2])):
                    dve.wait_ge(v_made, 2 * n + half + 1)
                    m = len(tiles)
                    nc.vector.tensor_tensor(t.v[:, ds(NT * n + tiles[0], m), :, 0:HD], p_v[:, 0:m, :].rearrange("p j (h d) -> p j h d", h=NH),
                                            b_v[:, :].rearrange("p (h d) -> p h d", h=NH).unsqueeze(1).to_broadcast([TP, m, NH, HD]),
                                            ALU.add).then_inc(v_ready, 1)
                for w in range(2):
                    cut[w].third(dve, n)

            add_sums(0)
            xf.normalize(dve, 0)
            with dve.Fori(0, B - 1) as n:
                t.dve.enter(n, len(joined) + xf.STEPS + 4)
                body(n, True)
                t.dve.leave(B - 1)
            body(B - 1, False)

        @block.gpsimd
        def _(pool):
            def body(n, more):
                if more:
                    xf.invert(pool, n + 1)
                for w in range(2):
                    cut[w].second(pool, n)

            xf.invert(pool, 0)
            with pool.Fori(0, B - 1) as n:
                t.pool.enter(n, xf.POOL_STEPS)
                body(n, True)
                t.pool.leave(B - 1)
            body(B - 1, False)


def route_and_share1(nc, io, t, new_sem, ctx):
    def sb(name, shape, dt=F32):
        return ctx.enter_context(nc.sbuf_tensor("r1_" + name, shape, dt))

    def ps(name, shape, dt=F32):
        return ctx.enter_context(nc.psum_tensor("r1_" + name, shape, dt))

    def sm(name):
        return new_sem("r1_" + name)

    K1 = 2
    MC = HID // 128
    EARLY = 4
    xf = NormalizedTransposed(nc, t, "r1", new_sem, sb, ps)
    loaded, w_loaded, filled, row_filled, rows_ready, stored = (sm("loaded"), sm("w_loaded"), sm("filled"), sm("row_filled"),
                                                                 sm("rows_ready"), sm("stored"))
    tid_ready, xt_kept = sm("tid_ready"), sm("xt_kept")
    lg_made, lg_read, gap_ready, exp_made = sm("lg_made"), sm("lg_read"), sm("gap_ready"), sm("exp_made")
    taken_ready, pos_made, pos_read = sm("taken_ready"), sm("pos_made"), sm("pos_read")
    total_made, slots_ready = sm("total_made"), sm("slots_ready")
    back = [sm(f"back{u}") for u in range(2)]
    slot_copied, sent, = sm("slot_copied"), sm("sent")
    h_made, s_ready, z_made, z_added = sm("h_made"), sm("s_ready"), sm("z_made"), sm("z_added")
    gate = sb("gate", [128, 2, E1])
    before32, before = sb("before32", [TP, TP]), sb("before", [TP, TP], BF16)
    ones = sb("ones", [TP, 128], BF16)
    rows = sb("rows", [TP, NT, ROW])
    lg = sb("lg", [TP, NT, E1])
    top, topi = sb("top", [TP, NT, 8]), sb("topi", [TP, NT, 8], U32)
    gap = sb("gap", [TP, NT])
    pick, work = sb("pick", [TP, NT, K1, E1]), sb("work", [TP, NT, K1, E1])
    taken, taken_before = sb("taken", [TP, NT, E1], BF16), sb("taken_before", [TP, E1], BF16)
    place, expert = sb("place", [TP, G, K1]), sb("expert", [TP, G, K1])
    pick_all = sb("pick_all", [TP, G * K1, E1])
    slots = sb("slots", [TP, G, K1], U32)
    slot_now = [sb(f"slot_now{u}", [TP, NT * K1], U32) for u in range(2)]
    row_now = [sb(f"row_now{u}", [TP, NT, ROW]) for u in range(2)]
    tidu, tid = sb("tidu", [TP, NT], U32), sb("tid", [TP, NT])
    need, needu = sb("need", [128, E1]), sb("needu", [128, E1], U32)
    upto, start, plain = sb("upto", [128, E1]), sb("start", [128, E1]), sb("plain", [128, E1])
    over = sb("over", [128, SLOT_TILES, E1])
    silu = sb("silu", [128, MC, S])
    sw1, sw2 = sb("sw1", [128, 2, HID]), sb("sw2", [128, MC, D])
    kept = t.att[:, :, :].rearrange("p g d -> p (g d)")[:, 0:B * 2 * S].rearrange("p (n c s) -> p n c s", n=B, c=2)
    p_rt = ps("prt", [128, 2, 256])
    p_lg = p_rt[0:TP, 0, 0:NT * E1].rearrange("p (j e) -> p j e", j=NT)
    p_pos = p_rt[0:TP, 1, 0:NT * E1].rearrange("p (j e) -> p j e", j=NT)
    p_total = p_rt[:, 1, 0:E1]
    p_h = [ps(f"ph{u}", [128, 512]) for u in range(2)]
    p_z = [ps(f"pz{u}", [TP, 512]) for u in range(2)]
    loads = [(gate[:, :, :], io["gate1"]), (before32[:, :], io["before"]), (sw1[:, :, :], io["sw1"]), (sw2[:, :, :], io["sw2"])]
    ids, wts = rows[:, :, IDS:IDS + K1], rows[:, :, WTS:WTS + K1]

    with nc.Block() as block:
        @block.sync
        def _(sp):
            for dst, src in loads:
                sp.dma_start(dst, src).then_inc(loaded, 16)
            for e in range(E1):
                sp.dma_start(t.w1s[:, e, :, :], io["ew1"][e]).then_inc(w_loaded, 16)
            with sp.Fori(0, B) as n:
                sp.wait_ge(rows_ready, n + 1)
                sp.wait_ge(row_filled, n + 1)
                sp.dma_start(t.rows1[ds(S * n, S), :].rearrange("(j p) r -> p j r", p=TP), rows[:, :, :]).then_inc(stored, 16)
            sp.wait_ge(stored, 16 * B)
            sp.wait_ge(w_loaded, 16 * E1)
            with sp.Fori(0, B // 2) as i:
                for u in range(2):
                    n = 2 * i + u
                    sp.wait_ge(sent, 16 * NT * K1 * (2 * i))
                    sp.dma_start(row_now[u][:, :, :], t.rows1[ds(S * n, S), :].rearrange("(j p) r -> p j r", p=TP)).then_inc(back[u], 16)

        @block.gpsimd
        def _(pool):
            fills = [(ones[:, :], 1.0), (taken_before[:, :], 0.0), (rows[:, :, IDS:ROW], 0.0), (plain[:, :], 1.0)]
            for n, (dst, value) in enumerate(fills):
                nc.gpsimd.memset(dst, value).then_inc(filled, 1)
                pool.wait_ge(filled, n + 1)
            nc.gpsimd.iota(tidu[:, :], [[TP, NT]], base=0, channel_multiplier=1).then_inc(filled, 1)
            def body(n, more):
                pool.wait_ge(xf.xt_ready, n + 1)
                settle(pool, t)
                nc.gpsimd.tensor_copy(kept[:, ds(n, 1), :, :].rearrange("p a c s -> p (a c) s"), xf.xT[:, :, :]).then_inc(xt_kept, 1)
                if more:
                    xf.invert(pool, n + 1)

            xf.invert(pool, 0)
            with pool.Fori(0, B - 1) as n:
                t.pool.enter(n, xf.POOL_STEPS)
                body(n, True)
                t.pool.leave(B - 1)
            body(B - 1, False)
            pool.wait_ge(slots_ready, 1)
            with pool.Fori(0, B // 2) as i:
                for u in range(2):
                    n = 2 * i + u
                    pool.wait_ge(sent, 16 * NT * K1 * n)
                    settle(pool, t)
                    nc.gpsimd.tensor_copy(slot_now[u][:, :], slots[:, ds(NT * n, NT), :].rearrange("p j k -> p (j k)")).then_inc(slot_copied, 1)
                    pool.wait_ge(slot_copied, n + 1)
                    pool.wait_ge(back[u], 16 * (i + 1))
                    settle(pool, t)
                    for j in range(NT):
                        for k in range(K1):
                            nc.gpsimd.indirect_dma_start(t.disp1, bass.IndirectOffsetOnAxis(ap=slot_now[u][:, K1 * j + k:K1 * j + k + 1], axis=0),
                                                         row_now[u][:, j, :], None, bounds_check=SLOT_TILES * 128 - 1,
                                                         oob_is_err=True).then_inc(sent, 16)
            pool.wait_ge(sent, 16 * NT * K1 * B)

        @block.tensor
        def _(pe):
            pe.wait_ge(loaded, 16 * len(loads))
            pe.wait_ge(tid_ready, 1)
            def shared_up(n):
                for m in range(MC):
                    pe.wait_ge(s_ready, MC * n + max(m - 1, 0))
                    for c in range(2):
                        mm = nc.tensor.matmul(p_h[m % 2][:, 0:S], sw1[:, c, 128 * m:128 * m + 128], kept[:, ds(n, 1), c, :].rearrange("p a s -> p (a s)"),
                                              start=(c == 0), stop=(c == 1))
                    mm.then_inc(h_made, 1)

            def shared_down(n):
                pe.wait_ge(s_ready, MC * (n + 1))
                for j in range(NT):
                    pe.wait_ge(z_added, NT * n + max(j - 1, 0))
                    for m in range(MC):
                        mm = nc.tensor.matmul(p_z[j % 2][:, 0:D], silu[:, m, TP * j:TP * j + TP], sw2[:, m, :], start=(m == 0), stop=(m == MC - 1))
                    mm.then_inc(z_made, 1)

            def body(n, more, shared):
                pe.wait_ge(xf.xt_ready, n + 1)
                pe.wait_ge(pos_read, n)
                for j in range(NT):
                    for c in range(2):
                        mm = nc.tensor.matmul(p_lg[:, j, :], xf.xT[:, c, TP * j:TP * j + TP], gate[:, c, :], start=(c == 0), stop=(c == 1))
                mm.then_inc(lg_made, 1)
                pe.wait_ge(lg_made, n + 1)
                pe.wait_ge(xt_kept, n + 1)
                pe.sem_inc(xf.xt_used, 1)
                if shared:
                    shared_up(n)
                if more:
                    xf.turn(pe, n + 1)
                if shared:
                    shared_down(n)
                pe.wait_ge(taken_ready, n + 1)
                for j in range(NT):
                    nc.tensor.matmul(p_pos[:, j, :], before[:, :], taken[:, j, :], start=True, stop=False)
                    for i in range(j):
                        nc.tensor.matmul(p_pos[:, j, :], ones[:, 0:TP], taken[:, i, :], start=False, stop=False)
                    mm = nc.tensor.matmul(p_pos[:, j, :], ones[:, 0:TP], taken_before[:, :], start=False, stop=True)
                mm.then_inc(pos_made, 1)

            xf.turn(pe, 0)
            with pe.Fori(0, EARLY) as n:
                body(n, True, True)
            with pe.Fori(EARLY, B - 1) as n:
                body(n, True, False)
            body(B - 1, False, False)
            pe.wait_ge(tid_ready, 1 + B)
            pe.wait_ge(pos_read, B)
            nc.tensor.matmul(p_total, ones[:, :], taken_before[:, :], start=True, stop=True).then_inc(total_made, 1)
            with pe.Fori(EARLY, B) as n:
                shared_up(n)
                shared_down(n)

        @block.scalar
        def _(act):
            def silus(n):
                act.wait_ge(z_made, NT * n)
                for m in range(MC):
                    act.wait_ge(h_made, MC * n + m + 1)
                    nc.scalar.activation(silu[:, m, :], p_h[m % 2][:, 0:S], ACT.Silu).then_inc(s_ready, 1)

            def body(n, more, shared):
                act.wait_ge(xf.xn_ready, n + 1)
                act.wait_ge(stored, 16 * n)
                nc.scalar.activation(rows[:, :, 0:D], xf.xn[:, :, :], ACT.Copy).then_inc(row_filled, 1)
                act.wait_ge(gap_ready, n + 1)
                nc.scalar.activation(gap[:, :], gap[:, :], ACT.Exp).then_inc(exp_made, 1)
                if shared:
                    silus(n)
                if more:
                    xf.copy(act, n + 1)

            xf.copy(act, 0)
            with act.Fori(0, EARLY) as n:
                body(n, True, True)
            with act.Fori(EARLY, B - 1) as n:
                body(n, True, False)
            body(B - 1, False, False)
            with act.Fori(EARLY, B) as n:
                silus(n)

        @block.vector
        def _(dve):
            def step(ins):
                t.dve.did(ins)
                t.dve.wait()

            dve.wait_ge(loaded, 16 * len(loads))
            dve.wait_ge(filled, 5)
            step(nc.vector.tensor_copy(before[:, :], before32[:, :]))
            nc.vector.tensor_copy(tid[:, :], tidu[:, :]).then_inc(tid_ready, 1)
            dve.wait_ge(tid_ready, 1)
            def add_shared(n):
                for j in range(NT):
                    dve.wait_ge(z_made, NT * n + j + 1)
                    h = t.h[:, ds(NT * n + j, 1), :].rearrange("p a d -> p (a d)")
                    nc.vector.tensor_tensor(h, h, p_z[j % 2][:, 0:D], ALU.add).then_inc(z_added, 1)

            def body(n, more, shared):
                dve.wait_ge(lg_made, n + 1)
                step(nc.vector.tensor_copy(lg[:, :, :], p_lg))
                for j in range(NT):
                    settle(dve, t)
                    step(nc.vector.max(top[:, j, :], lg[:, j, :]))
                for j in range(NT):
                    settle(dve, t)
                    step(nc.vector.max_index(topi[:, j, :], top[:, j, :], lg[:, j, :]))
                nc.vector.tensor_tensor(gap[:, :], top[:, :, 1], top[:, :, 0], ALU.subtract).then_inc(gap_ready, 1)
                dve.wait_ge(stored, 16 * n)
                step(nc.vector.tensor_copy(ids, topi[:, :, 0:K1]))
                step(nc.vector.tensor_copy(expert[:, ds(NT * n, NT), :], topi[:, :, 0:K1]))
                step(nc.vector.tensor_tensor(pick[:, :, :, :], t.iota[0:TP, 0:E1].unsqueeze(1).unsqueeze(1).to_broadcast([TP, NT, K1, E1]),
                                             ids.unsqueeze(3).to_broadcast([TP, NT, K1, E1]), ALU.is_equal))
                with nc.allow_low_precision(reason="zeros and ones are exact"):
                    nc.vector.tensor_reduce(taken[:, :, :], pick[:, :, :, :].rearrange("p j k e -> p j e k"), AX_X, ALU.add).then_inc(taken_ready, 1)
                if more:
                    xf.row_stats(dve, n + 1)
                    dve.wait_ge(row_filled, n + 1)
                    xf.normalize(dve, n + 1)
                dve.wait_ge(exp_made, n + 1)
                step(nc.vector.tensor_scalar(wts[:, :, 0], gap[:, :], 1.0, None, ALU.add))
                step(nc.vector.reciprocal(wts[:, :, 0], wts[:, :, 0]))
                step(nc.vector.tensor_tensor(wts[:, :, 1], wts[:, :, 0], gap[:, :], ALU.mult))
                step(nc.vector.tensor_copy(rows[:, :, TID].bitcast(U32), tid[:, :]))
                step(nc.vector.tensor_scalar(tid[:, :], tid[:, :], float(S), None, ALU.add))
                dve.sem_inc(rows_ready, 1)
                if shared:
                    add_shared(n)
                dve.wait_ge(pos_made, n + 1)
                step(nc.vector.tensor_tensor(work[:, :, :, :], pick[:, :, :, :], p_pos.unsqueeze(2).to_broadcast([TP, NT, K1, E1]), ALU.mult))
                dve.sem_inc(pos_read, 1)
                step(nc.vector.tensor_reduce(place[:, ds(NT * n, NT), :], work[:, :, :, :], AX_X, ALU.add))
                for j in range(NT):
                    step(nc.vector.tensor_tensor(taken_before[:, :], taken_before[:, :], taken[:, j, :], ALU.add))
                dve.sem_inc(tid_ready, 1)

            xf.row_stats(dve, 0)
            xf.normalize(dve, 0)
            with dve.Fori(0, EARLY) as n:
                t.dve.enter(n, 20 + xf.STEPS)
                body(n, True, True)
                t.dve.leave(EARLY)
            with dve.Fori(0, B - 1 - EARLY) as i:
                t.dve.enter(i, 20 + xf.STEPS)
                body(i + EARLY, True, False)
                t.dve.leave(B - 1 - EARLY)
            body(B - 1, False, False)
            dve.wait_ge(total_made, 1)
            step(nc.vector.tensor_scalar(needu[:, :], p_total, 127.0, None, ALU.add))
            step(nc.vector.tensor_scalar(needu[:, :], needu[:, :], 7, None, ALU.logical_shift_right))
            step(nc.vector.tensor_copy(need[:, :], needu[:, :]))
            step(nc.vector.tensor_tensor_scan(upto[:, :], plain[:, :], need[:, :], 0.0, ALU.mult, ALU.add))
            step(nc.vector.tensor_tensor(start[:, :], upto[:, :], need[:, :], ALU.subtract))
            step(nc.vector.tensor_scalar(start[:, :], start[:, :], 128.0, None, ALU.mult))
            choice = [TP, G * K1, E1]
            experts_of = expert[:, :, :].rearrange("p g k -> p (g k)")
            places = place[:, :, :].rearrange("p g k -> p (g k)")
            step(nc.vector.tensor_tensor(pick_all[:, :, :], t.iota[0:TP, 0:E1].unsqueeze(1).to_broadcast(choice),
                                         experts_of.unsqueeze(2).to_broadcast(choice), ALU.is_equal))
            step(nc.vector.tensor_tensor(pick_all[:, :, :], pick_all[:, :, :], start[0:TP, :].unsqueeze(1).to_broadcast(choice), ALU.mult))
            step(nc.vector.tensor_reduce(experts_of, pick_all[:, :, :], AX_X, ALU.add))
            step(nc.vector.tensor_tensor(places, places, experts_of, ALU.add))
            nc.vector.tensor_copy(slots[:, :, :], place[:, :, :]).then_inc(slots_ready, 1)
            cells = [128, SLOT_TILES, E1]
            step(nc.vector.tensor_tensor(over[:, :, :], upto[:, :].unsqueeze(1).to_broadcast(cells),
                                         t.iota[:, 0:SLOT_TILES].unsqueeze(2).to_broadcast(cells), ALU.is_le))
            step(nc.vector.tensor_reduce(t.tile_expert[:, :], over[:, :, :], AX_X, ALU.add))
            step(nc.vector.tensor_scalar(t.tile_expert[:, :], t.tile_expert[:, :], float(E1 - 1), None, ALU.min))
            step(nc.vector.tensor_copy(t.tile_expert_u[:, :], t.tile_expert[:, :]))
            with dve.Fori(EARLY, B) as n:
                add_shared(n)



def experts1(nc, io, t, new_sem, ctx):
    def sb(name, shape, dt=F32):
        return ctx.enter_context(nc.sbuf_tensor("e1_" + name, shape, dt))

    def ps(name, shape, dt=F32):
        return ctx.enter_context(nc.psum_tensor("e1_" + name, shape, dt))

    def sm(name):
        return new_sem("e1_" + name)

    K1, MC, HALF = 2, HID // 128, HID // 2
    w_loaded, x_loaded = sm("w_loaded"), [sm(f"x_loaded{u}") for u in range(2)]
    x_free, x_turned, x_ready = sm("x_free"), sm("x_turned"), sm("x_ready")
    h_made, s_ready, s_turned, g_ready = sm("h_made"), sm("s_ready"), sm("s_turned"), sm("g_ready")
    y_made, y_ready, y_added = sm("y_made"), sm("y_ready"), sm("y_added")
    w2s = sb("w2s", [128, E1, MC, D])
    x = [sb(f"x{u}", [128, ROW]) for u in range(2)]
    who = [sb(f"who{u}", [128, 2 * K1 + 1]) for u in range(2)]
    xT = [sb(f"xT{u}", [128, 2, 128]) for u in range(2)]
    silu = sb("silu", [128, HID])
    g = sb("g", [128, MC, 128])
    y = [sb(f"y{u}", [128, D]) for u in range(2)]
    match, weight = [sb(f"match{u}", [128, K1]) for u in range(2)], [sb(f"weight{u}", [128, 1]) for u in range(2)]
    p_x = ps("px", [128, 4, 128])
    p_h = [ps(f"ph{u}", [128, 512]) for u in range(2)]
    p_s = [ps(f"ps{u}", [128, 4, 128]) for u in range(2)]
    p_y = [ps(f"py{u}", [128, 512]) for u in range(2)]
    assert SLOT_TILES % 2 == 1

    with nc.Block() as block:
        @block.sync
        def _(sp):
            def load(i, r, u):
                sp.wait_ge(x_free, i + 1)
                sp.dma_start(x[u][:, :], t.disp1[ds(128 * i, 128), :]).then_inc(x_loaded[u], 16)

            load(0, 0, 0)
            for e in range(E1):
                sp.dma_start(w2s[:, e, :, :], io["ew2"][e]).then_inc(w_loaded, 16)
            with sp.Fori(0, (SLOT_TILES - 1) // 2) as r:
                load(2 * r + 1, r, 1)
                load(2 * r + 2, r, 0)

        @block.tensor
        def _(pe):
            def turn(i, r, u):
                pe.wait_ge(x_loaded[u], 16 * (r + 1))
                pe.wait_ge(x_ready, i)
                for c in range(2):
                    mm = nc.tensor.transpose(p_x[:, c, :], x[u][:, 128 * c:128 * c + 128], t.ident[:, :])
                mm.then_inc(x_turned, 1)

            def up(i, u):
                e = nc.tensor.value_load(t.tile_expert_u[0:1, ds(i, 1)], min_val=0, max_val=E1 - 1)
                pe.wait_ge(x_ready, i + 1)
                for m in range(2):
                    pe.wait_ge(s_ready, 2 * i - 1 + m if not isinstance(i, int) or i else 0)
                    for c in range(2):
                        mm = nc.tensor.matmul(p_h[m][:, :], xT[u][:, c, :], t.w1s[:, ds(e, 1), c, HALF * m:HALF * m + HALF].rearrange("p a n -> p (a n)"),
                                              start=(c == 0), stop=(c == 1))
                    mm.then_inc(h_made, 1)
                return e

            def turn_hidden(i):
                for m in range(2):
                    pe.wait_ge(s_ready, 2 * i + m + 1)
                    pe.wait_ge(g_ready, 2 * i - 1 + m if not isinstance(i, int) or i else 0)
                    for k in range(4):
                        mm = nc.tensor.transpose(p_s[m][:, k, :], silu[:, HALF * m + 128 * k:HALF * m + 128 * k + 128], t.ident[:, :])
                    mm.then_inc(s_turned, 1)

            def down(i, u):
                e = nc.tensor.value_load(t.tile_expert_u[0:1, ds(i, 1)], min_val=0, max_val=E1 - 1)
                pe.wait_ge(g_ready, 2 * i + 2)
                pe.wait_ge(y_ready, i)
                for m in range(MC):
                    mm = nc.tensor.matmul(p_y[u][:, 0:D], g[:, m, :], w2s[:, ds(e, 1), m, :].rearrange("p a n -> p (a n)"),
                                          start=(m == 0), stop=(m == MC - 1))
                mm.then_inc(y_made, 1)

            turn(0, 0, 0)
            up(0, 0)
            turn(1, 0, 1)
            turn_hidden(0)
            pe.wait_ge(w_loaded, 16 * E1)
            with pe.Fori(0, (SLOT_TILES - 3) // 2) as r:
                up(2 * r + 1, 1)
                turn(2 * r + 2, r + 1, 0)
                down(2 * r, 0)
                turn_hidden(2 * r + 1)
                up(2 * r + 2, 0)
                turn(2 * r + 3, r + 1, 1)
                down(2 * r + 1, 1)
                turn_hidden(2 * r + 2)
            last = SLOT_TILES - 1
            up(last - 1, 1)
            turn(last, last // 2, 0)
            down(last - 2, 0)
            turn_hidden(last - 1)
            up(last, 0)
            down(last - 1, 1)
            turn_hidden(last)
            down(last, 0)

        @block.scalar
        def _(act):
            def copy_x(i, u):
                act.wait_ge(x_turned, i + 1)
                act.wait_ge(h_made, 2 * i - 2 if not isinstance(i, int) or i > 1 else 0)
                nc.scalar.activation(xT[u][:, :, :], p_x[:, 0:2, :], ACT.Copy).then_inc(x_ready, 1)

            def hidden(i):
                for m in range(2):
                    act.wait_ge(h_made, 2 * i + m + 1)
                    act.wait_ge(s_turned, 2 * i - 1 + m if not isinstance(i, int) or i else 0)
                    nc.scalar.activation(silu[:, HALF * m:HALF * m + HALF], p_h[m][:, :], ACT.Silu).then_inc(s_ready, 1)

            copy_x(0, 0)
            hidden(0)
            with act.Fori(0, (SLOT_TILES - 1) // 2) as r:
                copy_x(2 * r + 1, 1)
                hidden(2 * r + 1)
                copy_x(2 * r + 2, 0)
                hidden(2 * r + 2)

        @block.vector
        def _(dve):
            def who_of(i, r, u):
                dve.wait_ge(x_loaded[u], 16 * (r + 1))
                dve.wait_ge(y_added, 16 * (max(i - 1, 0) if isinstance(i, int) else i - 1))
                t.dve.did(nc.vector.tensor_copy(who[u][:, 0:1].bitcast(U32), x[u][:, TID:TID + 1].bitcast(U32)))
                t.dve.did(nc.vector.tensor_scalar(match[u][:, :], x[u][:, IDS:IDS + K1], t.tile_expert[:, ds(i, 1)], None, ALU.is_equal))
                t.dve.wait()
                t.dve.did(nc.vector.tensor_tensor_reduce(match[u][:, :], match[u][:, :], x[u][:, WTS:WTS + K1], 1.0, 0.0,
                                                         ALU.mult, ALU.add, weight[u][:, :]))
                t.dve.wait()
                dve.wait_ge(x_turned, i + 1)
                dve.sem_inc(x_free, 1)

            def copy_hidden(i):
                for m in range(2):
                    dve.wait_ge(s_turned, 2 * i + m + 1)
                    dve.wait_ge(y_made, i)
                    nc.vector.tensor_copy(g[:, 4 * m:4 * m + 4, :], p_s[m][:, :, :]).then_inc(g_ready, 1)

            def weighted(i, u):
                dve.wait_ge(y_made, i + 1)
                dve.wait_ge(y_added, 16 * (max(i - 1, 0) if isinstance(i, int) else i - 1))
                nc.vector.tensor_scalar(y[u][:, :], p_y[u][:, 0:D], weight[u][:, :], None, ALU.mult).then_inc(y_ready, 1)

            dve.sem_inc(x_free, 2)
            dve.sem_inc(y_ready, 1)
            who_of(0, 0, 0)
            copy_hidden(0)
            who_of(1, 0, 1)
            weighted(0, 0)
            copy_hidden(1)
            with dve.Fori(0, (SLOT_TILES - 3) // 2) as r:
                t.dve.enter(r, 6)
                who_of(2 * r + 2, r + 1, 0)
                weighted(2 * r + 1, 1)
                copy_hidden(2 * r + 2)
                who_of(2 * r + 3, r + 1, 1)
                weighted(2 * r + 2, 0)
                copy_hidden(2 * r + 3)
                t.dve.leave((SLOT_TILES - 3) // 2)
            who_of(SLOT_TILES - 1, (SLOT_TILES - 1) // 2, 0)
            weighted(SLOT_TILES - 2, 1)
            copy_hidden(SLOT_TILES - 1)
            weighted(SLOT_TILES - 1, 0)

        @block.gpsimd
        def _(pool):
            def add(i, u):
                pool.wait_ge(y_ready, i + 2)
                settle(pool, t)
                nc.gpsimd.indirect_dma_start(t.sum1, bass.IndirectOffsetOnAxis(ap=who[u][:, 0:1].bitcast(U32), axis=0),
                                             y[u][:, :], None, bounds_check=T + 127, oob_is_err=True,
                                             compute_op=ALU.add).then_inc(y_added, 16)
                pool.wait_ge(y_added, 16 * (i + 1))

            with pool.Fori(0, (SLOT_TILES - 1) // 2) as r:
                add(2 * r, 0)
                add(2 * r + 1, 1)
            add(SLOT_TILES - 1, 0)


def finish(nc, io, t, new_sem, ctx):
    loaded, added, stored = new_sem("f_loaded"), new_sem("f_added"), new_sem("f_stored")
    with nc.Block() as block:
        @block.sync
        def _(sp):
            sp.dma_start(t.att[0:TP, :, :], t.sum1[0:T, :].rearrange("(g p) d -> p g d", p=TP)).then_inc(loaded, 16)
            for n in range(4):
                sp.wait_ge(added, n + 1)
                g0 = G // 4 * n
                sp.dma_start(io["out"][TP * g0:TP * (g0 + G // 4), :].rearrange("(g p) d -> p g d", p=TP), t.h[:, g0:g0 + G // 4, :]).then_inc(stored, 16)
            sp.wait_ge(stored, 64)

        @block.vector
        def _(dve):
            dve.wait_ge(loaded, 16)
            for n in range(4):
                h = t.h[:, G // 4 * n:G // 4 * (n + 1), :]
                nc.vector.tensor_tensor(h, h, t.att[0:TP, G // 4 * n:G // 4 * (n + 1), :], ALU.add).then_inc(added, 1)


class Names:
    pass


def build_program(nc, io):
    with ExitStack() as ctx:
        def sb(name, shape, dt=F32, where=ctx):
            return where.enter_context(nc.sbuf_tensor(name, shape, dt))

        def new_sem(name):
            return ctx.enter_context(nc.semaphore(name))

        t, sem = Names(), Names()
        sem.consts, sem.filled, sem.prepared = new_sem("consts"), new_sem("filled"), new_sem("prepared")
        sem.prefilled = new_sem("prefilled")
        sem.cosines, sem.settled = new_sem("cosines"), new_sem("settled")
        t.sem = sem
        t.dve = Steps(nc.vector, new_sem("dve_steps"))
        t.pool = Steps(nc.gpsimd, new_sem("pool_steps"))

        t.h = sb("h", [TP, G, D])
        t.att = sb("att", [128, G, D])
        t.ident = sb("ident", [128, 128])
        t.identb = sb("identb", [128, 128], BF16)
        t.half = sb("half", [128, 4])
        t.iota = sb("iota", [128, E0])
        t.tile_expert = sb("tile_expert", [128, SLOT_TILES])
        t.tile_expert_u = sb("tile_expert_u", [128, SLOT_TILES], U32)
        t.empty = sb("empty", [128, ROW])
        t.disp0 = nc.dram_tensor("disp0", [E0 * CAP, ROW], F32).ap()
        t.disp1 = nc.dram_tensor("disp1", [SLOT_TILES * 128, ROW], F32).ap()
        t.rows1 = nc.dram_tensor("rows1", [T, ROW], F32).ap()
        t.sum0 = [nc.dram_tensor(f"sum0{u}", [T + 128, D], F32).ap() for u in range(2)]
        t.sum1 = nc.dram_tensor("sum1", [T + 128, D], F32).ap()
        t.split = nc.dram_tensor("split", [B, 2, NPART, D, S], BF16).ap()
        t.rowmax = nc.dram_tensor("rowmax", [B, 2, NPART, NHALF, S], BF16).ap()

        def phase(body):
            with ExitStack() as inner:
                used = []

                def phase_sem(name):
                    used.append(inner.enter_context(nc.semaphore(name)))
                    return used[-1]

                body(phase_sem, inner)
                with nc.Block() as block:
                    @block.gpsimd
                    def _(pool):
                        for one in used:
                            pool.sem_clear(one)

        with ExitStack() as early:
            t.v = sb("v", [TP, G, NH, HD], F32, early)
            t.basis = sb("basis", [128, 2, 96], F32, early)
            t.basis_o = sb("basis_o", [128, 2, 32], F32, early)
            t.holo = sb("holo", [128, D], F32, early)
            t.wo = sb("wo", [128, 2, D], F32, early)
            t.bo = sb("bo", [TP, D], F32, early)
            t.above = sb("above", [TP, 3, TP], BF16, early)
            with ExitStack() as tok:
                t.xs = [sb(f"xs{u}", [F + 1, H, IMG], F32, tok) for u in range(2)]
                t.tok_kv = sb("tok_kv", [F + 1, 2 * F], F32, tok)
                t.tok_q = sb("tok_q", [F + 1, F], F32, tok)
                t.tok_res = sb("tok_res", [F + 1, H, F], F32, tok)
                t.ewT = sb("ewT", [128, 2, IMG], F32, tok)
                t.mask8 = sb("mask8", [128, 2, IMG // 4], U32, tok)
                t.maskf = sb("maskf", [128, 2, IMG], F32, tok)
                t.tok_out = sb("tok_out_w", [128, 2, D], F32, tok)
                t.gb = sb("gb", [TP, 2, D], F32, tok)
                t.phase = sb("phase", [128, D], F32, tok)
                t.amp = sb("amp", [128, D], F32, tok)
                t.trig = sb("trig", [128, 2, D], F32, tok)
                t.above32 = sb("above32", [TP, 3, TP], F32, tok)
                load_constants(nc, io, t, sem)
                phase(lambda ns, c: token_layer(nc, io, t, ns, tok))
            phase(lambda ns, c: holo_qkv(nc, io, t, ns, c))
            phase(lambda ns, c: attention(nc, t, "a0", False, ns, c))
            phase(lambda ns, c: attention_out(nc, t, "o0", 32, ns, c))
            phase(lambda ns, c: route_and_share0(nc, io, t, ns, c))
            phase(lambda ns, c: experts0(nc, io, t, ns, c))
            phase(lambda ns, c: rotary_qkv(nc, io, t, ns, c))
            phase(lambda ns, c: attention(nc, t, "a1", True, ns, c))
            phase(lambda ns, c: attention_out(nc, t, "o1", 0, ns, c))
        with ExitStack() as late:
            t.w1s = sb("w1s", [128, E1, 2, HID], F32, late)
            phase(lambda ns, c: route_and_share1(nc, io, t, ns, c))
            phase(lambda ns, c: experts1(nc, io, t, ns, c))
            phase(lambda ns, c: finish(nc, io, t, ns, c))


def layouts(a):
    f = {}

    def T_(w):
        return w.T

    def chunked(w, p=128):
        return w.reshape(w.shape[0] // p, p, w.shape[1]).transpose(1, 0, 2)

    f["x"] = a["x"].transpose(0, 1, 3, 2)
    f["txt"] = a["txt"]
    f["tok_kv"] = np.concatenate([np.concatenate([a["L0_tok_Wk_w"].T, a["L0_tok_Wv_w"].T], 1),
                                  np.concatenate([a["L0_tok_Wk_b"], a["L0_tok_Wv_b"]])[None]], 0)
    f["tok_kv"] = f["tok_kv"][:, :]
    f["tok_q"] = np.concatenate([a["L0_tok_Wq_w"].T, a["L0_tok_Wq_b"][None]], 0)
    eye = np.eye(F, dtype=np.float32)
    f["tok_res"] = np.concatenate([np.broadcast_to(eye[:, None, :], (F, H, F)), a["L0_tok_out_b"].reshape(1, H, F)], 0)
    f["bias_t"] = chunked(a["L0_tok_w_bias"].T)
    f["mask_t"] = chunked(np.ascontiguousarray(a["L0_tok_local_mask"].T).view(np.uint32))
    f["tok_out"] = chunked(a["L0_tok_out_w"])
    f["ln_g"], f["ln_b"] = a["L0_tok_ln_g"], a["L0_tok_ln_b"]
    f["ident"] = np.eye(128, dtype=np.float32)
    f["basis"] = chunked(np.concatenate([a[f"L0_attn_basis_{c}"].T for c in "qkv"], 1))
    f["basis_o"] = chunked(a["L0_attn_basis_o"].T)
    f["phase"] = np.concatenate([a[f"L0_attn_phase_{c}"].T for c in "qkvo"], 0)
    f["amp"] = np.concatenate([a[f"L0_attn_amp_{c}"].T for c in "qkvo"], 0)
    f["iota"] = np.arange(E0, dtype=np.float32)
    f["before"] = np.triu(np.ones((TP, TP), np.float32), 1)
    f["gate0"], f["gate0_b"] = chunked(a["L0_ffn_gate_w"].T), a["L0_ffn_gate_b"]
    f["ws1"], f["ws3"], f["ws2"] = (chunked(a["L0_ffn_ws1"].T), chunked(a["L0_ffn_ws3"].T), chunked(a["L0_ffn_ws2"].T, IC))
    w13 = np.concatenate([a["L0_ffn_w1"].transpose(0, 2, 1), a["L0_ffn_w3"].transpose(0, 2, 1)], 2)
    f["w13"] = w13.reshape(E0, 2, 128, 2 * I0).transpose(0, 2, 1, 3)
    f["w2"] = a["L0_ffn_w2"].transpose(0, 2, 1).reshape(E0, 2, IC, D).transpose(0, 2, 1, 3)
    f["wo"], f["bo"] = chunked(a["L1_attn_wo"]), a["L1_attn_bo"]
    after = np.triu(np.full((TP, TP), -1e30, np.float32), 1)
    f["above"] = np.stack([after, after.T, np.full_like(after, -1e30)], 1)
    f["w_c"] = chunked(np.concatenate([a["L1_attn_wq"], a["L1_attn_wkv"]], 1))
    f["w_low"] = np.concatenate([a["L1_attn_wqc"], a["L1_attn_wkc"]], 0)
    swap = np.r_[64:128, 0:64]
    f["w_rope"] = np.stack([np.stack([chunked(w), chunked(w[:, swap])]) for w in (a["L1_attn_wqr"], a["L1_attn_wkr"])])
    bq, bk = a["L1_attn_bqr"], a["L1_attn_bkr"]
    f["biases"] = np.stack([np.concatenate([a["L1_attn_bq"], a["L1_attn_bkv"]]), a["L1_attn_bqc"], a["L1_attn_bkc"],
                            bq, bq[swap], bk, bk[swap]], 1)
    f["w_v"], f["b_v"] = a["L1_attn_wv"], a["L1_attn_bv"]
    inv = (1.0 / np.float32(10000.0) ** (np.arange(0, 128, 2, dtype=np.float32) / np.float32(128))).astype(np.float32)
    angle = np.arange(S, dtype=np.float32)[None] * np.concatenate([inv, inv])[:, None]
    sign = np.where(np.arange(128) < 64, -1.0, 1.0).astype(np.float32)[:, None]
    f["rope"] = np.stack([np.cos(angle), np.sin(angle) * sign], 1).astype(np.float32)
    f["gate1"] = chunked(a["L1_ffn_gate_w"].T)
    f["sw1"], f["sw2"] = chunked(a["L1_ffn_shared_w1"].T), chunked(a["L1_ffn_shared_w2"].T)
    f["ew1"] = a["L1_ffn_experts_w1"].transpose(0, 2, 1).reshape(E1, 2, 128, HID).transpose(0, 2, 1, 3)
    f["ew2"] = a["L1_ffn_experts_w2"].transpose(0, 2, 1).reshape(E1, HID // 128, 128, D).transpose(0, 2, 1, 3)
    return {k: np.ascontiguousarray(v) for k, v in f.items()}


def kernel(**inputs):
    import concourse.bacc as bacc
    from concourse.bass_utils import run_bass_kernel_spmd

    laid = layouts({name: np.asarray(value) for name, value in inputs.items()})
    nc = bacc.Bacc("TRN2", target_bir_lowering=False, num_devices=1)
    io, arrays = {}, {}
    for name, value in laid.items():
        arrays["in_" + name] = value
        io[name] = nc.dram_tensor("in_" + name, value.shape, mybir.dt.from_np(value.dtype), kind="ExternalInput").ap()
    io["out"] = nc.dram_tensor("out", (T, D), F32, kind="ExternalOutput").ap()
    build_program(nc, io)
    results = run_bass_kernel_spmd(nc, [arrays], core_ids=[0])
    return results.results[0]["out"].reshape(B, S, D)
```
